# Optimizing a Trainium2 kernel written in Bass

```python
import numpy as np
import jax
import jax.numpy as jnp

def _softmax(x, axis=-1):
    return jax.nn.softmax(x, axis=axis)

def _gelu(x):
    return jax.nn.gelu(x, approximate=True)

def _silu(x):
    return jax.nn.silu(x)

def _sigmoid(x):
    return jax.nn.sigmoid(x)

def _layernorm(x, axis=-1, eps=1e-05):
    m = jnp.mean(x, axis=axis, keepdims=True)
    v = jnp.var(x, axis=axis, keepdims=True)
    return (x - m) / jnp.sqrt(v + eps)

def _scatter_add(tgt, idx, src, axis=0):
    return tgt.at[idx].add(src)

def _segment_sum(src, seg, n):
    return jax.ops.segment_sum(src, seg, n)
kernel_name = 'mk_vit_tower_d2_tok_img1024_r4_f20928'

def setup_inputs(seed: int=0):
    np.random.seed(seed)
    _w = jnp.asarray

    def _rec_inputs():
        import jax
        import jax.numpy as jnp
        _rk = jax.random.key(seed)
        x = -0.00016672 + 0.999947 * jax.random.normal(jax.random.fold_in(_rk, 1), (64, 3, 96, 96), jnp.float32)
        return x
    x = _rec_inputs()

    def _L0_tok_setup():
        import jax, jax.numpy as jnp
        import numpy as np
        IMG = 96
        PATCH = 16
        C_IN = 3
        EMBED = 256
        NPH = IMG // PATCH
        NUM_PATCHES = NPH * NPH
        PATCH_DIM = PATCH * PATCH * C_IN
        key = jax.random.key(seed)
        k_x, k_w, k_b, k_cls, k_pos = jax.random.split(key, 5)
        x = jax.random.normal(k_x, (64, C_IN, IMG, IMG), dtype=jnp.float32)
        W = jax.random.normal(k_w, (EMBED, PATCH_DIM), dtype=jnp.float32) * (1.0 / np.sqrt(PATCH_DIM))
        b = jax.random.normal(k_b, (EMBED,), dtype=jnp.float32) * 0.01
        cls_token = jax.random.normal(k_cls, (1, 1, EMBED), dtype=jnp.float32) * 0.02
        pos_embed = jax.random.normal(k_pos, (1, NUM_PATCHES + 1, EMBED), dtype=jnp.float32) * 0.02
        return {'x': x, 'W': W, 'b': b, 'cls_token': cls_token, 'pos_embed': pos_embed}
    _L0_tok_all = _L0_tok_setup()
    _L0_tok_in = {k: v for k, v in _L0_tok_all.items() if k in ('W', 'b', 'cls_token', 'pos_embed')}
    del _L0_tok_all

    def _L0_attn_setup():
        import jax, jax.numpy as jnp
        import numpy as np
        D_MODEL, H, DK, DV = (256, 16, 64, 64)
        key = jax.random.key(seed)
        ks = jax.random.split(key, 9)
        s = lambda fan_in: 1.0 / np.sqrt(fan_in)
        return {'x': jax.random.normal(ks[0], (2, 512, D_MODEL), dtype=jnp.float32), 'Wq': jax.random.uniform(ks[1], (D_MODEL, H * DK), jnp.float32, -s(D_MODEL), s(D_MODEL)), 'bq': jax.random.uniform(ks[2], (H * DK,), jnp.float32, -s(D_MODEL), s(D_MODEL)), 'Wk': jax.random.uniform(ks[3], (D_MODEL, DK), jnp.float32, -s(D_MODEL), s(D_MODEL)), 'bk': jax.random.uniform(ks[4], (DK,), jnp.float32, -s(D_MODEL), s(D_MODEL)), 'Wv': jax.random.uniform(ks[5], (D_MODEL, DV), jnp.float32, -s(D_MODEL), s(D_MODEL)), 'bv': jax.random.uniform(ks[6], (DV,), jnp.float32, -s(D_MODEL), s(D_MODEL)), 'Wo': jax.random.uniform(ks[7], (H * DV, D_MODEL), jnp.float32, -s(H * DV), s(H * DV)), 'bo': jax.random.uniform(ks[8], (D_MODEL,), jnp.float32, -s(H * DV), s(H * DV))}
    _L0_attn_all = _L0_attn_setup()
    _L0_attn_in = {k: v for k, v in _L0_attn_all.items() if k in ('Wq', 'bq', 'Wk', 'bk', 'Wv', 'bv', 'Wo', 'bo')}
    del _L0_attn_all

    def _L0_ffn_setup():
        import jax, jax.numpy as jnp
        import numpy as np
        B, S, D = (4, 1024, 256)
        DD = 4 * D
        N_EXPERTS = 8
        CAPACITY = 1.0
        LN_EPS = 1e-05
        key = jax.random.key(seed)
        ks = jax.random.split(key, 8)
        s1 = 1.0 / np.sqrt(D)
        s2 = 1.0 / np.sqrt(DD)
        return {'x': jax.random.normal(ks[0], (B, S, D), jnp.float32), 'gate_w': jax.random.normal(ks[1], (N_EXPERTS, D), jnp.float32) * 0.02, 'ln_w': jnp.ones((D,), jnp.float32), 'ln_b': jnp.zeros((D,), jnp.float32), 'fc1s': jax.random.normal(ks[2], (N_EXPERTS, DD, D), jnp.float32) * s1, 'b1s': jax.random.normal(ks[3], (N_EXPERTS, DD), jnp.float32) * s1, 'fc2s': jax.random.normal(ks[4], (N_EXPERTS, D, DD), jnp.float32) * s2, 'b2s': jax.random.normal(ks[5], (N_EXPERTS, D), jnp.float32) * s2}
    _L0_ffn_all = _L0_ffn_setup()
    _L0_ffn_in = {k: v for k, v in _L0_ffn_all.items() if k in ('gate_w', 'ln_w', 'ln_b', 'fc1s', 'b1s', 'fc2s', 'b2s')}
    del _L0_ffn_all

    def _L1_attn_setup():
        import jax, jax.numpy as jnp
        import numpy as np
        B, S, DIM, HDIM = (8, 256, 256, 128)
        H = DIM // HDIM
        GN_EPS = 0.001

        def group_norm(y, gamma, beta, groups, eps=GN_EPS):
            b, s, c = y.shape
            g = y.reshape(b, s, groups, c // groups)
            mean = g.mean(axis=(1, 3), keepdims=True)
            var = g.var(axis=(1, 3), keepdims=True)
            g = (g - mean) * jax.lax.rsqrt(var + eps)
            return g.reshape(b, s, c) * gamma + beta
        key = jax.random.key(seed)
        ks = jax.random.split(key, 7)
        x = jax.random.normal(ks[0], (B, S, DIM), dtype=jnp.float32)
        sc_h = 1.0 / np.sqrt(HDIM).astype(np.float32)
        sc_d = 1.0 / np.sqrt(DIM).astype(np.float32)
        Wq = jax.random.normal(ks[1], (H, HDIM, HDIM), dtype=jnp.float32) * sc_h
        Wk = jax.random.normal(ks[2], (H, HDIM, HDIM), dtype=jnp.float32) * sc_h
        Wv = jax.random.normal(ks[3], (H, HDIM, HDIM), dtype=jnp.float32) * sc_h
        Wg = jax.random.normal(ks[4], (DIM, DIM), dtype=jnp.float32) * sc_d
        Wo = jax.random.normal(ks[5], (DIM, DIM), dtype=jnp.float32) * sc_d
        gn_gamma = jnp.ones((DIM,), dtype=jnp.float32)
        gn_beta = jnp.zeros((DIM,), dtype=jnp.float32)
        return {'x': x, 'Wq': Wq, 'Wk': Wk, 'Wv': Wv, 'Wg': Wg, 'Wo': Wo, 'gn_gamma': gn_gamma, 'gn_beta': gn_beta}
    _L1_attn_all = _L1_attn_setup()
    _L1_attn_in = {k: v for k, v in _L1_attn_all.items() if k in ('Wq', 'Wk', 'Wv', 'Wg', 'Wo', 'gn_gamma', 'gn_beta')}
    del _L1_attn_all

    def _L1_ffn_setup():
        import jax, jax.numpy as jnp
        import numpy as np
        TOP_K = 2
        ROUTE_SCALE = 1.0
        EPS = 1e-20
        B, S, D = (2, 128, 256)
        E = 8
        F = 192
        FS = 192 * 1
        key = jax.random.key(seed)
        ks = jax.random.split(key, 9)
        s = 0.02
        return {'hidden_states': jax.random.normal(ks[0], (B, S, D), dtype=jnp.float32), 'W_gate_router': jax.random.normal(ks[1], (D, E), dtype=jnp.float32) * s, 'expert_bias': jnp.zeros((E,), dtype=jnp.float32), 'Wg': jax.random.normal(ks[2], (E, D, F), dtype=jnp.float32) * s, 'Wu': jax.random.normal(ks[3], (E, D, F), dtype=jnp.float32) * s, 'Wd': jax.random.normal(ks[4], (E, F, D), dtype=jnp.float32) * s, 'Wg_s': jax.random.normal(ks[5], (D, FS), dtype=jnp.float32) * s, 'Wu_s': jax.random.normal(ks[6], (D, FS), dtype=jnp.float32) * s, 'Wd_s': jax.random.normal(ks[7], (FS, D), dtype=jnp.float32) * s}
    _L1_ffn_all = _L1_ffn_setup()
    _L1_ffn_in = {k: v for k, v in _L1_ffn_all.items() if k in ('W_gate_router', 'expert_bias', 'Wg', 'Wu', 'Wd', 'Wg_s', 'Wu_s', 'Wd_s')}
    del _L1_ffn_all
    return {'x': x, 'L0_tok_W': _L0_tok_in['W'], 'L0_tok_b': _L0_tok_in['b'], 'L0_tok_cls_token': _L0_tok_in['cls_token'], 'L0_tok_pos_embed': _L0_tok_in['pos_embed'], 'L0_attn_Wq': _L0_attn_in['Wq'], 'L0_attn_bq': _L0_attn_in['bq'], 'L0_attn_Wk': _L0_attn_in['Wk'], 'L0_attn_bk': _L0_attn_in['bk'], 'L0_attn_Wv': _L0_attn_in['Wv'], 'L0_attn_bv': _L0_attn_in['bv'], 'L0_attn_Wo': _L0_attn_in['Wo'], 'L0_attn_bo': _L0_attn_in['bo'], 'L0_ffn_gate_w': _L0_ffn_in['gate_w'], 'L0_ffn_ln_w': _L0_ffn_in['ln_w'], 'L0_ffn_ln_b': _L0_ffn_in['ln_b'], 'L0_ffn_fc1s': _L0_ffn_in['fc1s'], 'L0_ffn_b1s': _L0_ffn_in['b1s'], 'L0_ffn_fc2s': _L0_ffn_in['fc2s'], 'L0_ffn_b2s': _L0_ffn_in['b2s'], 'L1_attn_Wq': _L1_attn_in['Wq'], 'L1_attn_Wk': _L1_attn_in['Wk'], 'L1_attn_Wv': _L1_attn_in['Wv'], 'L1_attn_Wg': _L1_attn_in['Wg'], 'L1_attn_Wo': _L1_attn_in['Wo'], 'L1_attn_gn_gamma': _L1_attn_in['gn_gamma'], 'L1_attn_gn_beta': _L1_attn_in['gn_beta'], 'L1_ffn_W_gate_router': _L1_ffn_in['W_gate_router'], 'L1_ffn_expert_bias': _L1_ffn_in['expert_bias'], 'L1_ffn_Wg': _L1_ffn_in['Wg'], 'L1_ffn_Wu': _L1_ffn_in['Wu'], 'L1_ffn_Wd': _L1_ffn_in['Wd'], 'L1_ffn_Wg_s': _L1_ffn_in['Wg_s'], 'L1_ffn_Wu_s': _L1_ffn_in['Wu_s'], 'L1_ffn_Wd_s': _L1_ffn_in['Wd_s']}

def reference(x, L0_tok_W, L0_tok_b, L0_tok_cls_token, L0_tok_pos_embed, L0_attn_Wq, L0_attn_bq, L0_attn_Wk, L0_attn_bk, L0_attn_Wv, L0_attn_bv, L0_attn_Wo, L0_attn_bo, L0_ffn_gate_w, L0_ffn_ln_w, L0_ffn_ln_b, L0_ffn_fc1s, L0_ffn_b1s, L0_ffn_fc2s, L0_ffn_b2s, L1_attn_Wq, L1_attn_Wk, L1_attn_Wv, L1_attn_Wg, L1_attn_Wo, L1_attn_gn_gamma, L1_attn_gn_beta, L1_ffn_W_gate_router, L1_ffn_expert_bias, L1_ffn_Wg, L1_ffn_Wu, L1_ffn_Wd, L1_ffn_Wg_s, L1_ffn_Wu_s, L1_ffn_Wd_s):
    import jax
    import jax.numpy as jnp

    def _L0_tok_ref(x, W, b, cls_token, pos_embed):
        import jax, jax.numpy as jnp
        import numpy as np
        IMG = 96
        PATCH = 16
        C_IN = 3
        EMBED = 256
        NPH = IMG // PATCH
        NUM_PATCHES = NPH * NPH
        PATCH_DIM = PATCH * PATCH * C_IN
        B, C, H, Wd = x.shape
        nph, npw = (H // PATCH, Wd // PATCH)
        patches = x.reshape(B, C, nph, PATCH, npw, PATCH)
        patches = patches.transpose(0, 2, 4, 1, 3, 5)
        patches = patches.reshape(B, nph * npw, C * PATCH * PATCH)
        proj = jnp.einsum('bnd,ed->bne', patches, W) + b
        cls = jnp.broadcast_to(cls_token, (B, 1, cls_token.shape[-1]))
        out = jnp.concatenate([cls, proj], axis=1) + pos_embed
        return out

    def _L0_attn_ref(x, Wq, bq, Wk, bk, Wv, bv, Wo, bo):
        import jax, jax.numpy as jnp
        import numpy as np
        D_MODEL, H, DK, DV = (256, 16, 64, 64)
        B, S, _ = x.shape
        q = (x @ Wq + bq).reshape(B, S, H, DK)
        k = x @ Wk + bk
        v = x @ Wv + bv
        scores = jnp.einsum('bshd,btd->bhst', q, k) / np.sqrt(DK).astype(x.dtype)
        w = jax.nn.softmax(scores, axis=-1)
        out = jnp.einsum('bhst,btd->bshd', w, v).reshape(B, S, H * DV)
        return out @ Wo + bo

    def _L0_ffn_ref(x, gate_w, ln_w, ln_b, fc1s, b1s, fc2s, b2s):
        import jax, jax.numpy as jnp
        import numpy as np
        B, S, D = (4, 1024, 256)
        DD = 4 * D
        N_EXPERTS = 8
        CAPACITY = 1.0
        LN_EPS = 1e-05
        og_shape = x.shape
        d = og_shape[-1]
        xf = x.reshape(-1, d)
        bs = xf.shape[0]
        n = gate_w.shape[0]
        k = int(bs * CAPACITY) // n
        scores = jax.nn.softmax(xf @ gate_w.T, axis=-1)
        vals, idx = jax.lax.top_k(scores.T, k)
        kept_w = vals.T
        kept_idx = idx.T
        flat_idx = kept_idx.reshape(-1)
        y = xf[flat_idx].reshape(k, n, d)
        mu = y.mean(-1, keepdims=True)
        var = ((y - mu) ** 2).mean(-1, keepdims=True)
        y = (y - mu) * jax.lax.rsqrt(var + LN_EPS) * ln_w + ln_b
        h = jnp.einsum('knd,nfd->knf', y, fc1s) + b1s
        h = jax.nn.gelu(h, approximate=True)
        out = jnp.einsum('knf,ndf->knd', h, fc2s) + b2s
        out = out * kept_w[..., None]
        xf = xf.at[flat_idx].add(out.reshape(k * n, d))
        return xf.reshape(og_shape)

    def _L1_attn_ref(x, Wq, Wk, Wv, Wg, Wo, gn_gamma, gn_beta):
        import jax, jax.numpy as jnp
        import numpy as np
        B, S, DIM, HDIM = (8, 256, 256, 128)
        H = DIM // HDIM
        GN_EPS = 0.001

        def group_norm(y, gamma, beta, groups, eps=GN_EPS):
            b, s, c = y.shape
            g = y.reshape(b, s, groups, c // groups)
            mean = g.mean(axis=(1, 3), keepdims=True)
            var = g.var(axis=(1, 3), keepdims=True)
            g = (g - mean) * jax.lax.rsqrt(var + eps)
            return g.reshape(b, s, c) * gamma + beta
        b, s, c = x.shape
        h, hd = (Wq.shape[0], Wq.shape[1])
        Wgate = jax.nn.relu(jnp.einsum('bsc,cd->bsd', x, Wg))
        xh = x.reshape(b, s, h, hd)
        Q = jnp.einsum('bshd,hde->bhse', xh, Wq)
        K = jnp.einsum('bshd,hde->bhse', xh, Wk)
        V = jnp.einsum('bshd,hde->bhse', xh, Wv)
        idx = jnp.arange(s, dtype=jnp.float32)
        gammas = 1.0 - 2.0 ** (-5.0 - jnp.arange(h, dtype=jnp.float32))
        decay = gammas[:, None, None] ** (idx[None, :, None] - idx[None, None, :])
        scores = jnp.einsum('bhsd,bhtd->bhst', Q, K) * decay[None]
        ret = jnp.einsum('bhst,bhtd->bhsd', scores, V)
        y = ret.transpose(0, 2, 1, 3).reshape(b, s, c)
        Y = group_norm(y, gn_gamma, gn_beta, groups=hd)
        return jnp.einsum('bsc,cd->bsd', Wgate * Y, Wo)

    def _L1_ffn_ref(hidden_states, W_gate_router, expert_bias, Wg, Wu, Wd, Wg_s, Wu_s, Wd_s):
        import jax, jax.numpy as jnp
        import numpy as np
        TOP_K = 2
        ROUTE_SCALE = 1.0
        EPS = 1e-20
        B, S, D = (2, 128, 256)
        E = 8
        F = 192
        FS = 192 * 1
        b, s, d = hidden_states.shape
        x = hidden_states.reshape(-1, d)
        T = x.shape[0]
        logits = x @ W_gate_router
        scores = jax.nn.sigmoid(logits.astype(jnp.float32))
        _, sel = jax.lax.top_k(scores + expert_bias, TOP_K)
        top_scores = jnp.take_along_axis(scores, sel, axis=1)
        top_scores = top_scores / (top_scores.sum(-1, keepdims=True) + EPS)
        top_scores = top_scores * ROUTE_SCALE
        shared = jax.nn.silu(x @ Wg_s) * (x @ Wu_s) @ Wd_s
        tok = jnp.repeat(jnp.arange(T), TOP_K)
        exp = sel.reshape(-1)
        w = top_scores.reshape(-1)
        xr = x[tok]
        h = jax.nn.silu(jnp.einsum('nd,edf->enf', xr, Wg)) * jnp.einsum('nd,edf->enf', xr, Wu)
        out_all = jnp.einsum('enf,efd->end', h, Wd)
        routed = out_all[exp, jnp.arange(exp.shape[0])]
        routed = (routed.astype(jnp.float32) * w[:, None]).astype(hidden_states.dtype)
        out = shared.at[tok].add(routed)
        return out.reshape(b, s, d)
    h = _L0_tok_ref(x, L0_tok_W, L0_tok_b, L0_tok_cls_token, L0_tok_pos_embed)
    h = h + _L0_attn_ref(_layernorm(h, axis=-1), L0_attn_Wq, L0_attn_bq, L0_attn_Wk, L0_attn_bk, L0_attn_Wv, L0_attn_bv, L0_attn_Wo, L0_attn_bo)
    h = h + _L0_ffn_ref(_layernorm(h, axis=-1), L0_ffn_gate_w, L0_ffn_ln_w, L0_ffn_ln_b, L0_ffn_fc1s, L0_ffn_b1s, L0_ffn_fc2s, L0_ffn_b2s)
    h = h + _L1_attn_ref(_layernorm(h, axis=-1), L1_attn_Wq, L1_attn_Wk, L1_attn_Wv, L1_attn_Wg, L1_attn_Wo, L1_attn_gn_gamma, L1_attn_gn_beta)
    h = h + _L1_ffn_ref(_layernorm(h, axis=-1), L1_ffn_W_gate_router, L1_ffn_expert_bias, L1_ffn_Wg, L1_ffn_Wu, L1_ffn_Wd, L1_ffn_Wg_s, L1_ffn_Wu_s, L1_ffn_Wd_s)
    return h

_drawn_inputs = setup_inputs


def setup_inputs(seed=0):
    import zlib

    import numpy as np

    out = dict(_drawn_inputs(seed))
    spreads = {'L0_ffn_ln_w': (1.0, 0.6),
     'L0_ffn_ln_b': (0.0, 0.8),
     'L1_attn_gn_gamma': (1.0, 0.2),
     'L1_attn_gn_beta': (0.0, 0.1),
     'L1_ffn_expert_bias': (0.0, 0.8)}
    factors = {'L0_tok_b': 3.702,
     'L0_attn_bq': 8.0,
     'L0_attn_bk': 8.0,
     'L0_ffn_b1s': 8.0,
     'L0_ffn_b2s': 8.0,
     'L1_ffn_W_gate_router': 8.0,
     'L1_ffn_Wg': 8.0,
     'L1_ffn_Wu': 8.0,
     'L1_ffn_Wd': 8.0,
     'L1_ffn_Wg_s': 8.0,
     'L1_ffn_Wu_s': 8.0,
     'L1_ffn_Wd_s': 8.0}
    for name, (base, spread) in spreads.items():
        noise = np.random.default_rng([zlib.crc32(name.encode()), seed]).standard_normal(out[name].shape)
        drawn = base * np.exp(spread * noise) if base else spread * noise
        out[name] = jnp.asarray(drawn.astype(out[name].dtype))
    for name, factor in factors.items():
        out[name] = (out[name] * factor).astype(out[name].dtype)
    return out
```

```python
from contextlib import ExitStack

import concourse.bass as bass
from concourse import mybir

ALU = mybir.AluOpType
ACT = mybir.ActivationFunctionType
F32 = mybir.dt.float32
BF16 = mybir.dt.bfloat16
I32 = mybir.dt.int32
AX_X = mybir.AxisListType.X

P = 128
D = 256
NB = 64
C, IMG, PATCH = 3, 96, 16
NPH = IMG // PATCH
S = NPH * NPH + 1
KP = C * PATCH * PATCH // P
H0, DK = 16, 64
NPAIR = H0 // 2
IPT = 3
R = IPT * S
IPG = 2 * IPT
GT = 2 * R
NT = -(-NB // IPG) * 2
NG = NT // 2
TOK = NB * S
NE = 8
CAP = TOK // NE
YW = D + NE
LN_EPS = 1e-5
GN_EPS = 1e-3
SCALE0 = DK ** -0.5


def program(nc, x, tok_W, tok_b, cls_token, pos_embed, Wq, bq, Wk, bk, Wv, bv, Wo, bo, gate_w, ln_w, ln_b,
            fc1s, b1s, fc2s, b2s, rWq, rWk, rWv, rWg, rWo, gn_gamma, gn_beta, router_w, expert_bias,
            eWg, eWu, eWd, sWg, sWu, sWd, out):
    with ExitStack() as ctx:
        acc_rows = nc.dram_tensor("acc_rows", (NT * R, D), F32, kind="Internal").ap()
        y_rows = nc.dram_tensor("y_rows", (NT * R, YW), F32, kind="Internal").ap()
        scores = ctx.enter_context(nc.sbuf_tensor("scores", [P, NT, NE], F32))
        sum_rows = nc.dram_tensor("sum_rows", (NT * R + P, D), F32, kind="Internal").ap()
        x3_rows = nc.dram_tensor("x3_rows", (NT * R, D), F32, kind="Internal").ap()
        logits = ctx.enter_context(nc.sbuf_tensor("logits", [P, NT, NE], F32))
        const = constants(nc, ctx)
        with ExitStack() as stage:
            embed_and_attend(nc, stage, const, x, tok_W, tok_b, cls_token, pos_embed, Wq, bq, Wk, bk, Wv, bv,
                             Wo, bo, gate_w, ln_w, ln_b, acc_rows, y_rows, scores)
        end_stage(nc, const)
        with ExitStack() as stage:
            expert_choice(nc, stage, const, scores, fc1s, b1s, fc2s, b2s, acc_rows, y_rows)
        end_stage(nc, const)
        with ExitStack() as stage:
            retention(nc, stage, const, acc_rows, rWq, rWk, rWv, rWg, rWo, gn_gamma, gn_beta, router_w, sWg, sWu, sWd,
                      sum_rows, x3_rows, logits)
        end_stage(nc, const)
        with ExitStack() as stage:
            token_choice(nc, stage, const, logits, expert_bias, eWg, eWu, eWd, sum_rows, x3_rows, out)


class Const:
    pass


def constants(nc, ctx):
    c = Const()
    c.semaphores = []
    sb = lambda n, s, d: ctx.enter_context(nc.sbuf_tensor(n, s, d))
    c.ident = sb("ident", [P, P], F32)
    c.zero = sb("zero", [P, P], F32)
    c.neg_half = sb("neg_half", [P, 2], F32)
    made = c.made = ctx.enter_context(nc.semaphore("const_made"))
    c.waits_passed = ctx.enter_context(nc.semaphore("waits_passed"))
    with nc.Block() as block:
        @block.gpsimd
        def _(pool):
            nc.gpsimd.memset(c.neg_half[:, :], -0.5).then_inc(made, 1)
            nc.gpsimd.memset(c.zero[:, :], 0.0).then_inc(made, 1)
            pool.wait_ge(made, 2)
            nc.gpsimd.affine_select(out=c.ident[:, :], in_=c.zero[:, :], compare_op=ALU.not_equal, fill=1.0,
                                    base=0, pattern=[[-1, P]], channel_multiplier=1).then_inc(made, 1)
            pool.wait_ge(made, 3)
    return c


def embed_and_attend(nc, ctx, const, x, tok_W, tok_b, cls_token, pos_embed, Wq, bq, Wk, bk, Wv, bv,
                     Wo, bo, gate_w, ln_w, ln_b, acc_rows, y_rows, scores):
    sb = lambda n, s, d=F32: ctx.enter_context(nc.sbuf_tensor(n, s, d))
    sem = lambda n: semaphore(nc, const, "a_" + n)

    w_rows = sb("w_rows", [P, D // P, KP * P])
    w_tok = sb("w_tok", [P, KP, D])
    w_q = sb("w_q", [P, 2, H0 * DK])
    w_k2 = sb("w_k2", [P, 2, 2, DK])
    w_v2 = sb("w_v2", [P, 2, 2, DK])
    w_o = sb("w_o", [P, NPAIR, D])
    gate_rows = sb("gate_rows", [NE, D])
    w_gate = sb("w_gate", [P, 2, P])
    bq_rows = sb("bq_rows", [NPAIR, P])
    b_q = sb("b_q", [P, NPAIR])
    b_k2 = sb("b_k2", [P, 1])
    b_v2 = sb("b_v2", [P, 1])
    b_o = sb("b_o", [R, D])
    pos = sb("pos", [R, D])
    base = sb("base", [R, D])
    table = sb("table", [R, D])
    lnw = sb("lnw", [R, D])
    lnb = sb("lnb", [R, D])
    vmask = sb("vmask", [2 * S, P])
    ones_s = sb("ones_s", [2 * S, P])

    x_in = [sb(f"x_in{i}", [IPG * NPH, C, PATCH * IMG]) for i in range(2)]
    x_pat = sb("x_pat", [IPG * NPH, C, NPH, PATCH * PATCH])
    patT = sb("patT", [P, KP, GT])
    h0 = sb("h0", [R, 2, D])
    h0b = [sb(f"h0b{i}", [R, 2, D]) for i in range(2)]
    stats0 = sb("stats0", [R, 2, 6])
    mv0 = sb("mv0", [R, 2, 2])
    ve0 = sb("ve0", [R, 2])
    rstd0 = sb("rstd0", [R, 2])
    xn = sb("xn", [R, 2, D])
    xnT = sb("xnT", [P, 2, GT])
    QT = [sb(f"QT{i}", [P, IPG, NPAIR, S]) for i in range(2)]
    Kbd = [sb(f"Kbd{i}", [P, IPG + 1, 2, S]) for i in range(2)]
    VT = sb("VT", [P, IPG, 2, S])
    Vbd = [sb(f"Vbd{i}", [2 * S, IPG, P]) for i in range(2)]
    NCH = 3
    SUB = 2 * NCH * 2
    W3 = 2 * NCH * 2 * S
    smax = sb("smax", [R, 3, SUB])
    ssum = sb("ssum", [R, 3, SUB])
    sinv = sb("sinv", [R, 3, SUB])
    prob = sb("prob", [R, 3, W3])
    PT = [sb(f"PT{i}", [2 * S, NPAIR * S]) for i in range(2)]
    OT = sb("OT", [P, NPAIR, GT])
    h1 = [sb(f"h1_{i}", [R, 2, D]) for i in range(2)]
    stats1 = sb("stats1", [R, 2, 6])
    mv1 = sb("mv1", [R, 2, 2])
    ve1 = sb("ve1", [R, 2])
    rstd1 = sb("rstd1", [R, 2])
    xn1 = sb("xn1", [R, 2, D])
    res = sb("res", [R, 2, D])
    xn1T = sb("xn1T", [P, 2, GT])
    lmax = sb("lmax", [R, 2])
    lexp = sb("lexp", [R, 2, NE])
    lsum = sb("lsum", [R, 2])
    linv = sb("linv", [R, 2])
    stats2 = sb("stats2", [R, 2, 6])
    mv2 = sb("mv2", [R, 2, 2])
    ve2 = sb("ve2", [R, 2])
    rstd2 = sb("rstd2", [R, 2])
    yn = sb("yn", [R, 2, D])
    ym = sb("ym", [R, 2, D])
    yo = sb("yo", [R, 2, YW])

    ring = [ctx.enter_context(nc.psum_tensor(f"a_ring{i}", [P, 512], F32)) for i in range(3)]
    pS = [ctx.enter_context(nc.psum_tensor(f"a_score{i}", [P, 512], F32)) for i in range(3)]
    pPT = ctx.enter_context(nc.psum_tensor("a_pt", [P, 512], F32))
    pO = ctx.enter_context(nc.psum_tensor("a_o", [P, 512], F32))

    loaded = sem("loaded")
    base_in, cls_in = sem("base_in"), sem("cls_in")
    cleared, masked = sem("cleared"), sem("masked")
    wT_done, wT_out = sem("wT_done"), sem("wT_out")
    table_made = sem("table_made")
    x_here = [sem(f"x_here{i}") for i in range(2)]
    x_sorted = [sem(f"x_sorted{c}") for c in range(C)]
    xt_done, xt_act, xt_dve = sem("xt_done"), sem("xt_act"), sem("xt_dve")
    emb_done, emb_out, h0b_made = sem("emb_done"), sem("emb_out"), sem("h0b_made")
    ln0_stat, ln0_var, ln0_eps, ln0_rstd, xn_made = (sem(n) for n in ("ln0_stat", "ln0_var", "ln0_eps", "ln0_rstd", "xn_made"))
    xnT_done, xnT_out = sem("xnT_done"), sem("xnT_out")
    q_done, q_act, q_dve = sem("q_done"), sem("q_act"), sem("q_dve")
    kv_done, k_out, v_out = sem("kv_done"), sem("k_out"), sem("v_out")
    vt_done, vt_out = sem("vt_done"), sem("vt_out")
    s_done, s_max, s_sub, s_exp, s_sum, s_inv, s_prob = (sem(n) for n in ("s_done", "s_max", "s_sub", "s_exp", "s_sum", "s_inv", "s_prob"))
    pt_done, pt_out, o_done, o_out = sem("pt_done"), sem("pt_out"), sem("o_done"), sem("o_out")
    wo_done, h1_made = sem("wo_done"), sem("h1_made")
    ln1_stat, ln1_var, ln1_eps, ln1_rstd, xn1_made = (sem(n) for n in ("ln1_stat", "ln1_var", "ln1_eps", "ln1_rstd", "xn1_made"))
    res_made, res_stored = sem("res_made"), sem("res_stored")
    xn1T_done, xn1T_out = sem("xn1T_done"), sem("xn1T_out")
    lg_done, lg_max, lg_sub, lg_exp, lg_sum, lg_inv, lg_out, lg_kept = (
        sem(n) for n in ("lg_done", "lg_max", "lg_sub", "lg_exp", "lg_sum", "lg_inv", "lg_out", "lg_kept"))
    ln2_stat, ln2_var, ln2_eps, ln2_rstd, yn_made, ym_made, y_made, y_stored = (
        sem(n) for n in ("ln2_stat", "ln2_var", "ln2_eps", "ln2_rstd", "yn_made", "ym_made", "y_made", "y_stored"))

    x_dram = x.rearrange("b c (t y) w -> b t c (y w)", t=NPH)
    def sort_pixels(eng, copy, c, f, half, par):
        eng.wait_ge(x_here[1 - par], 16 * IPG * (half + 1 + par))
        wait_alone(eng, const, xt_done, 3 * f)
        src = x_in[1 - par][:, c, :].rearrange("p (y w u) -> p w y u", y=PATCH, w=NPH)
        copy(x_pat[:, c, :, :].rearrange("p w (y u) -> p w y u", y=PATCH), src).then_inc(x_sorted[c], 1)

    acc_t = acc_rows.rearrange("(t p) d -> p t d", p=R)
    y_t = y_rows.rearrange("(t p) d -> p t d", p=R)
    N_LOADS = 20

    def steps(eng, step):
        step(eng, -1, -1, 1, attend=False, front=True, tail=False)
        step(eng, 0, 0, 0, attend=True, front=True, tail=False)
        step(eng, 1, 0, 1, attend=True, front=True, tail=True)
        with eng.Fori(1, NG // 2) as i:
            step(eng, 2 * i, i, 0, attend=True, front=True, tail=True)
            step(eng, 2 * i + 1, i, 1, attend=True, front=True, tail=True)
        step(eng, NG - 1, NG // 2, 0, attend=True, front=False, tail=True)
        step(eng, NG, NG // 2, 1, attend=False, front=False, tail=True)

    with nc.Block() as block:

        @block.sync
        def _(sp):
            loads = 0
            for dst, src in [
                (w_rows[:, :, :], tok_W.rearrange("(a p) k -> p a k", p=P)),
                (w_q[:, :, :], Wq.rearrange("(a p) n -> p a n", p=P)),
                (w_k2[:, :, 0, :], Wk.rearrange("(a p) n -> p a n", p=P)),
                (w_k2[:, :, 1, :], Wk.rearrange("(a p) n -> p a n", p=P)),
                (w_v2[:, :, 0, :], Wv.rearrange("(a p) n -> p a n", p=P)),
                (w_v2[:, :, 1, :], Wv.rearrange("(a p) n -> p a n", p=P)),
                (w_o[:, :, :], Wo.rearrange("(j p) n -> p j n", p=P)),
                (gate_rows[:, :], gate_w),
                (bq_rows[:, :], bq.rearrange("(j p) -> j p", p=P)),
                (b_k2[0:DK, :], bk.rearrange("(p a) -> p a", a=1)),
                (b_k2[DK:P, :], bk.rearrange("(p a) -> p a", a=1)),
                (b_v2[0:DK, :], bv.rearrange("(p a) -> p a", a=1)),
                (b_v2[DK:P, :], bv.rearrange("(p a) -> p a", a=1)),
                (b_o[:, :], bo.rearrange("(a d) -> a d", a=1).broadcast_to([R, D])),
                (lnw[:, :], ln_w.rearrange("(a d) -> a d", a=1).broadcast_to([R, D])),
                (lnb[:, :], ln_b.rearrange("(a d) -> a d", a=1).broadcast_to([R, D])),
                (pos[0:S, :], pos_embed[0]),
                (pos[S:2 * S, :], pos_embed[0]),
                (pos[2 * S:3 * S, :], pos_embed[0]),
            ]:
                sp.dma_start(dst, src).then_inc(loaded, 16)
                loads += 1
            assert loads == N_LOADS - 1
            sp.dma_start(base[:, :], tok_b.rearrange("(a d) -> a d", a=1).broadcast_to([R, D])).then_inc(base_in, 16)
            sp.wait_ge(base_in, 16)
            for i in range(IPT):
                sp.dma_start(base[i * S:i * S + 1, :], cls_token[0]).then_inc(cls_in, 16)

            def images(g, parity):
                for b in range(IPG):
                    n = min(IPG * g + b, NB - 1) if isinstance(g, int) else IPG * g + b
                    sp.dma_start(x_in[parity][b * NPH:(b + 1) * NPH, :, :], x_dram[n]).then_inc(x_here[parity], 16)

            images(0, 0)
            images(1, 1)

            def store(g):
                sp.wait_ge(res_made, g + 1)
                sp.dma_start(acc_t[:, bass.ds(2 * g, 2), :], res[:, :, :]).then_inc(res_stored, 16)
                sp.wait_ge(y_made, g + 1)
                sp.wait_ge(lg_out, g + 1)
                sp.dma_start(y_t[:, bass.ds(2 * g, 2), :], yo[:, :, :]).then_inc(y_stored, 16)

            def x_free(g):
                for c in range(C):
                    sp.wait_ge(x_sorted[c], g + 1)

            for g in range(2):
                x_free(g)
                images(g + 2, g)
            with sp.Fori(1, NG // 2 - 1) as i:
                for u in range(2):
                    x_free(2 * i + u)
                    images(2 * i + u + 2, u)
                    store(2 * i + u - 2)
            x_free(NG - 3)
            images(NG - 1, 0)
            for g in range(NG - 5, NG):
                store(g)
            sp.wait_ge(res_stored, 16 * NG)
            sp.wait_ge(y_stored, 16 * NG)

        @block.tensor
        def _(pe):
            pe.wait_ge(loaded, 16 * (N_LOADS - 1))
            n = 0
            for k in range(0, KP, 2):
                for kk in (k, k + 1):
                    for a in range(2):
                        n += 1
                        mm = nc.tensor.transpose(ring[k // 2][:, (kk - k) * D + a * P:(kk - k) * D + (a + 1) * P],
                                                 w_rows[:, a, kk * P:(kk + 1) * P], const.ident[:, :])
                mm.then_inc(wT_done, 1)
            for a in range(2):
                mm = nc.tensor.transpose(pS[0][:, a * NE:(a + 1) * NE], gate_rows[:, a * P:(a + 1) * P],
                                         const.ident[0:NE, 0:NE])
            mm = nc.tensor.transpose(pS[0][:, 2 * NE:2 * NE + NPAIR], bq_rows[:, :], const.ident[0:NPAIR, 0:NPAIR])
            mm.then_inc(wT_done, 1)
            pe.wait_ge(wT_out, 5)
            pe.wait_ge(cleared, 1)

            def step(pe, g, half, par, attend, front, tail):
                f = g + 1
                fp = 1 - par
                t = g - 1
                def patch_transposes(j):
                    wait_alone(pe, const, x_sorted[j], f + 1)
                    for k in (2 * j, 2 * j + 1):
                        for w in range(NPH):
                            o = (k % 2) * NPH * IPG * NPH + w * IPG * NPH
                            mm = nc.tensor.transpose(ring[j][:, o:o + IPG * NPH],
                                                     x_pat[:, k // 2, w, (k % 2) * P:(k % 2 + 1) * P],
                                                     const.ident[0:IPG * NPH, 0:IPG * NPH])
                    mm.then_inc(xt_done, 1)

                def scores_of(j):
                    pe.wait_ge(s_sub, 3 * g + j - 2) if not isinstance(g, int) or g > 0 else None
                    for b in (2 * j, 2 * j + 1):
                        for c in range(NCH):
                            pair = min(NCH * c, NPAIR - NCH)
                            o = ((b % 2) * NCH + c) * 2 * S
                            mm = nc.tensor.matmul(
                                pS[j][0:R, o:o + R],
                                QT[par][:, b, pair:pair + NCH, :].rearrange("p j s -> p (j s)"),
                                Kbd[par][:, b:b + 2, :, :].rearrange("p b e s -> p (b e s)")[:, 0:R],
                                start=True, stop=True)
                    mm.then_inc(s_done, 1)

                def prob_transposes(b):
                    if b % 2 == 0:
                        pe.wait_ge(s_prob, 3 * g + b // 2 + 1)
                    pe.wait_ge(pt_out, 6 * g + b)
                    for c in range(NCH):
                        pair = min(NCH * c, NPAIR - NCH)
                        o = ((b % 2) * NCH + c) * 2 * S
                        mm = nc.tensor.transpose(pPT[0:2 * S, pair * S:pair * S + R], prob[:, b // 2, o:o + 2 * S],
                                                 const.ident[0:R, 0:R])
                    mm.then_inc(pt_done, 1)

                def values_of(b):
                    pe.wait_ge(pt_out, 6 * g + b + 1)
                    pe.wait_ge(o_out, 6 * g + b)
                    nc.tensor.matmul(pO[:, 0:NPAIR * S], Vbd[par][:, b, :], PT[b % 2][:, :],
                                     start=True, stop=True).then_inc(o_done, 1)

                def q_pairs(j, bank):
                    for m in (2 * j, 2 * j + 1):
                        for k in range(2):
                            mm = nc.tensor.matmul(ring[bank][:, (m % 2) * GT:(m % 2 + 1) * GT],
                                                  w_q[:, k, m * P:(m + 1) * P], xnT[:, k, :],
                                                  start=(k == 0), stop=(k == 1))
                    mm.then_inc(q_done, 1)

                if attend:
                    pe.wait_ge(q_act, 2 * (g + 1))
                    pe.wait_ge(q_dve, 2 * (g + 1))
                    pe.wait_ge(k_out, 2 * (g + 1))
                    for j in range(3):
                        scores_of(j)
                if front:
                    pe.wait_ge(vt_out, 2 * f)
                    patch_transposes(0)
                    patch_transposes(1)
                    if attend:
                        pe.wait_ge(h1_made, g)
                    patch_transposes(2)
                    pe.wait_ge(xt_act, 2 * (f + 1))
                    pe.wait_ge(xt_dve, f + 1)
                    for tile in range(2):
                        for k in range(KP):
                            mm = nc.tensor.matmul(ring[0][0:R, tile * D:(tile + 1) * D],
                                                  patT[:, k, tile * R:(tile + 1) * R], w_tok[:, k, :],
                                                  start=(k == 0), stop=(k == KP - 1))
                    mm.then_inc(emb_done, 1)
                if tail:
                    if not front:
                        pe.wait_ge(vt_out, 2 * NG)
                        pe.wait_ge(h1_made, min(g, NG))
                    pe.wait_ge(xn1_made, 2 * (t + 1))
                    for tile in range(2):
                        for k in range(2):
                            mm = nc.tensor.transpose(ring[1][:, k * GT + tile * R:k * GT + (tile + 1) * R],
                                                     xn1[:, tile, k * P:(k + 1) * P], const.ident[0:R, 0:R])
                    mm.then_inc(xn1T_done, 1)
                if attend:
                    prob_transposes(0)
                    prob_transposes(1)
                    values_of(0)
                if tail:
                    pe.wait_ge(xn1T_out, t + 1)
                    for tile in range(2):
                        for k in range(2):
                            mm = nc.tensor.matmul(ring[2][0:R, tile * P:(tile + 1) * P],
                                                  xn1T[:, k, tile * R:(tile + 1) * R], w_gate[:, k, :],
                                                  start=(k == 0), stop=(k == 1))
                    mm.then_inc(lg_done, 1)
                if attend:
                    values_of(1)
                if front:
                    pe.wait_ge(emb_out, f + 1)
                    pe.wait_ge(xn_made, 2 * (f + 1))
                    for tile in range(2):
                        for k in range(2):
                            mm = nc.tensor.transpose(ring[0][:, k * GT + tile * R:k * GT + (tile + 1) * R],
                                                     xn[:, tile, k * P:(k + 1) * P], const.ident[0:R, 0:R])
                    mm.then_inc(xnT_done, 1)
                if attend:
                    prob_transposes(2)
                if front:
                    pe.wait_ge(xnT_out, f + 1)
                    if tail:
                        pe.wait_ge(xn1T_out, t + 1)
                    q_pairs(0, 1)
                if attend:
                    values_of(2)
                    prob_transposes(3)
                if front:
                    if tail:
                        pe.wait_ge(lg_sub, t + 1)
                    q_pairs(1, 2)
                    q_pairs(2, 0)
                if attend:
                    values_of(3)
                    prob_transposes(4)
                if front:
                    pe.wait_ge(q_act, 2 * f + 1)
                    q_pairs(3, 1)
                if attend:
                    values_of(4)
                    prob_transposes(5)
                if front:
                    pe.wait_ge(q_dve, 2 * f + 1)
                    for n, w in ((0, w_k2), (1, w_v2)):
                        for k in range(2):
                            mm = nc.tensor.matmul(ring[2][:, n * GT:(n + 1) * GT],
                                                  w[:, k, :, :], xnT[:, k, :], start=(k == 0), stop=(k == 1))
                    mm.then_inc(kv_done, 1)
                if attend:
                    values_of(5)
                if front:
                    pe.wait_ge(v_out, f + 1)
                    pe.wait_ge(q_act, 2 * f + 2)
                    for b in range(4):
                        mm = nc.tensor.transpose(ring[0][0:2 * S, b * P:(b + 1) * P], VT[:, b, :, :].rearrange("p e s -> p (e s)"),
                                                 const.ident[:, :])
                    mm.then_inc(vt_done, 1)
                    pe.wait_ge(q_dve, 2 * f + 2)
                    for b in range(4, IPG):
                        mm = nc.tensor.transpose(ring[1][0:2 * S, (b - 4) * P:(b - 3) * P], VT[:, b, :, :].rearrange("p e s -> p (e s)"),
                                                 const.ident[:, :])
                    mm.then_inc(vt_done, 1)
                if attend:
                    if front:
                        pe.wait_ge(k_out, 2 * (f + 1))
                    elif tail:
                        pe.wait_ge(lg_sub, t + 1)
                    pe.wait_ge(o_out, 6 * (g + 1))
                    for tile in range(2):
                        for j in range(NPAIR):
                            mm = nc.tensor.matmul(ring[2][0:R, tile * D:(tile + 1) * D],
                                                  OT[:, j, tile * R:(tile + 1) * R], w_o[:, j, :],
                                                  start=(j == 0), stop=(j == NPAIR - 1))
                    mm.then_inc(wo_done, 1)

            steps(pe, step)

        @block.scalar
        def _(act):
            for j in range(3):
                act.wait_ge(wT_done, j + 1)
                nc.scalar.activation(w_tok[:, 2 * j:2 * j + 2, :].rearrange("p k e -> p (k e)"), ring[j][:, :],
                                     ACT.Copy).then_inc(wT_out, 1)
            act.wait_ge(wT_done, 4)
            act.wait_ge(cleared, 1)
            nc.scalar.activation(w_gate[:, :, 0:NE], pS[0][:, 0:2 * NE].rearrange("p (k e) -> p k e", k=2),
                                 ACT.Copy).then_inc(wT_out, 1)
            nc.scalar.activation(b_q[:, :], pS[0][:, 2 * NE:2 * NE + NPAIR], ACT.Copy).then_inc(wT_out, 1)
            act.wait_ge(wT_out, 5)
            act.wait_ge(loaded, 16 * (N_LOADS - 1))

            def step(act, g, half, par, attend, front, tail):
                f, fp, t = g + 1, 1 - par, g - 1

                def exp_of(j):
                    act.wait_ge(s_sub, 3 * g + j + 1)
                    nc.scalar.activation(prob[:, j, :], prob[:, j, :], ACT.Exp, scale=SCALE0).then_inc(s_exp, 1)

                def patch_out(j):
                    act.wait_ge(xt_done, 3 * f + j + 1)
                    act.wait_ge(emb_done, f)
                    nc.scalar.activation(patch_slots(patT, 2 * j), patch_columns(ring[j], 0), ACT.Copy)
                    nc.scalar.activation(patch_slots(patT, 2 * j + 1), patch_columns(ring[j], 1), ACT.Copy).then_inc(xt_act, 1)

                def q_out(j):
                    act.wait_ge(q_done, 4 * f + j + 1)
                    for m in range(2):
                        last = nc.scalar.activation(QT[fp][:, :, 2 * j + m, :], q_columns(ring[Q_BANK[j]], m), ACT.Identity,
                                                    bias=b_q[:, 2 * j + m:2 * j + m + 1])
                    last.then_inc(q_act, 1)

                def pt_copy(b):
                    act.wait_ge(pt_done, 6 * g + b + 1)
                    if b >= 2:
                        act.wait_ge(o_done, 6 * g + b - 1)
                    else:
                        act.wait_ge(o_done, 6 * g)
                    nc.scalar.activation(PT[b % 2][:, :], pPT[0:2 * S, 0:NPAIR * S], ACT.Copy).then_inc(pt_out, 1)

                if front:
                    sort_pixels(act, lambda o, i: nc.scalar.activation(o, i, ACT.Copy), 0, f, half, par)
                if attend:
                    exp_of(0)
                if front:
                    patch_out(0)
                if attend:
                    exp_of(1)
                if front:
                    patch_out(2)
                if attend:
                    exp_of(2)
                if tail:
                    act.wait_ge(xn1T_done, t + 1)
                    nc.scalar.activation(xn1T[:, :, :].rearrange("p k t -> p (k t)"), ring[1][:, 0:2 * GT],
                                         ACT.Copy).then_inc(xn1T_out, 1)
                if attend:
                    pt_copy(0)
                    pt_copy(1)
                if tail:
                    act.wait_ge(lg_sub, t + 1)
                    nc.scalar.activation(lexp[:, :, :], lexp[:, :, :], ACT.Exp).then_inc(lg_exp, 1)
                if front:
                    act.wait_ge(xnT_done, f + 1)
                    act.wait_ge(kv_done, f)
                    nc.scalar.activation(xnT[:, :, :].rearrange("p k t -> p (k t)"), ring[0][:, 0:2 * GT],
                                         ACT.Copy).then_inc(xnT_out, 1)
                if attend:
                    pt_copy(2)
                if front:
                    q_out(0)
                if attend:
                    pt_copy(3)
                if front:
                    q_out(2)
                if attend:
                    pt_copy(4)
                    pt_copy(5)
                if front:
                    act.wait_ge(kv_done, f + 1)
                    nc.scalar.activation(VT[:, :, :, :], ring[2][:, GT:2 * GT].rearrange("p (b s) -> p b s", s=S).unsqueeze(2).broadcast_to([P, IPG, 2, S]), ACT.Identity, bias=b_v2[:, 0:1]).then_inc(v_out, 1)

            steps(act, step)

        @block.gpsimd
        def _(pool):
            nc.gpsimd.memset(w_gate[:, :, :], 0.0)
            for i in range(2):
                nc.gpsimd.memset(Kbd[i][:, :, :, :], 0.0)
            for b in range(IPG):
                last = nc.gpsimd.memset(patT[:, :, b * S:b * S + 1], 0.0)
            last = nc.gpsimd.memset(ones_s[:, :], 1.0)
            last.then_inc(cleared, 1)
            pool.wait_ge(cleared, 1)
            nc.gpsimd.affine_select(out=vmask[:, 0:DK], in_=ones_s[:, 0:DK], compare_op=ALU.is_gt, fill=0.0,
                                    base=S, pattern=[[0, DK]], channel_multiplier=-1)
            nc.gpsimd.affine_select(out=vmask[:, DK:P], in_=ones_s[:, DK:P], compare_op=ALU.is_ge, fill=0.0,
                                    base=-S, pattern=[[0, DK]], channel_multiplier=1).then_inc(masked, 1)
            pool.wait_ge(loaded, 16 * (N_LOADS - 1))
            pool.wait_ge(cls_in, 16 * IPT)
            nc.gpsimd.tensor_tensor(table[:, :], base[:, :], pos[:, :], ALU.add).then_inc(table_made, 1)

            def rstd_of(mv, ve, rstd, stat, eps, done, n):
                wait_alone(pool, const, stat, 2 * (n + 1))
                nc.gpsimd.tensor_scalar(ve[:, :], mv[:, :, 1], LN_EPS, None, ALU.add).then_inc(eps, 1)
                pool.wait_ge(eps, n + 1)
                nc.gpsimd.tensor_tensor(rstd[:, :], ve[:, :], const.neg_half[0:R, :], ALU.pow).then_inc(done, 1)

            def step(pool, g, half, par, attend, front, tail):
                f, fp, t = g + 1, 1 - par, g - 1
                if tail:
                    rstd_of(mv1, ve1, rstd1, ln1_var, ln1_eps, ln1_rstd, t)

                def scale(j):
                    pool.wait_ge(s_inv, 3 * g + j + 1)
                    pool.wait_ge(s_exp, 3 * g + j + 1)
                    v = prob[:, j, :].rearrange("p (n s) -> p n s", s=S)
                    nc.gpsimd.tensor_tensor(v, v, spread(sinv[:, j, :], S), ALU.mult).then_inc(s_prob, 1)

                if attend:
                    scale(0)
                    scale(1)
                    scale(2)
                if front:
                    rstd_of(mv0, ve0, rstd0, ln0_var, ln0_eps, ln0_rstd, f)
                if tail:
                    rstd_of(mv2, ve2, rstd2, ln2_var, ln2_eps, ln2_rstd, t)
                    pool.wait_ge(xn1_made, 2 * (t + 1))
                    pool.wait_ge(res_stored, 16 * t)
                    nc.gpsimd.tensor_tensor(res[:, :, :], h1[fp][:, :, :], xn1[:, :, :], ALU.add).then_inc(res_made, 1)
                if front:
                    pool.wait_ge(emb_out, f + 1)
                    nc.gpsimd.tensor_tensor(h0b[fp][:, :, :], h0[:, :, :], both(b_o[:, :]), ALU.add).then_inc(h0b_made, 1)
                if tail:
                    pool.wait_ge(yn_made, 2 * (t + 1))
                    nc.gpsimd.tensor_tensor(ym[:, :, :], yn[:, :, :], both(lnw[:, :]), ALU.mult).then_inc(ym_made, 1)
                    pool.wait_ge(ym_made, t + 1)
                    pool.wait_ge(y_stored, 16 * t)
                    nc.gpsimd.tensor_tensor(yo[:, :, 0:D], ym[:, :, :], both(lnb[:, :]), ALU.add).then_inc(y_made, 1)

            steps(pool, step)

        @block.vector
        def _(dve):
            def norm_stats(src, stats, mv, stat, var, n):
                for tile in range(2):
                    nc.vector.bn_stats(stats[:, tile, :], src[:, tile, :]).then_inc(stat, 1)
                for tile in range(2):
                    wait_alone(dve, const, stat, 2 * n + tile + 1)
                    nc.vector.bn_aggr(mv[:, tile, :], stats[:, tile, :]).then_inc(var, 1)

            def normalise(dst, src, mv, rstd, rstd_made, made, n):
                dve.wait_ge(rstd_made, n + 1)
                for tile in range(2):
                    nc.vector.tensor_scalar(dst[:, tile, :], src[:, tile, :], mv[:, tile, 0:1], rstd[:, tile:tile + 1],
                                            ALU.subtract, ALU.mult).then_inc(made, 1)

            dve.wait_ge(masked, 1)
            dve.wait_ge(table_made, 1)
            dve.wait_ge(wT_out, 5)
            dve.wait_ge(loaded, 16 * (N_LOADS - 1))

            def step(dve, g, half, par, attend, front, tail):
                f, fp, t = g + 1, 1 - par, g - 1

                def patch_out(j):
                    dve.wait_ge(xt_done, 3 * f + j + 1)
                    dve.wait_ge(emb_done, f)
                    nc.vector.tensor_copy(patch_slots(patT, 2 * j), patch_columns(ring[j], 0))
                    nc.vector.tensor_copy(patch_slots(patT, 2 * j + 1), patch_columns(ring[j], 1)).then_inc(xt_dve, 1)

                def shift(j):
                    dve.wait_ge(s_done, 3 * g + j + 1)
                    if j == 0:
                        dve.wait_ge(pt_done, 6 * g)
                    v = pS[j][0:R, 0:W3].rearrange("p (n s) -> p n s", s=S)
                    nc.vector.tensor_reduce(smax[:, j, :], v, AX_X, ALU.max).then_inc(s_max, 1)
                    dve.wait_ge(s_max, 3 * g + j + 1)
                    nc.vector.tensor_tensor(prob[:, j, :].rearrange("p (n s) -> p n s", s=S), v,
                                            spread(smax[:, j, :], S), ALU.subtract).then_inc(s_sub, 1)

                def inverse(j):
                    dve.wait_ge(s_exp, 3 * g + j + 1)
                    if j == 0:
                        dve.wait_ge(s_prob, 3 * g)
                    v = prob[:, j, :].rearrange("p (n s) -> p n s", s=S)
                    nc.vector.tensor_reduce(ssum[:, j, :], v, AX_X, ALU.add).then_inc(s_sum, 1)
                    dve.wait_ge(s_sum, 3 * g + j + 1)
                    nc.vector.reciprocal(sinv[:, j, :], ssum[:, j, :]).then_inc(s_inv, 1)

                def o_copy(b):
                    dve.wait_ge(o_done, 6 * g + b + 1)
                    if b == 0:
                        dve.wait_ge(wo_done, g)
                    nc.vector.tensor_copy(OT[:, :, b * S:(b + 1) * S],
                                          pO[:, 0:NPAIR * S].rearrange("p (j s) -> p j s", s=S)).then_inc(o_out, 1)

                def q_out(j):
                    dve.wait_ge(q_done, 4 * f + j + 1)
                    for m in range(2):
                        last = nc.vector.tensor_scalar(QT[fp][:, :, 2 * j + m, :], q_columns(ring[Q_BANK[j]], m),
                                                       b_q[:, 2 * j + m:2 * j + m + 1], None, ALU.add)
                    last.then_inc(q_dve, 1)

                if front:
                    sort_pixels(dve, nc.vector.tensor_copy, 1, f, half, par)
                    sort_pixels(dve, nc.vector.tensor_copy, 2, f, half, par)
                if tail:
                    dve.wait_ge(h1_made, t + 1)
                    norm_stats(h1[fp], stats1, mv1, ln1_stat, ln1_var, t)
                if attend:
                    shift(0)
                if tail:
                    dve.wait_ge(xn1T_done, t)
                    dve.wait_ge(res_made, t)
                    normalise(xn1, h1[fp], mv1, rstd1, ln1_rstd, xn1_made, t)
                if attend:
                    shift(1)
                    inverse(0)
                if front:
                    patch_out(1)
                if attend:
                    shift(2)
                    inverse(1)
                if attend:
                    inverse(2)
                if front:
                    dve.wait_ge(emb_done, f + 1)
                    dve.wait_ge(h0b_made, f)
                    nc.vector.tensor_tensor(h0[:, :, :], ring[0][0:R, :].rearrange("p (t d) -> p t d", t=2),
                                            both(table[:, :]), ALU.add).then_inc(emb_out, 1)
                    dve.wait_ge(emb_out, f + 1)
                    norm_stats(h0, stats0, mv0, ln0_stat, ln0_var, f)
                if tail:
                    dve.wait_ge(xn1_made, 2 * (t + 1))
                    norm_stats(xn1, stats2, mv2, ln2_stat, ln2_var, t)
                if attend:
                    o_copy(0)
                if tail:
                    dve.wait_ge(lg_done, t + 1)
                    dve.wait_ge(lg_exp, t)
                    lv = ring[2][0:R, 0:2 * P].rearrange("p (t e) -> p t e", t=2)[:, :, 0:NE]
                    nc.vector.tensor_reduce(lmax[:, :], lv, AX_X, ALU.max).then_inc(lg_max, 1)
                    dve.wait_ge(lg_max, t + 1)
                    nc.vector.tensor_tensor(lexp[:, :, :], lv, spread(lmax[:, :], NE), ALU.subtract).then_inc(lg_sub, 1)
                if front:
                    dve.wait_ge(xnT_done, f)
                    normalise(xn, h0, mv0, rstd0, ln0_rstd, xn_made, f)
                if attend:
                    o_copy(1)
                if tail:
                    dve.wait_ge(ym_made, t)
                    normalise(yn, xn1, mv2, rstd2, ln2_rstd, yn_made, t)
                    dve.wait_ge(lg_exp, t + 1)
                    nc.vector.tensor_reduce(lsum[:, :], lexp[:, :, :], AX_X, ALU.add).then_inc(lg_sum, 1)
                    dve.wait_ge(lg_sum, t + 1)
                    nc.vector.reciprocal(linv[:, :], lsum[:, :]).then_inc(lg_inv, 1)
                    dve.wait_ge(lg_inv, t + 1)
                    dve.wait_ge(y_stored, 16 * t)
                    nc.vector.tensor_tensor(yo[:, :, D:YW], lexp[:, :, :], spread(linv[:, :], NE), ALU.mult).then_inc(lg_out, 1)
                    nc.vector.tensor_tensor(scores[0:R, bass.ds(2 * t, 2), :], lexp[:, :, :], spread(linv[:, :], NE),
                                            ALU.mult).then_inc(lg_kept, 1)
                    dve.wait_ge(lg_kept, t + 1)
                if attend:
                    o_copy(2)
                if front:
                    q_out(1)
                if attend:
                    o_copy(3)
                if front:
                    q_out(3)
                if attend:
                    o_copy(4)
                if front:
                    dve.wait_ge(v_out, f + 1)
                    for e in range(2):
                        rows = slice(e * DK, (e + 1) * DK)
                        nc.vector.tensor_scalar(Kbd[fp][rows, 0:IPG, e, :],
                                                ring[2][rows, 0:GT].rearrange("p (b s) -> p b s", s=S),
                                                b_k2[rows, 0:1], None, ALU.add).then_inc(k_out, 1)
                if attend:
                    o_copy(5)
                if front:
                    for n, (b0, b1) in enumerate(((0, 4), (4, IPG))):
                        dve.wait_ge(vt_done, 2 * f + n + 1)
                        nc.vector.tensor_tensor(Vbd[fp][:, b0:b1, :],
                                                ring[n][0:2 * S, 0:(b1 - b0) * P].rearrange("p (b d) -> p b d", d=P),
                                                every(vmask[:, :], b1 - b0), ALU.mult).then_inc(vt_out, 1)
                if attend:
                    dve.wait_ge(wo_done, g + 1)
                    dve.wait_ge(h0b_made, g + 1)
                    nc.vector.tensor_tensor(h1[par][:, :, :], ring[2][0:R, :].rearrange("p (t d) -> p t d", t=2),
                                            h0b[par][:, :, :], ALU.add).then_inc(h1_made, 1)

            steps(dve, step)


def expert_choice(nc, ctx, const, scores, fc1s, b1s, fc2s, b2s, acc_rows, y_rows):
    sb = lambda n, s, d=F32: ctx.enter_context(nc.sbuf_tensor(n, s, d))
    sem = lambda n: semaphore(nc, const, "c_" + n)
    ps = lambda n, d=F32: ctx.enter_context(nc.psum_tensor(n, [P, 512], d))
    NF = 8
    F = NF * P
    NST = -(-CAP // P)
    LAST = CAP - (NST - 1) * P
    rows_in = [P] * (NST - 1) + [LAST]
    FAR = 4095.0
    BITS = 30

    valid = sb("valid", [R, NT])
    valid1 = sb("valid1", [R, NT])
    sc = sb("sc", [R, NE, NT])
    cur = sb("cur", [R, NE])
    bit = sb("bit", [R, NE], I32)
    cand = sb("cand", [R, NE])
    over = sb("over", [R, NE, NT], BF16)
    cnt = sb("cnt", [R, NE], BF16)
    kept = sb("kept", [R, NE])
    ones_b = sb("ones_b", [R, P], BF16)
    tri = sb("tri", [R, R], BF16)
    sel = sb("sel", [R, 2, NE, NT], BF16)
    reset = sb("reset", [R, 2 * NE * NT])
    incl = sb("incl", [R, 2, NE, NT])
    excl = sb("excl", [R, 2, NE, NT])
    posn = sb("posn", [R, 2, NE, NT])
    slot_g = sb("slot_g", [R, NE, NT])
    slot_q = sb("slot_q", [R, NE, NT])
    slot_e = sb("slot_e", [R, NE, NT])
    slot = sb("slot", [R, NE, NT], I32)
    hi_i = sb("hi_i", [R, NE, NT], I32)
    lo_i = sb("lo_i", [R, NE, NT], I32)
    hi = sb("hi", [R, NE * NT])
    lo = sb("lo", [R, NE, NT])
    iota_s = sb("iota_s", [R, P], BF16)
    iota_j = sb("iota_j", [R, NST], F32)
    tile_no = sb("tile_no", [R, NE, NT], F32)
    row_no = sb("row_no", [R, 1], F32)
    in_tile = sb("in_tile", [R, NE * NT, NST], F32)
    marks = sb("marks", [R, NE, NT, 2, NST], BF16)
    hot = [sb(f"hot{i}", [R, NT, P], BF16) for i in range(2)]
    idx_f = sb("idx_f", [P, NE, NST])
    idx = sb("idx", [P, NE, NST], I32)
    tokens = [sb(f"tokens{i}", [P, NST], I32) for i in range(2)]

    fc1_rows = [sb(f"fc1_rows{i}", [P, NF, D]) for i in range(2)]
    fc2_rows = [sb(f"fc2_rows{i}", [P, 2, F]) for i in range(2)]
    fc1T = [sb(f"fc1T{i}", [P, 2, F]) for i in range(2)]
    fc2T = [sb(f"fc2T{i}", [P, NF, D]) for i in range(2)]
    b1_rows = sb("b1_rows", [NE, F])
    b1T = sb("b1T", [P, NF, NE])
    b2 = [sb(f"b2_{i}", [P, D]) for i in range(2)]
    yg = [sb(f"yg{i}", [P, NST, YW]) for i in range(2)]
    yT = [sb(f"yT{i}", [P, 2, CAP]) for i in range(2)]
    hT = sb("hT", [P, NF, CAP])
    ob = sb("ob", [P, NST, D])
    ow = sb("ow", [P, NST, D])

    pW = [ps(f"c_w{i}") for i in range(2)]
    pY = [ps(f"c_y{i}") for i in range(2)]
    pH = [ps(f"c_h{i}") for i in range(2)]
    pO = [ps(f"c_o{i}") for i in range(2)]

    made, init = sem("made"), sem("init")
    counted, reduced, summed, kept_made, cur_made, bit_made, cand_made = (
        sem(n) for n in ("counted", "reduced", "summed", "kept_made", "cur_made", "bit_made", "cand_made"))
    routed = sem("routed")
    prefix_done, hot_made, ids_done, idx_made = sem("prefix_done"), sem("hot_made"), sem("ids_done"), sem("idx_made")
    w_here = [sem(f"w_here{i}") for i in range(2)]
    b2_here = [sem(f"b2_here{i}") for i in range(2)]
    b1_here, b1_done, b1_out = sem("b1_here"), sem("b1_done"), sem("b1_out")
    wt_done, wt_act, wt_dve = sem("wt_done"), sem("wt_act"), sem("wt_dve")
    y_here = [sem(f"y_here{i}") for i in range(2)]
    yt_done, yt_out = sem("yt_done"), sem("yt_out")
    h_done, h_out = sem("h_done"), sem("h_out")
    o_done, ob_made, ow_made = sem("o_done"), sem("ob_made"), sem("ow_made")
    scattered, tokens_made = sem("scattered"), sem("tokens_made")

    def steps(eng, step):
        with eng.Fori(0, NE // 2 - 1) as i:
            step(eng, 2 * i, i, 0, prepare=True)
            step(eng, 2 * i + 1, i, 1, prepare=True)
        step(eng, NE - 2, NE // 2 - 1, 0, prepare=True)
        step(eng, NE - 1, NE // 2 - 1, 1, prepare=False)

    with nc.Block() as block:

        @block.sync
        def _(sp):
            fc1_d = fc1s.rearrange("e (j p) d -> e p j d", p=P)
            fc2_d = fc2s.rearrange("e (a p) f -> e p a f", p=P)

            def weights(e, par):
                sp.dma_start(fc1_rows[par][:, :, :], fc1_d[e]).then_inc(w_here[par], 16)
                sp.dma_start(fc2_rows[par][:, :, :], fc2_d[e]).then_inc(w_here[par], 16)

            def bias2(e, par):
                sp.dma_start(b2[par][:, :], b2s[bass.ds(e, 1), :].broadcast_to([P, D])).then_inc(b2_here[par], 16)

            sp.dma_start(b1_rows[:, :], b1s).then_inc(b1_here, 16)
            for e in range(2):
                weights(e, e)
                bias2(e, e)
            with sp.Fori(0, NE // 2 - 1) as i:
                for u in range(2):
                    sp.wait_ge(wt_done, NF * (2 * i + u + 1))
                    weights(2 * i + u + 2, u)
                    sp.wait_ge(ob_made, 2 * (2 * i + u + 1))
                    bias2(2 * i + u + 2, u)

        @block.gpsimd
        def _(pool):
            nc.gpsimd.memset(ones_b[:, :], 1.0)
            nc.gpsimd.memset(valid[:, :], 1.0).then_inc(made, 1)
            pool.wait_ge(made, 1)
            nc.gpsimd.affine_select(out=tri[:, :], in_=ones_b[:, 0:R], compare_op=ALU.is_gt, fill=0.0,
                                    base=0, pattern=[[1, R]], channel_multiplier=-1)
            nc.gpsimd.affine_select(out=valid[:, NT - 1:NT], in_=ones_b[:, 0:1], compare_op=ALU.is_gt, fill=0.0,
                                    base=TOK - (NT - 1) * R, pattern=[[0, 1]], channel_multiplier=-1)
            nc.gpsimd.iota(iota_s[:, :], pattern=[[1, P]], base=0, channel_multiplier=0,
                           allow_small_or_imprecise_dtypes=True)
            nc.gpsimd.iota(iota_j[:, :], pattern=[[1, NST]], base=0, channel_multiplier=0,
                           allow_small_or_imprecise_dtypes=True)
            nc.gpsimd.iota(tile_no[:, :, :], pattern=[[0, NE], [1, NT]], base=0, channel_multiplier=0,
                           allow_small_or_imprecise_dtypes=True)
            nc.gpsimd.iota(row_no[:, :], pattern=[[0, 1]], base=0, channel_multiplier=1,
                           allow_small_or_imprecise_dtypes=True).then_inc(made, 1)

            def gather(e, par):
                nc.gpsimd.tensor_copy(tokens[par][:, :], idx[:, e, :]).then_inc(tokens_made, 1)
                wait_alone(pool, const, tokens_made, e + 1)
                for j in range(NST):
                    n = rows_in[j]
                    nc.gpsimd.indirect_dma_start(
                        out=yg[par][0:n, j, :], out_offset=None, in_=y_rows[:, :],
                        in_offset=bass.IndirectOffsetOnAxis(ap=tokens[par][0:n, j:j + 1], axis=0)).then_inc(y_here[par], 16)

            pool.wait_ge(idx_made, 1)
            gather(0, 0)

            def step(pool, e, half, par, prepare):
                if prepare:
                    pool.wait_ge(yt_done, 2 * e)
                    pool.wait_ge(scattered, 16 * NST * e)
                    gather(e + 1, 1 - par)
                for j in range(NST):
                    wait_alone(pool, const, ow_made, NST * e + j + 1)
                    if j == 0:
                        wait_alone(pool, const, scattered, 16 * NST * e)
                    n = rows_in[j]
                    nc.gpsimd.indirect_dma_start(
                        out=acc_rows[:, :], out_offset=bass.IndirectOffsetOnAxis(ap=tokens[par][0:n, j:j + 1], axis=0),
                        in_=ow[0:n, j, :], in_offset=None, compute_op=ALU.add).then_inc(scattered, 16)

            steps(pool, step)
            pool.wait_ge(scattered, 16 * NST * NE)

        @block.tensor
        def _(pe):
            def weight_transposes(e, half, par, n):
                if n == 0:
                    pe.wait_ge(w_here[par], 32 * (half + 1))
                k = NF * e + n
                if n % 2 == 0:
                    pe.wait_ge(wt_act, NF // 2 * e + n // 2)
                else:
                    pe.wait_ge(wt_dve, NF // 2 * e + n // 2)
                bank = pW[n % 2]
                for q in range(4):
                    if n < 4:
                        src = fc1_rows[par][:, 4 * (n % 2) + q, (n // 2) * P:(n // 2 + 1) * P]
                    else:
                        j, a = 2 * (n - 4) + q // 2, q % 2
                        src = fc2_rows[par][:, a, j * P:(j + 1) * P]
                    mm = nc.tensor.transpose(bank[:, q * P:(q + 1) * P], src, const.ident[:, :])
                mm.then_inc(wt_done, 1)

            pe.wait_ge(b1_here, 16)
            for j in range(NF):
                mm = nc.tensor.transpose(pO[0][:, j * NE:(j + 1) * NE], b1_rows[:, j * P:(j + 1) * P],
                                         const.ident[0:NE, 0:NE])
            mm.then_inc(b1_done, 1)
            for n in range(NF):
                weight_transposes(0, 0, 0, n)

            pe.wait_ge(made, 2)
            with pe.Fori(0, BITS) as i:
                pe.wait_ge(reduced, i + 1)
                nc.tensor.matmul(pH[0][0:R, 0:NE], ones_b[:, 0:R], cnt[:, :], start=True, stop=True).then_inc(summed, 1)
            pe.wait_ge(routed, 4)
            nc.tensor.matmul(pH[0][0:R, 0:2 * NE * NT], tri[:, :], sel[:, :, :, :].rearrange("p a e t -> p (a e t)"),
                             start=True, stop=True)
            nc.tensor.matmul(pH[1][0:R, 0:2 * NE * NT], ones_b[:, 0:R], sel[:, :, :, :].rearrange("p a e t -> p (a e t)"),
                             start=True, stop=True).then_inc(prefix_done, 1)
            with pe.Fori(0, NE // 2) as i:
                for u in range(2):
                    e = 2 * i + u
                    pe.wait_ge(hot_made, e + 1)
                    for t in range(NT):
                        mm = nc.tensor.matmul(pY[0][:, bass.ds(e * 2 * NST, 2 * NST)], hot[u][:, t, :],
                                              marks[:, e, t, :, :].rearrange("p v j -> p (v j)"),
                                              start=(t == 0), stop=(t == NT - 1))
                    mm.then_inc(ids_done, 1)

            def row_transposes(e, half, par):
                pe.wait_ge(y_here[par], 16 * NST * (half + 1))
                pe.wait_ge(yt_out, 2 * e)
                for k in range(2):
                    for j in range(NST):
                        n = rows_in[j]
                        mm = nc.tensor.transpose(pY[k][:, j * P:j * P + n], yg[par][0:n, j, k * P:(k + 1) * P],
                                                 const.ident[0:n, 0:n])
                    mm.then_inc(yt_done, 1)

            pe.wait_ge(idx_made, 1)
            row_transposes(0, 0, 0)

            def step(pe, e, half, par, prepare):
                pe.wait_ge(yt_out, 2 * (e + 1))
                pe.wait_ge(wt_act, NF // 2 * (e + 1))
                pe.wait_ge(wt_dve, NF // 2 * (e + 1))
                for j in range(NF):
                    pe.wait_ge(h_out, NF * e + max(j - 1, 0))
                    for k in range(2):
                        mm = nc.tensor.matmul(pH[j % 2][:, 0:CAP], fc1T[par][:, k, j * P:(j + 1) * P], yT[par][:, k, :],
                                              start=(k == 0), stop=(k == 1))
                    mm.then_inc(h_done, 1)
                    if prepare:
                        weight_transposes(e + 1, half + par, 1 - par, j)
                if prepare:
                    row_transposes(e + 1, half + par, 1 - par)
                pe.wait_ge(h_out, NF * (e + 1))
                pe.wait_ge(ob_made, 2 * e)
                for j in range(NST):
                    n = rows_in[j]
                    for f in range(NF):
                        mm = nc.tensor.matmul(pO[j // 2][0:n, (j % 2) * D:(j % 2 + 1) * D], hT[:, f, j * P:j * P + n],
                                              fc2T[par][:, f, :], start=(f == 0), stop=(f == NF - 1))
                    if j:
                        mm.then_inc(o_done, 1)

            steps(pe, step)

        @block.scalar
        def _(act):
            act.wait_ge(b1_done, 1)
            nc.scalar.activation(b1T[:, :, :].rearrange("p j e -> p (j e)"), pO[0][:, 0:NF * NE], ACT.Copy).then_inc(b1_out, 1)
            act.wait_ge(b1_out, 1)

            def weights_out(e, par, n):
                act.wait_ge(wt_done, NF * e + n + 1)
                nc.scalar.activation(*weight_bank(par, n), ACT.Copy).then_inc(wt_act, 1)

            def weight_bank(par, n):
                if n < 4:
                    return fc1T[par][:, n // 2, (n % 2) * 4 * P:(n % 2 + 1) * 4 * P], pW[n % 2][:, :]
                return fc2T[par][:, 2 * (n - 4):2 * (n - 3), :].rearrange("p j d -> p (j d)"), pW[n % 2][:, :]

            for n in range(0, NF, 2):
                weights_out(0, 0, n)

            def step(act, e, half, par, prepare):
                for j in range(NF):
                    act.wait_ge(h_done, NF * e + j + 1)
                    if j == 0:
                        act.wait_ge(o_done, 2 * e)
                    nc.scalar.activation(hT[:, j, :], pH[j % 2][:, 0:CAP], ACT.Gelu_apprx_tanh,
                                         bias=b1T[:, j, bass.ds(e, 1)]).then_inc(h_out, 1)
                    if prepare and j % 2 == 0:
                        weights_out(e + 1, 1 - par, j)

            steps(act, step)

        @block.vector
        def _(dve):
            def weights_out(e, par, n):
                dve.wait_ge(wt_done, NF * e + n + 1)
                if n < 4:
                    dst = fc1T[par][:, n // 2, (n % 2) * 4 * P:(n % 2 + 1) * 4 * P]
                else:
                    dst = fc2T[par][:, 2 * (n - 4):2 * (n - 3), :].rearrange("p j d -> p (j d)")
                nc.vector.tensor_copy(dst, pW[n % 2][:, :]).then_inc(wt_dve, 1)

            for n in range(1, NF, 2):
                weights_out(0, 0, n)
            link = [0]

            def chained(ins):
                link[0] += 1
                ins.then_inc(init, 1)
                dve.wait_ge(init, link[0])

            dve.wait_ge(made, 2)
            nc.vector.memset(cur[:, :], 0.0)
            nc.vector.memset(bit[:, :], 1 << (BITS - 1))
            nc.vector.memset(reset[:, :], 1.0)
            chained(nc.vector.tensor_scalar(valid1[:, :], valid[:, :], -1.0, None, ALU.add))
            nc.vector.memset(reset[:, :].rearrange("p (n t) -> p n t", t=NT)[:, :, 0:1], 0.0)
            chained(nc.vector.tensor_tensor(sc[:, :, :], scores[0:R, :, :].rearrange("p t e -> p e t"),
                                            every(valid[:, :], NE), ALU.mult))
            chained(nc.vector.tensor_tensor(sc[:, :, :], sc[:, :, :], every(valid1[:, :], NE), ALU.add))
            cur_i, cand_i = cur[:, :].bitcast(I32), cand[:, :].bitcast(I32)
            with dve.Fori(0, BITS) as i:
                dve.wait_ge(cur_made, i)
                dve.wait_ge(bit_made, i)
                nc.vector.tensor_tensor(cand_i, cur_i, bit[:, :], ALU.bitwise_or).then_inc(cand_made, 1)
                dve.wait_ge(cand_made, i + 1)
                nc.vector.tensor_tensor(over[:, :, :], sc[:, :, :], spread(cand[:, :], NT), ALU.is_ge).then_inc(counted, 1)
                dve.wait_ge(counted, i + 1)
                with nc.allow_low_precision("counts up to NT are exact in bfloat16"):
                    nc.vector.tensor_reduce(cnt[:, :], over[:, :, :], AX_X, ALU.add).then_inc(reduced, 1)
                nc.vector.tensor_scalar(bit[:, :], bit[:, :], 1, None, ALU.logical_shift_right).then_inc(bit_made, 1)
                dve.wait_ge(summed, i + 1)
                nc.vector.scalar_tensor_tensor(kept[:, :], pH[0][0:R, 0:NE], float(CAP), cand[:, :],
                                               ALU.is_ge, ALU.mult).then_inc(kept_made, 1)
                dve.wait_ge(kept_made, i + 1)
                nc.vector.tensor_tensor(cur[:, :], cur[:, :], kept[:, :], ALU.max).then_inc(cur_made, 1)
            dve.wait_ge(cur_made, BITS)
            nc.vector.tensor_tensor(sel[:, 0, :, :], sc[:, :, :], spread(cur[:, :], NT), ALU.is_gt).then_inc(routed, 2)
            nc.vector.tensor_tensor(sel[:, 1, :, :], sc[:, :, :], spread(cur[:, :], NT), ALU.is_equal).then_inc(routed, 2)
            flat = lambda t: t[:, :, :, :].rearrange("p a e t -> p (a e t)")
            dve.wait_ge(prefix_done, 1)
            chained(nc.vector.tensor_tensor_scan(flat(incl), reset[:, :], pH[1][0:R, 0:2 * NE * NT], 0.0, ALU.mult, ALU.add))
            chained(nc.vector.tensor_tensor(flat(excl), flat(incl), pH[1][0:R, 0:2 * NE * NT], ALU.subtract))
            chained(nc.vector.tensor_tensor(flat(posn), flat(excl), pH[0][0:R, 0:2 * NE * NT], ALU.add))
            over_count = incl[:, 0, :, NT - 1]
            nc.vector.scalar_tensor_tensor(slot_g[:, :, :], posn[:, 0, :, :], -FAR, sel[:, 0, :, :], ALU.add, ALU.mult)
            chained(nc.vector.tensor_tensor(slot_q[:, :, :], posn[:, 1, :, :], spread(over_count, NT), ALU.add))
            chained(nc.vector.scalar_tensor_tensor(slot_e[:, :, :], slot_q[:, :, :], -FAR, sel[:, 1, :, :], ALU.add, ALU.mult))
            chained(nc.vector.scalar_tensor_tensor(slot[:, :, :], slot_g[:, :, :], FAR, slot_e[:, :, :], ALU.add, ALU.add))
            nc.vector.tensor_scalar(hi_i[:, :, :], slot[:, :, :], 7, None, ALU.logical_shift_right)
            chained(nc.vector.tensor_scalar(lo_i[:, :, :], slot[:, :, :], P - 1, None, ALU.bitwise_and))
            nc.vector.tensor_copy(hi[:, :], hi_i[:, :, :].rearrange("p e t -> p (e t)"))
            chained(nc.vector.tensor_copy(lo[:, :, :], lo_i[:, :, :]))
            chained(nc.vector.tensor_tensor(in_tile[:, :, :], spread(hi[:, :], NST), every(iota_j[:, :], NE * NT), ALU.is_equal))
            m = marks[:, :, :, :, :].rearrange("p e t v j -> p (e t) v j")
            nc.vector.tensor_tensor(m[:, :, 0, :], in_tile[:, :, :],
                                    spread(tile_no[:, :, :].rearrange("p e t -> p (e t)"), NST), ALU.mult)
            chained(nc.vector.tensor_scalar(m[:, :, 1, :], in_tile[:, :, :], row_no[:, 0:1], None, ALU.mult))
            with dve.Fori(0, NE // 2) as i:
                for u in range(2):
                    e = 2 * i + u
                    if u == 0:
                        dve.wait_ge(ids_done, e)
                    for t in range(NT):
                        last = nc.vector.tensor_scalar(hot[u][:, t, :], iota_s[:, :], lo[:, e, t:t + 1], None, ALU.is_equal)
                    last.then_inc(hot_made, 1)
            dve.wait_ge(ids_done, NE)
            ids = pY[0][:, 0:NE * 2 * NST].rearrange("p (e v j) -> p e v j", v=2, j=NST)
            chained(nc.vector.tensor_scalar(idx_f[:, :, :], ids[:, :, 0, :], float(R), None, ALU.mult))
            nc.vector.tensor_tensor(idx[:, :, :], idx_f[:, :, :], ids[:, :, 1, :], ALU.add).then_inc(idx_made, 1)

            def rows_out(e, par):
                for k in range(2):
                    dve.wait_ge(yt_done, 2 * e + k + 1)
                    nc.vector.tensor_copy(yT[par][:, k, :], pY[k][:, 0:CAP]).then_inc(yt_out, 1)

            rows_out(0, 0)

            def step(dve, e, half, par, prepare):
                if prepare:
                    for n in range(1, NF, 2):
                        weights_out(e + 1, 1 - par, n)
                    rows_out(e + 1, 1 - par)
                dve.wait_ge(b2_here[par], 16 * (half + 1))
                dve.wait_ge(ow_made, NST * e)
                for bank, j0, nt, n in ((0, 0, 2, P), (1, 2, 1, LAST)):
                    dve.wait_ge(o_done, 2 * e + bank + 1)
                    nc.vector.tensor_tensor(ob[0:n, j0:j0 + nt, :],
                                            pO[bank][0:n, 0:nt * D].rearrange("p (t d) -> p t d", t=nt),
                                            every(b2[par][0:n, :], nt), ALU.add).then_inc(ob_made, 1)
                dve.wait_ge(ob_made, 2 * (e + 1))
                dve.wait_ge(scattered, 16 * NST * e)
                for j in range(NST):
                    n = rows_in[j]
                    nc.vector.tensor_scalar(ow[0:n, j, :], ob[0:n, j, :], yg_score(par, n, j, e), None,
                                            ALU.mult).then_inc(ow_made, 1)

            def yg_score(par, n, j, e):
                return yg[par][0:n, j, bass.ds(D + e, 1)]

            steps(dve, step)


def retention(nc, ctx, const, acc_rows, rWq, rWk, rWv, rWg, rWo, gn_gamma, gn_beta, router_w, sWg, sWu, sWd,
              sum_rows, x3_rows, logits):
    sb = lambda n, s, d=F32: ctx.enter_context(nc.sbuf_tensor("r_" + n, s, d))
    sem = lambda n: semaphore(nc, const, "r_" + n)
    H1 = rWq.shape[0]
    FS = sWg.shape[1]
    FB = FS - P
    PER = IPG * H1

    w_q = sb("w_q", [P, H1, P])
    w_k = sb("w_k", [P, H1, P])
    w_v = sb("w_v", [P, H1, P])
    w_g = sb("w_g", [P, 2, D])
    w_o = sb("w_o", [P, 2, D])
    w_r = sb("w_r", [P, 2, P])
    w_sg = sb("w_sg", [P, 2, FS])
    w_su = sb("w_su", [P, 2, FS])
    w_sd0 = sb("w_sd0", [P, D])
    w_sd1 = sb("w_sd1", [FB, D])
    gam_rows = sb("gam_rows", [2, P])
    bet_rows = sb("bet_rows", [2, P])
    gam_bet = sb("gam_bet", [P, 4])
    gap = sb("gap", [R, R])
    gammas = sb("gammas", [R, R])
    power = sb("power", [R, H1, R])
    decay_a = sb("decay_a", [R, H1, R])
    decay = sb("decay", [R, H1, R])
    pair_a = sb("pair_a", [P, P])
    pair_b = sb("pair_b", [P, P])
    pair = sb("pair", [P, P])
    half_neg = sb("half_neg", [P, PER])

    h2 = [sb(f"h2_{i}", [R, 2, D]) for i in range(2)]
    stats2 = sb("stats2", [R, 2, 6])
    mv2 = sb("mv2", [R, 2, 2])
    ve2 = sb("ve2", [R, 2])
    rstd2 = sb("rstd2", [R, 2])
    xn = sb("xn", [R, 2, D])
    xnT = sb("xnT", [P, 2, GT])
    QT = [sb(f"QT{i}", [P, H1, GT]) for i in range(2)]
    KT = [sb(f"KT{i}", [P, H1, GT]) for i in range(2)]
    V = [sb(f"V{i}", [R, 2, H1, P]) for i in range(2)]
    gate = [sb(f"gate{i}", [P, 2, GT]) for i in range(2)]
    dec = sb("dec", [R, 2, H1, R])
    ysum = sb("ysum", [P, PER])
    ymean = sb("ymean", [P, PER])
    yc = sb("yc", [P, PER, S])
    ysq = sb("ysq", [P, PER, S])
    ysum2 = sb("ysum2", [P, PER])
    yvar = sb("yvar", [P, PER])
    yrstd = sb("yrstd", [P, PER])
    z1 = sb("z1", [P, 2, GT])
    z2 = sb("z2", [P, 2, GT])
    zT = sb("zT", [P, 2, GT])
    h3 = [sb(f"h3_{i}", [R, 2, D]) for i in range(2)]
    stats3 = sb("stats3", [R, 2, 6])
    mv3 = sb("mv3", [R, 2, 2])
    ve3 = sb("ve3", [R, 2])
    rstd3 = sb("rstd3", [R, 2])
    x3 = sb("x3", [R, 2, D])
    x3T = sb("x3T", [P, 2, GT])
    sg0 = sb("sg0", [P, GT])
    sg1 = sb("sg1", [FB, GT])
    hid0 = sb("hid0", [P, GT])
    hid1 = sb("hid1", [FB, GT])
    h4 = sb("h4", [R, 2, D])

    bank = [ctx.enter_context(nc.psum_tensor(f"r_bank{i}", [P, 512], F32)) for i in range(8)]
    pS, pY, pM, pF0, pF1, pT0, pT1, pT2 = bank

    loaded, made, setup = sem("loaded"), sem("made"), sem("setup")
    gb_done, gb_out = sem("gb_done"), sem("gb_out")
    h2_here = [sem(f"h2_here{i}") for i in range(2)]
    ln2_stat, ln2_var, ln2_eps, ln2_rstd, xn_made = (sem(n) for n in ("ln2_stat", "ln2_var", "ln2_eps", "ln2_rstd", "xn_made"))
    xnT_done, xnT_out = sem("xnT_done"), sem("xnT_out")
    q_done, q_out, k_done, k_out, v_done, v_out, g_done, g_out = (
        sem(n) for n in ("q_done", "q_out", "k_done", "k_out", "v_done", "v_out", "g_done", "g_out"))
    s_done, s_out, y_done, y_sum, m_done, m_out, y_cent, y_sq, y_sum2, v2_done, y_var, y_rstd = (
        sem(n) for n in ("s_done", "s_out", "y_done", "y_sum", "m_done", "m_out", "y_cent", "y_sq", "y_sum2",
                         "v2_done", "y_var", "y_rstd"))
    z1_made, z2_made, z_made, wo_done, h3_made = (sem(n) for n in ("z1_made", "z2_made", "z_made", "wo_done", "h3_made"))
    ln3_stat, ln3_var, ln3_eps, ln3_rstd, x3_made, x3_stored = (
        sem(n) for n in ("ln3_stat", "ln3_var", "ln3_eps", "ln3_rstd", "x3_made", "x3_stored"))
    x3T_done, x3T_out, lg_done, lg_out = sem("x3T_done"), sem("x3T_out"), sem("lg_done"), sem("lg_out")
    sh_done, silu_done, hid_made, dn_done, h4_made, h4_stored = (
        sem(n) for n in ("sh_done", "silu_done", "hid_made", "dn_done", "h4_made", "h4_stored"))

    acc_t = acc_rows.rearrange("(t p) d -> p t d", p=R)
    sum_t = sum_rows[0:NT * R, :].rearrange("(t p) d -> p t d", p=R)
    x3_t = x3_rows.rearrange("(t p) d -> p t d", p=R)
    N_LOADS = 12

    def steps(eng, step):
        step(eng, -1, -1, 1, attend=False, front=True, tail=False)
        step(eng, 0, 0, 0, attend=True, front=True, tail=False)
        step(eng, 1, 0, 1, attend=True, front=True, tail=True)
        with eng.Fori(1, NG // 2) as i:
            step(eng, 2 * i, i, 0, attend=True, front=True, tail=True)
            step(eng, 2 * i + 1, i, 1, attend=True, front=True, tail=True)
        step(eng, NG - 1, NG // 2, 0, attend=True, front=False, tail=True)
        step(eng, NG, NG // 2, 1, attend=False, front=False, tail=True)

    with nc.Block() as block:

        @block.sync
        def _(sp):
            def rows(g, par):
                sp.dma_start(h2[par][:, :, :], acc_t[:, bass.ds(2 * g, 2), :]).then_inc(h2_here[par], 16)

            rows(0, 0)
            rows(1, 1)
            for dst, src in [
                (gam_rows[:, :], gn_gamma.rearrange("(k p) -> k p", p=P)),
                (bet_rows[:, :], gn_beta.rearrange("(k p) -> k p", p=P)),
                (w_q[:, :, :], rWq.rearrange("h p n -> p h n")),
                (w_k[:, :, :], rWk.rearrange("h p n -> p h n")),
                (w_v[:, :, :], rWv.rearrange("h p n -> p h n")),
                (w_g[:, :, :], rWg.rearrange("(k p) n -> p k n", p=P)),
                (w_o[:, :, :], rWo.rearrange("(k p) n -> p k n", p=P)),
                (w_sg[:, :, :], sWg.rearrange("(k p) n -> p k n", p=P)),
                (w_su[:, :, :], sWu.rearrange("(k p) n -> p k n", p=P)),
                (w_sd0[:, :], sWd[0:P, :]),
                (w_sd1[:, :], sWd[P:FS, :]),
            ]:
                sp.dma_start(dst, src).then_inc(loaded, 16)
            sp.wait_ge(made, 1)
            sp.dma_start(w_r[:, :, 0:NE], router_w.rearrange("(k p) e -> p k e", p=P)).then_inc(loaded, 16)

            def store(g):
                sp.wait_ge(x3_made, 2 * (g + 1))
                sp.dma_start(x3_t[:, bass.ds(2 * g, 2), :], x3[:, :, :]).then_inc(x3_stored, 16)
                sp.wait_ge(h4_made, g + 1)
                sp.dma_start(sum_t[:, bass.ds(2 * g, 2), :], h4[:, :, :]).then_inc(h4_stored, 16)

            for g in range(2):
                sp.wait_ge(h3_made, g + 1)
                rows(g + 2, g)
            with sp.Fori(1, NG // 2 - 1) as i:
                for u in range(2):
                    store(2 * i + u - 2)
                    sp.wait_ge(h3_made, 2 * i + u + 1)
                    rows(2 * i + u + 2, u)
            store(NG - 5)
            sp.wait_ge(h3_made, NG - 2)
            rows(NG - 1, 0)
            for g in range(NG - 4, NG):
                store(g)
            sp.wait_ge(x3_stored, 16 * NG)
            sp.wait_ge(h4_stored, 16 * NG)

        @block.tensor
        def _(pe):
            pe.wait_ge(loaded, 16 * N_LOADS)
            nc.tensor.transpose(pS[:, 0:2], gam_rows[:, :], const.ident[0:2, 0:2])
            nc.tensor.transpose(pS[:, 2:4], bet_rows[:, :], const.ident[0:2, 0:2]).then_inc(gb_done, 1)
            pe.wait_ge(gb_out, 1)
            pe.wait_ge(made, 4)

            def step(pe, g, half, par, attend, front, tail):
                f, fp, t = g + 1, 1 - par, g - 1

                def transposes(dst, src, done):
                    for tile in range(2):
                        for k in range(2):
                            mm = nc.tensor.transpose(dst[:, k * GT + tile * R:k * GT + (tile + 1) * R],
                                                     src[:, tile, k * P:(k + 1) * P], const.ident[0:R, 0:R])
                    mm.then_inc(done, 1)

                if attend:
                    pe.wait_ge(q_out, g + 1)
                    pe.wait_ge(k_out, g + 1)
                    pe.wait_ge(s_out, g)
                    for tile in range(2):
                        for h in range(H1):
                            cols = slice(tile * R, (tile + 1) * R)
                            mm = nc.tensor.matmul(pS[0:R, (tile * H1 + h) * R:(tile * H1 + h + 1) * R],
                                                  KT[par][:, h, cols], QT[par][:, h, cols], start=True, stop=True)
                    mm.then_inc(s_done, 1)
                if front:
                    pe.wait_ge(xn_made, 2 * (f + 1))
                    pe.wait_ge(g_out, f)
                    transposes(pF0, xn, xnT_done)
                if tail:
                    pe.wait_ge(x3_made, 2 * (t + 1))
                    pe.wait_ge(lg_out, t)
                    transposes(pT0, x3, x3T_done)
                if attend:
                    pe.wait_ge(s_out, g + 1)
                    pe.wait_ge(v_out, g + 1)
                    pe.wait_ge(y_cent, g)
                    for tile in range(2):
                        for h in range(H1):
                            mm = nc.tensor.matmul(pY[:, h * GT + tile * R:h * GT + (tile + 1) * R], V[par][:, tile, h, :],
                                                  dec[:, tile, h, :], start=True, stop=True)
                    mm.then_inc(y_done, 1)
                if front:
                    pe.wait_ge(xnT_out, f + 1)
                    pe.wait_ge(v_out, f)
                    for h in range(H1):
                        mm = nc.tensor.matmul(pF1[:, h * GT:(h + 1) * GT], w_q[:, h, :], xnT[:, h, :], start=True, stop=True)
                    mm.then_inc(q_done, 1)
                    for h in range(H1):
                        mm = nc.tensor.matmul(pF0[:, h * GT:(h + 1) * GT], w_k[:, h, :], xnT[:, h, :], start=True, stop=True)
                    mm.then_inc(k_done, 1)
                if tail:
                    pe.wait_ge(x3T_out, t + 1)
                    pe.wait_ge(h4_made, t)
                    for n, w in ((0, w_sg), (1, w_su)):
                        for k in range(2):
                            nc.tensor.matmul(pT1[:, n * GT:(n + 1) * GT], w[:, k, 0:P], x3T[:, k, :],
                                             start=(k == 0), stop=(k == 1))
                    for n, w in ((0, w_sg), (1, w_su)):
                        for k in range(2):
                            mm = nc.tensor.matmul(pT2[0:FB, n * GT:(n + 1) * GT], w[:, k, P:FS], x3T[:, k, :],
                                                  start=(k == 0), stop=(k == 1))
                    mm.then_inc(sh_done, 1)
                if attend:
                    pe.wait_ge(y_sum, g + 1)
                    pe.wait_ge(h3_made, g)
                    nc.tensor.matmul(pM[:, 0:PER], pair[:, :], ysum[:, :], start=True, stop=True).then_inc(m_done, 1)
                if front:
                    pe.wait_ge(q_out, f + 1)
                    for tile in range(2):
                        for h in range(H1):
                            mm = nc.tensor.matmul(pF1[0:R, (tile * H1 + h) * P:(tile * H1 + h + 1) * P],
                                                  xnT[:, h, tile * R:(tile + 1) * R], w_v[:, h, :], start=True, stop=True)
                    mm.then_inc(v_done, 1)
                    pe.wait_ge(k_out, f + 1)
                    for m in range(2):
                        for k in range(2):
                            mm = nc.tensor.matmul(pF0[:, m * GT:(m + 1) * GT], w_g[:, k, m * P:(m + 1) * P], xnT[:, k, :],
                                                  start=(k == 0), stop=(k == 1))
                    mm.then_inc(g_done, 1)
                if tail:
                    for tile in range(2):
                        for k in range(2):
                            mm = nc.tensor.matmul(pT0[0:R, tile * P:(tile + 1) * P], x3T[:, k, tile * R:(tile + 1) * R],
                                                  w_r[:, k, :], start=(k == 0), stop=(k == 1))
                    mm.then_inc(lg_done, 1)
                if attend:
                    pe.wait_ge(y_sum2, g + 1)
                    pe.wait_ge(m_out, g + 1)
                    nc.tensor.matmul(pM[:, 0:PER], pair[:, :], ysum2[:, :], start=True, stop=True).then_inc(v2_done, 1)
                if tail:
                    pe.wait_ge(hid_made, 2 * (t + 1))
                    for tile in range(2):
                        cols = slice(tile * R, (tile + 1) * R)
                        nc.tensor.matmul(pT1[0:R, tile * D:(tile + 1) * D], hid0[:, cols], w_sd0[:, :], start=True, stop=False)
                        mm = nc.tensor.matmul(pT1[0:R, tile * D:(tile + 1) * D], hid1[:, cols], w_sd1[:, :],
                                              start=False, stop=True)
                    mm.then_inc(dn_done, 1)
                if attend:
                    pe.wait_ge(z_made, g + 1)
                    pe.wait_ge(y_var, g + 1)
                    for tile in range(2):
                        for k in range(2):
                            mm = nc.tensor.matmul(pM[0:R, tile * D:(tile + 1) * D], zT[:, k, tile * R:(tile + 1) * R],
                                                  w_o[:, k, :], start=(k == 0), stop=(k == 1))
                    mm.then_inc(wo_done, 1)

            steps(pe, step)

        @block.scalar
        def _(act):
            act.wait_ge(gb_done, 1)
            nc.scalar.activation(gam_bet[:, :], pS[:, 0:4], ACT.Copy).then_inc(gb_out, 1)
            act.wait_ge(gb_out, 1)

            def step(act, g, half, par, attend, front, tail):
                f, fp, t = g + 1, 1 - par, g - 1

                def out_of(dst, src, func, done, out, n):
                    act.wait_ge(done, n + 1)
                    nc.scalar.activation(dst, src, func).then_inc(out, 1)

                flat = lambda a: a[:, :, :].rearrange("p a b -> p (a b)")
                if front:
                    act.wait_ge(g_done, f)
                    out_of(flat(xnT), pF0[:, 0:2 * GT], ACT.Copy, xnT_done, xnT_out, f)
                if tail:
                    act.wait_ge(lg_done, t)
                    out_of(flat(x3T), pT0[:, 0:2 * GT], ACT.Copy, x3T_done, x3T_out, t)
                if front:
                    out_of(flat(QT[fp]), pF1[:, 0:2 * GT], ACT.Copy, q_done, q_out, f)
                    out_of(flat(KT[fp]), pF0[:, 0:2 * GT], ACT.Copy, k_done, k_out, f)
                if tail:
                    act.wait_ge(sh_done, t + 1)
                    nc.scalar.activation(sg0[:, :], pT1[:, 0:GT], ACT.Silu)
                    nc.scalar.activation(sg1[:, :], pT2[0:FB, 0:GT], ACT.Silu).then_inc(silu_done, 1)
                if attend:
                    act.wait_ge(y_cent, g + 1)
                    nc.scalar.activation(ysq[:, :, :], yc[:, :, :], ACT.Square).then_inc(y_sq, 1)
                if front:
                    act.wait_ge(g_done, f + 1)
                    act.wait_ge(z_made, f - 1) if attend else None
                    out_of(flat(gate[fp]), pF0[:, 0:2 * GT], ACT.Relu, g_done, g_out, f)
                if attend:
                    act.wait_ge(z1_made, g + 1)
                    act.wait_ge(z_made, g)
                    for k in range(2):
                        last = nc.scalar.activation(z2[:, k, :], z1[:, k, :], ACT.Identity, bias=gam_bet[:, 2 + k:3 + k],
                                                    scale=gam_bet[:, k:k + 1])
                    last.then_inc(z2_made, 1)

            steps(act, step)

        @block.gpsimd
        def _(pool):
            nc.gpsimd.memset(w_r[:, :, :], 0.0).then_inc(made, 1)
            nc.gpsimd.memset(half_neg[:, :], -0.5)
            nc.gpsimd.iota(gap[:, :], pattern=[[1, R]], base=0, channel_multiplier=-1, allow_small_or_imprecise_dtypes=True)
            for h in range(H1):
                nc.gpsimd.memset(gammas[:, :], 1.0 - 2.0 ** (-5 - h)).then_inc(setup, 1)
                pool.wait_ge(setup, 2 * h + 1)
                nc.gpsimd.tensor_tensor(power[:, h, :], gammas[:, :], gap[:, :], ALU.pow).then_inc(setup, 1)
                pool.wait_ge(setup, 2 * h + 2)
            for b in range(IPT):
                cols = slice(b * S, (b + 1) * S)
                last = nc.gpsimd.affine_select(out=decay_a[:, :, cols], in_=power[:, :, cols], compare_op=ALU.is_ge, fill=0.0,
                                               base=-b * S, pattern=[[0, H1], [0, S]], channel_multiplier=1)
            nc.gpsimd.memset(pair_a[:, :], 1.0 / (2 * S)).then_inc(setup, 1)
            pool.wait_ge(setup, 2 * H1 + 1)
            for b in range(IPT):
                cols = slice(b * S, (b + 1) * S)
                nc.gpsimd.affine_select(out=decay[:, :, cols], in_=decay_a[:, :, cols], compare_op=ALU.is_gt, fill=0.0,
                                        base=(b + 1) * S, pattern=[[0, H1], [0, S]], channel_multiplier=-1)
            pa, pb, pc = (x[:, :].rearrange("p (g e) -> p g e", e=2) for x in (pair_a, pair_b, pair))
            nc.gpsimd.affine_select(out=pb, in_=pa, compare_op=ALU.is_ge, fill=0.0, base=0,
                                    pattern=[[-2, P // 2], [0, 2]], channel_multiplier=1).then_inc(made, 1)
            pool.wait_ge(made, 2)
            nc.gpsimd.affine_select(out=pc, in_=pb, compare_op=ALU.is_ge, fill=0.0, base=1,
                                    pattern=[[2, P // 2], [0, 2]], channel_multiplier=-1).then_inc(made, 2)
            pool.wait_ge(made, 4)

            def rstd_of(mv, ve, rstd, stat, eps, done, n):
                wait_alone(pool, const, stat, 2 * (n + 1))
                nc.gpsimd.tensor_scalar(ve[:, :], mv[:, :, 1], LN_EPS, None, ALU.add).then_inc(eps, 1)
                pool.wait_ge(eps, n + 1)
                nc.gpsimd.tensor_tensor(rstd[:, :], ve[:, :], const.neg_half[0:R, :], ALU.pow).then_inc(done, 1)

            def step(pool, g, half, par, attend, front, tail):
                f, fp, t = g + 1, 1 - par, g - 1
                if front:
                    rstd_of(mv2, ve2, rstd2, ln2_var, ln2_eps, ln2_rstd, f)
                if tail:
                    rstd_of(mv3, ve3, rstd3, ln3_var, ln3_eps, ln3_rstd, t)
                if attend:
                    pool.wait_ge(y_var, g + 1)
                    nc.gpsimd.tensor_tensor(yrstd[:, :], yvar[:, :], half_neg[:, :], ALU.pow).then_inc(y_rstd, 1)
                    pool.wait_ge(y_rstd, g + 1)
                    pool.wait_ge(z2_made, g)
                    nc.gpsimd.tensor_tensor(z1[:, :, :].rearrange("p k (b s) -> p (k b) s", s=S), yc[:, :, :],
                                            spread(yrstd[:, :], S), ALU.mult).then_inc(z1_made, 1)
                    pool.wait_ge(z2_made, g + 1)
                    pool.wait_ge(g_out, g + 1)
                    pool.wait_ge(wo_done, g)
                    nc.gpsimd.tensor_tensor(zT[:, :, :], z2[:, :, :], gate[par][:, :, :], ALU.mult).then_inc(z_made, 1)

            steps(pool, step)

        @block.vector
        def _(dve):
            def norm_stats(src, stats, mv, stat, var, n):
                for tile in range(2):
                    nc.vector.bn_stats(stats[:, tile, :], src[:, tile, :]).then_inc(stat, 1)
                for tile in range(2):
                    wait_alone(dve, const, stat, 2 * n + tile + 1)
                    nc.vector.bn_aggr(mv[:, tile, :], stats[:, tile, :]).then_inc(var, 1)

            def normalise(dst, src, mv, rstd, rstd_made, made_, n):
                dve.wait_ge(rstd_made, n + 1)
                for tile in range(2):
                    nc.vector.tensor_scalar(dst[:, tile, :], src[:, tile, :], mv[:, tile, 0:1], rstd[:, tile:tile + 1],
                                            ALU.subtract, ALU.mult).then_inc(made_, 1)

            dve.wait_ge(made, 4)

            def step(dve, g, half, par, attend, front, tail):
                f, fp, t = g + 1, 1 - par, g - 1
                if front:
                    dve.wait_ge(h2_here[fp], 16 * (half + 1 + par))
                    norm_stats(h2[fp], stats2, mv2, ln2_stat, ln2_var, f)
                if tail:
                    dve.wait_ge(h3_made, t + 1)
                    norm_stats(h3[fp], stats3, mv3, ln3_stat, ln3_var, t)
                if attend:
                    dve.wait_ge(s_done, g + 1)
                    dve.wait_ge(y_done, g)
                    nc.vector.tensor_tensor(dec[:, :, :, :].rearrange("p a b c -> p a (b c)"),
                                            pS[0:R, 0:2 * GT].rearrange("p (a b) -> p a b", a=2),
                                            every(decay[:, :, :].rearrange("p h s -> p (h s)"), 2), ALU.mult).then_inc(s_out, 1)
                if front:
                    dve.wait_ge(xnT_done, f)
                    normalise(xn, h2[fp], mv2, rstd2, ln2_rstd, xn_made, f)
                if tail:
                    dve.wait_ge(x3T_done, t)
                    dve.wait_ge(x3_stored, 16 * t)
                    normalise(x3, h3[fp], mv3, rstd3, ln3_rstd, x3_made, t)
                if attend:
                    dve.wait_ge(y_done, g + 1)
                    dve.wait_ge(m_done, g)
                    yv = pY[:, 0:2 * GT].rearrange("p (n s) -> p n s", s=S)
                    nc.vector.tensor_reduce(ysum[:, :], yv, AX_X, ALU.add).then_inc(y_sum, 1)
                    dve.wait_ge(m_done, g + 1)
                    nc.vector.tensor_copy(ymean[:, :], pM[:, 0:PER]).then_inc(m_out, 1)
                    dve.wait_ge(m_out, g + 1)
                    dve.wait_ge(z1_made, g)
                    dve.wait_ge(y_sq, g)
                    nc.vector.tensor_tensor(yc[:, :, :], yv, spread(ymean[:, :], S), ALU.subtract).then_inc(y_cent, 1)
                if tail:
                    dve.wait_ge(silu_done, t + 1)
                    dve.wait_ge(dn_done, t)
                    nc.vector.tensor_tensor(hid0[:, :], sg0[:, :], pT1[:, GT:2 * GT], ALU.mult).then_inc(hid_made, 1)
                    nc.vector.tensor_tensor(hid1[:, :], sg1[:, :], pT2[0:FB, GT:2 * GT], ALU.mult).then_inc(hid_made, 1)
                if attend:
                    dve.wait_ge(y_sq, g + 1)
                    dve.wait_ge(v2_done, g)
                    nc.vector.tensor_reduce(ysum2[:, :], ysq[:, :, :], AX_X, ALU.add).then_inc(y_sum2, 1)
                if front:
                    dve.wait_ge(v_done, f + 1)
                    nc.vector.tensor_copy(V[fp][:, :, :, :].rearrange("p a b c -> p (a b c)"), pF1[0:R, :]).then_inc(v_out, 1)
                if attend:
                    dve.wait_ge(v2_done, g + 1)
                    dve.wait_ge(y_rstd, g)
                    nc.vector.tensor_scalar(yvar[:, :], pM[:, 0:PER], GN_EPS, None, ALU.add).then_inc(y_var, 1)
                if tail:
                    dve.wait_ge(lg_done, t + 1)
                    nc.vector.tensor_copy(logits[0:R, bass.ds(2 * t, 2), :],
                                          pT0[0:R, 0:2 * P].rearrange("p (t e) -> p t e", t=2)[:, :, 0:NE]).then_inc(lg_out, 1)
                    dve.wait_ge(dn_done, t + 1)
                    dve.wait_ge(h4_stored, 16 * t)
                    nc.vector.tensor_tensor(h4[:, :, :], pT1[0:R, :].rearrange("p (t d) -> p t d", t=2), h3[fp][:, :, :],
                                            ALU.add).then_inc(h4_made, 1)
                if attend:
                    dve.wait_ge(wo_done, g + 1)
                    nc.vector.tensor_tensor(h3[par][:, :, :], pM[0:R, :].rearrange("p (t d) -> p t d", t=2), h2[par][:, :, :],
                                            ALU.add).then_inc(h3_made, 1)

            steps(dve, step)


def token_choice(nc, ctx, const, logits, expert_bias, eWg, eWu, eWd, sum_rows, x3_rows, out):
    sb = lambda n, s, d=F32: ctx.enter_context(nc.sbuf_tensor("t_" + n, s, d))
    sem = lambda n: semaphore(nc, const, "t_" + n)
    ps = lambda n, d=F32: ctx.enter_context(nc.psum_tensor("t_" + n, [P, 512], d))
    TOPK = 2
    F = eWg.shape[2]
    FB = F - P
    NTILE = (TOK * TOPK + NE * (P - 1)) // P
    DUMP = NT * R
    NV = 6
    BIG = 1.0e30

    bias = sb("bias", [R, NE])
    valid = sb("valid", [R, NT])
    sig = sb("sig", [R, NT, NE])
    tot = sb("tot", [R, NT, NE])
    best = sb("best", [R, NT])
    tie = sb("tie", [R, NT, NE])
    rank = sb("rank", [R, NT, NE])
    first = sb("first", [R, NT])
    pick = [sb(f"pick{k}", [R, NT, NE]) for k in range(TOPK)]
    rest = sb("rest", [R, NT, NE])
    prod = sb("prod", [R, NT, NE])
    w = sb("w", [R, TOPK, NT])
    wsum = sb("wsum", [R, NT])
    winv = sb("winv", [R, NT])
    wn = sb("wn", [R, TOPK, NT])
    w_left = sb("w_left", [R, TOPK, NT])
    chosen = sb("chosen", [R, NE, NT], BF16)
    ones_b = sb("ones_b", [R, P], BF16)
    tri = sb("tri", [R, R], BF16)
    reset = sb("reset", [R, NE * NT])
    incl = sb("incl", [R, NE, NT])
    excl = sb("excl", [R, NE, NT])
    posn = sb("posn", [R, NE, NT])
    tiles_i = sb("tiles_i", [R, NE], I32)
    tiles_s = sb("tiles_s", [R, NE], I32)
    tiles = sb("tiles", [R, NE])
    one8 = sb("one8", [R, NE])
    upto = sb("upto", [R, NE])
    start = sb("start", [R, NE])
    slot_all = sb("slot_all", [R, NE, NT])
    slot_f = sb("slot_f", [R, TOPK, NT])
    slot = sb("slot", [R, TOPK, NT], I32)
    hi_i = sb("hi_i", [R, TOPK, NT], I32)
    lo_i = sb("lo_i", [R, TOPK, NT], I32)
    hi = sb("hi", [R, TOPK * NT])
    lo = sb("lo", [R, TOPK * NT])
    iota_s = sb("iota_s", [R, P], BF16)
    iota_j = sb("iota_j", [R, NTILE])
    iota_w = sb("iota_w", [R, NE])
    values = sb("values", [R, NV, TOPK * NT], BF16)
    in_tile = sb("in_tile", [R, TOPK * NT, NTILE], BF16)
    marks = [sb(f"marks{i}", [R, TOPK * NT // 2, NV, NTILE], BF16) for i in range(2)]
    hot = sb("hot", [R, TOPK * NT, P], BF16)
    told = sb("told", [P, NV, NTILE])
    tok_a = sb("tok_a", [P, NTILE])
    tok_b = sb("tok_b", [P, NTILE])
    free = sb("free", [P, NTILE])
    dump = sb("dump", [P, NTILE])
    src_idx = sb("src_idx", [P, NTILE], I32)
    dst_idx = sb("dst_idx", [P, NTILE], I32)
    w_a = sb("w_a", [P, NTILE])
    w_slot = sb("w_slot", [P, NTILE])
    owner_m = sb("owner_m", [1, NTILE, NE])
    owner_f = sb("owner_f", [1, NTILE])
    owner = sb("owner", [1, NTILE], I32)

    w_gu = sb("w_gu", [P, NE, 2, 2 * F])
    w_d0 = sb("w_d0", [P, NE, D])
    w_d1 = sb("w_d1", [FB, NE, D])
    tok_in = [sb(f"tok_in{i}", [P, 1], I32) for i in range(2)]
    tok_out = [sb(f"tok_out{i}", [P, 1], I32) for i in range(2)]
    xg = [sb(f"xg{i}", [P, D]) for i in range(2)]
    xT = [sb(f"xT{i}", [P, 2, P]) for i in range(2)]
    sg = [sb(f"sg{i}", [P, F]) for i in range(2)]
    hid = [sb(f"hid{i}", [P, F]) for i in range(2)]
    hT = [sb(f"hT{i}", [P, 2, P]) for i in range(2)]
    ow = [sb(f"ow{i}", [P, D]) for i in range(2)]

    pX = [ps(f"x{i}") for i in range(2)]
    pG = [ps(f"g{i}") for i in range(2)]
    pT = [ps(f"t{i}") for i in range(2)]
    pD = [ps(f"d{i}") for i in range(2)]

    loaded, w_here, made, link, sig_made = sem("loaded"), sem("w_here"), sem("made"), sem("link"), sem("sig_made")
    chosen_made, prefix_done, marks_made, told_done, idx_made = (
        sem(n) for n in ("chosen_made", "prefix_done", "marks_made", "told_done", "idx_made"))
    tok_in_made, tok_out_made, scattered = sem("tok_in_made"), sem("tok_out_made"), sem("scattered")
    x_here = [sem(f"x_here{i}") for i in range(2)]
    xT_done, xT_out, g_done, silu_done, hid_made, hT_done, hT_out, d_done, ow_made = (
        sem(n) for n in ("xT_done", "xT_out", "g_done", "silu_done", "hid_made", "hT_done", "hT_out", "d_done", "ow_made"))
    out_done = sem("out_done")

    with nc.Block() as block:

        @block.sync
        def _(sp):
            sp.dma_start(bias[:, :], expert_bias.rearrange("(a e) -> a e", a=1).broadcast_to([R, NE])).then_inc(loaded, 16)
            for dst, src in [
                (w_gu[:, :, 0, 0:F], eWg[:, 0:P, :].rearrange("e p f -> p e f")),
                (w_gu[:, :, 1, 0:F], eWg[:, P:D, :].rearrange("e p f -> p e f")),
                (w_gu[:, :, 0, F:2 * F], eWu[:, 0:P, :].rearrange("e p f -> p e f")),
                (w_gu[:, :, 1, F:2 * F], eWu[:, P:D, :].rearrange("e p f -> p e f")),
                (w_d0[:, :, :], eWd[:, 0:P, :].rearrange("e p d -> p e d")),
                (w_d1[:, :, :], eWd[:, P:F, :].rearrange("e p d -> p e d")),
            ]:
                sp.dma_start(dst, src).then_inc(w_here, 16)
            sp.wait_ge(scattered, 16 * NTILE)
            o = out.rearrange("b s d -> (b s) d")
            for q in range(2):
                rows = slice(q * TOK // 2, (q + 1) * TOK // 2)
                sp.dma_start(o[rows, :].rearrange("(a b) d -> a (b d)", a=32),
                             sum_rows[rows, :].rearrange("(a b) d -> a (b d)", a=32)).then_inc(out_done, 16)
            sp.wait_ge(out_done, 32)

        @block.gpsimd
        def _(pool):
            nc.gpsimd.memset(ones_b[:, :], 1.0)
            nc.gpsimd.memset(valid[:, :], 1.0)
            nc.gpsimd.memset(one8[:, :], 1.0)
            nc.gpsimd.memset(values[:, NV - 1, :], 1.0)
            nc.gpsimd.memset(reset[:, :], 1.0).then_inc(made, 1)
            pool.wait_ge(made, 1)
            nc.gpsimd.memset(reset[:, :].rearrange("p (n t) -> p n t", t=NT)[:, :, 0:1], 0.0)
            nc.gpsimd.affine_select(out=tri[:, :], in_=ones_b[:, 0:R], compare_op=ALU.is_gt, fill=0.0,
                                    base=0, pattern=[[1, R]], channel_multiplier=-1)
            nc.gpsimd.affine_select(out=valid[:, NT - 1:NT], in_=ones_b[:, 0:1], compare_op=ALU.is_gt, fill=0.0,
                                    base=TOK - (NT - 1) * R, pattern=[[0, 1]], channel_multiplier=-1)
            iota = lambda o, pattern, base=0, mult=0: nc.gpsimd.iota(
                o, pattern=pattern, base=base, channel_multiplier=mult, allow_small_or_imprecise_dtypes=True)
            iota(iota_s[:, :], [[1, P]])
            iota(iota_j[:, :], [[1, NTILE]])
            iota(iota_w[:, :], [[-1, NE]], base=NE)
            iota(values[:, 0, :].rearrange("p (k t) -> p k t", k=TOPK), [[0, TOPK], [1, NT]])
            iota(values[:, 1, :], [[0, TOPK * NT]], mult=1)
            iota(dump[:, :], [[0, NTILE]], base=DUMP, mult=1).then_inc(made, 1)

            def gather(j, par):
                nc.gpsimd.tensor_copy(tok_in[par][:, :], src_idx[:, bass.ds(j, 1)]).then_inc(tok_in_made, 1)
                wait_alone(pool, const, tok_in_made, j + 1)
                nc.gpsimd.indirect_dma_start(out=xg[par][:, :], out_offset=None, in_=x3_rows[:, :],
                                             in_offset=bass.IndirectOffsetOnAxis(ap=tok_in[par][:, 0:1], axis=0)
                                             ).then_inc(x_here[par], 16)

            def scatter(j, par):
                wait_alone(pool, const, scattered, 16 * j)
                nc.gpsimd.tensor_copy(tok_out[par][:, :], dst_idx[:, bass.ds(j, 1)]).then_inc(tok_out_made, 1)
                pool.wait_ge(tok_out_made, j + 1)
                wait_alone(pool, const, ow_made, j + 1)
                nc.gpsimd.indirect_dma_start(out=sum_rows[:, :],
                                             out_offset=bass.IndirectOffsetOnAxis(ap=tok_out[par][:, 0:1], axis=0),
                                             in_=ow[par][:, :], in_offset=None, compute_op=ALU.add).then_inc(scattered, 16)

            pool.wait_ge(idx_made, 2)
            for j in range(2):
                gather(j, j)
            with pool.Fori(0, NTILE // 2 - 1) as i:
                for u in range(2):
                    pool.wait_ge(xT_done, 2 * i + u + 1)
                    gather(2 * i + u + 2, u)
                    scatter(2 * i + u, u)
            for u in range(2):
                scatter(NTILE - 2 + u, u)

        @block.tensor
        def _(pe):
            pe.wait_ge(chosen_made, 1)
            pe.wait_ge(made, 2)
            c = chosen[:, :, :].rearrange("p e t -> p (e t)")
            nc.tensor.matmul(pX[0][0:R, 0:NE * NT], tri[:, :], c, start=True, stop=True)
            nc.tensor.matmul(pX[1][0:R, 0:NE * NT], ones_b[:, 0:R], c, start=True, stop=True).then_inc(prefix_done, 1)
            for n in range(TOPK * NT):
                if n % NT == 0:
                    pe.wait_ge(marks_made, n // NT + 1)
                mm = nc.tensor.matmul(pG[0][:, 0:NV * NTILE], hot[:, n, :],
                                      marks[n // NT][:, n % NT, :, :].rearrange("p v j -> p (v j)"),
                                      start=(n == 0), stop=(n == TOPK * NT - 1))
            mm.then_inc(told_done, 1)
            pe.wait_ge(w_here, 16 * 6)
            pe.wait_ge(idx_made, 2)

            def transpose_rows(j, half, par):
                pe.wait_ge(x_here[par], 16 * (half + 1))
                pe.wait_ge(xT_out, j)
                for k in range(2):
                    mm = nc.tensor.transpose(pX[par][:, k * P:(k + 1) * P], xg[par][:, k * P:(k + 1) * P], const.ident[:, :])
                mm.then_inc(xT_done, 1)

            def expert(j):
                return pe.value_load(owner[0:1, bass.ds(j, 1)], min_val=0, max_val=NE - 1)

            def gate_up(j, par):
                e = expert(j)
                pe.wait_ge(xT_out, j + 1)
                pe.wait_ge(hid_made, j - 1) if not isinstance(j, int) or j >= 1 else None
                for k in range(2):
                    mm = nc.tensor.matmul(pG[par][:, 0:2 * F], xT[par][:, k, :], w_gu[:, bass.ds(e, 1), k, :],
                                          start=(k == 0), stop=(k == 1))
                mm.then_inc(g_done, 1)

            def hidden_transposes(j, par):
                pe.wait_ge(hid_made, j + 1)
                pe.wait_ge(hT_out, j)
                nc.tensor.transpose(pT[par][:, 0:P], hid[par][:, 0:P], const.ident[:, :])
                nc.tensor.transpose(pT[par][0:FB, P:2 * P], hid[par][:, P:F], const.ident[:, :]).then_inc(hT_done, 1)

            def down(j, par):
                e = expert(j)
                pe.wait_ge(hT_out, j + 1)
                pe.wait_ge(ow_made, j - 1) if not isinstance(j, int) or j >= 1 else None
                nc.tensor.matmul(pD[par][:, 0:D], hT[par][:, 0, :], w_d0[:, bass.ds(e, 1), :], start=True, stop=False)
                nc.tensor.matmul(pD[par][:, 0:D], hT[par][0:FB, 1, :], w_d1[:, bass.ds(e, 1), :],
                                 start=False, stop=True).then_inc(d_done, 1)

            transpose_rows(0, 0, 0)
            gate_up(0, 0)

            def step(j, half, par, more):
                if more:
                    transpose_rows(j + 1, half + par, 1 - par)
                    gate_up(j + 1, 1 - par)
                hidden_transposes(j, par)
                down(j, par)

            step(0, 0, 0, True)
            step(1, 0, 1, True)
            with pe.Fori(1, NTILE // 2 - 1) as i:
                step(2 * i, i, 0, True)
                step(2 * i + 1, i, 1, True)
            step(NTILE - 2, NTILE // 2 - 1, 0, True)
            step(NTILE - 1, NTILE // 2 - 1, 1, False)

        @block.scalar
        def _(act):
            nc.scalar.activation(sig[:, :, :], logits[0:R, :, :], ACT.Sigmoid).then_inc(sig_made, 1)

            def step(j, par):
                act.wait_ge(g_done, j + 1)
                act.wait_ge(hid_made, j)
                nc.scalar.activation(sg[par][:, :], pG[par][:, 0:F], ACT.Silu).then_inc(silu_done, 1)
                act.wait_ge(hT_done, j + 1)
                act.wait_ge(d_done, j)
                nc.scalar.activation(hT[par][:, 0, :], pT[par][:, 0:P], ACT.Copy)
                nc.scalar.activation(hT[par][0:FB, 1, :], pT[par][0:FB, P:2 * P], ACT.Copy).then_inc(hT_out, 1)

            with act.Fori(0, NTILE // 2) as i:
                step(2 * i, 0)
                step(2 * i + 1, 1)

        @block.vector
        def _(dve):
            links = [0]

            def chained(ins):
                links[0] += 1
                ins.then_inc(link, 1)
                dve.wait_ge(link, links[0])

            dve.wait_ge(loaded, 16)
            dve.wait_ge(sig_made, 1)
            dve.wait_ge(made, 2)
            chained(nc.vector.tensor_tensor(tot[:, :, :], sig[:, :, :], every(bias[:, :], NT), ALU.add))
            for k in range(TOPK):
                src = (tot, rest)[k]
                chained(nc.vector.tensor_reduce(best[:, :], src[:, :, :], AX_X, ALU.max))
                chained(nc.vector.tensor_tensor(tie[:, :, :], src[:, :, :], spread(best[:, :], NE), ALU.is_equal))
                chained(nc.vector.tensor_tensor(rank[:, :, :], tie[:, :, :], every(iota_w[:, :], NT), ALU.mult))
                chained(nc.vector.tensor_reduce(first[:, :], rank[:, :, :], AX_X, ALU.max))
                chained(nc.vector.tensor_tensor(pick[k][:, :, :], rank[:, :, :], spread(first[:, :], NE), ALU.is_equal))
                if k == 0:
                    chained(nc.vector.scalar_tensor_tensor(rest[:, :, :], pick[0][:, :, :], -BIG, tot[:, :, :],
                                                           ALU.mult, ALU.add))
                chained(nc.vector.tensor_tensor(prod[:, :, :], pick[k][:, :, :], sig[:, :, :], ALU.mult))
                chained(nc.vector.tensor_reduce(w[:, k, :], prod[:, :, :], AX_X, ALU.add))
            chained(nc.vector.tensor_tensor(prod[:, :, :], pick[0][:, :, :], pick[1][:, :, :], ALU.add))
            nc.vector.tensor_tensor(chosen[:, :, :], prod[:, :, :].rearrange("p t e -> p e t"), every(valid[:, :], NE),
                                    ALU.mult).then_inc(chosen_made, 1)
            chained(nc.vector.tensor_tensor(wsum[:, :], w[:, 0, :], w[:, 1, :], ALU.add))
            chained(nc.vector.tensor_scalar(wsum[:, :], wsum[:, :], 1e-20, None, ALU.add))
            chained(nc.vector.reciprocal(winv[:, :], wsum[:, :]))
            chained(nc.vector.tensor_tensor(wn[:, :, :], w[:, :, :], every(winv[:, :], TOPK), ALU.mult))
            vw = lambda n: values[:, 2 + n, :].rearrange("p (k t) -> p k t", k=TOPK)
            chained(nc.vector.tensor_copy(vw(0), wn[:, :, :]))
            chained(nc.vector.tensor_tensor(w_left[:, :, :], wn[:, :, :], vw(0), ALU.subtract))
            chained(nc.vector.tensor_copy(vw(1), w_left[:, :, :]))
            chained(nc.vector.tensor_tensor(vw(2), w_left[:, :, :], vw(1), ALU.subtract))
            dve.wait_ge(prefix_done, 1)
            fl = lambda a: a[:, :, :].rearrange("p a b -> p (a b)")
            counts = pX[1][0:R, 0:NE * NT]
            chained(nc.vector.tensor_tensor_scan(fl(incl), reset[:, :], counts, 0.0, ALU.mult, ALU.add))
            chained(nc.vector.tensor_tensor(fl(excl), fl(incl), counts, ALU.subtract))
            nc.vector.tensor_tensor(fl(posn), fl(excl), pX[0][0:R, 0:NE * NT], ALU.add)
            chained(nc.vector.tensor_scalar(tiles_i[:, :], incl[:, :, NT - 1], float(P - 1), None, ALU.add))
            chained(nc.vector.tensor_scalar(tiles_s[:, :], tiles_i[:, :], 7, None, ALU.logical_shift_right))
            chained(nc.vector.tensor_copy(tiles[:, :], tiles_s[:, :]))
            chained(nc.vector.tensor_tensor_scan(upto[:, :], one8[:, :], tiles[:, :], 0.0, ALU.mult, ALU.add))
            chained(nc.vector.tensor_tensor(start[:, :], upto[:, :], tiles[:, :], ALU.subtract))
            chained(nc.vector.tensor_scalar(start[:, :], start[:, :], float(P), None, ALU.mult))
            chained(nc.vector.tensor_tensor(slot_all[:, :, :], posn[:, :, :], spread(start[:, :], NT), ALU.add))
            for k in range(TOPK):
                chained(nc.vector.tensor_tensor(prod[:, :, :], pick[k][:, :, :],
                                                slot_all[:, :, :].rearrange("p e t -> p t e"), ALU.mult))
                chained(nc.vector.tensor_reduce(slot_f[:, k, :], prod[:, :, :], AX_X, ALU.add))
            far = float(P * 127)
            chained(nc.vector.scalar_tensor_tensor(slot_f[:, :, :], slot_f[:, :, :], -far, every(valid[:, :], TOPK),
                                                   ALU.add, ALU.mult))
            chained(nc.vector.tensor_scalar(slot[:, :, :], slot_f[:, :, :], far, None, ALU.add))
            nc.vector.tensor_scalar(hi_i[:, :, :], slot[:, :, :], 7, None, ALU.logical_shift_right)
            chained(nc.vector.tensor_scalar(lo_i[:, :, :], slot[:, :, :], P - 1, None, ALU.bitwise_and))
            nc.vector.tensor_copy(hi[:, :], fl(hi_i))
            chained(nc.vector.tensor_copy(lo[:, :], fl(lo_i)))
            nc.vector.tensor_tensor(owner_m[:, :, :], every(upto[0:1, :], NTILE), spread(iota_j[0:1, :], NE), ALU.is_le)
            chained(nc.vector.tensor_tensor(in_tile[:, :, :], spread(hi[:, :], NTILE), every(iota_j[:, :], TOPK * NT),
                                            ALU.is_equal))
            chained(nc.vector.tensor_reduce(owner_f[:, :], owner_m[:, :, :], AX_X, ALU.add))
            nc.vector.tensor_scalar(owner[:, :], owner_f[:, :], float(NE - 1), None, ALU.min).then_inc(idx_made, 1)
            for k in range(TOPK):
                cols = slice(k * NT, (k + 1) * NT)
                for v in range(NV):
                    nc.vector.tensor_tensor(marks[k][:, :, v, :], in_tile[:, cols, :], spread(values[:, v, cols], NTILE), ALU.mult)
                for n in range(k * NT, (k + 1) * NT):
                    last = nc.vector.tensor_scalar(hot[:, n, :], iota_s[:, :], lo[:, n:n + 1], None, ALU.is_equal)
                last.then_inc(marks_made, 1)
            dve.wait_ge(told_done, 1)
            chained(nc.vector.tensor_copy(told[:, :, :], pG[0][:, 0:NV * NTILE].rearrange("p (v j) -> p v j", v=NV)))
            chained(nc.vector.scalar_tensor_tensor(tok_a[:, :], told[:, 0, :], float(R), told[:, 1, :], ALU.mult, ALU.add))
            nc.vector.tensor_copy(src_idx[:, :], tok_a[:, :])
            chained(nc.vector.tensor_scalar(free[:, :], told[:, 5, :], -1.0, 1.0, ALU.mult, ALU.add))
            chained(nc.vector.tensor_tensor(tok_b[:, :], free[:, :], dump[:, :], ALU.mult))
            chained(nc.vector.tensor_tensor(dst_idx[:, :], tok_a[:, :], tok_b[:, :], ALU.add))
            chained(nc.vector.tensor_tensor(w_a[:, :], told[:, 3, :], told[:, 4, :], ALU.add))
            nc.vector.tensor_tensor(w_slot[:, :], w_a[:, :], told[:, 2, :], ALU.add).then_inc(idx_made, 1)
            dve.wait_ge(idx_made, 2)

            def rows_out(j, par):
                dve.wait_ge(xT_done, j + 1)
                nc.vector.tensor_copy(xT[par][:, :, :].rearrange("p k s -> p (k s)"), pX[par][:, 0:2 * P]).then_inc(xT_out, 1)

            rows_out(0, 0)

            def step(j, par, more):
                if more:
                    rows_out(j + 1, 1 - par)
                dve.wait_ge(silu_done, j + 1)
                nc.vector.tensor_tensor(hid[par][:, :], sg[par][:, :], pG[par][:, F:2 * F], ALU.mult).then_inc(hid_made, 1)
                dve.wait_ge(d_done, j + 1)
                dve.wait_ge(scattered, 16 * (j - 1)) if not isinstance(j, int) or j >= 1 else None
                nc.vector.tensor_scalar(ow[par][:, :], pD[par][:, 0:D], w_slot[:, bass.ds(j, 1)], None, ALU.mult).then_inc(ow_made, 1)

            step(0, 0, True)
            step(1, 1, True)
            with dve.Fori(1, NTILE // 2 - 1) as i:
                step(2 * i, 0, True)
                step(2 * i + 1, 1, True)
            step(NTILE - 2, 0, True)
            step(NTILE - 1, 1, False)


def wait_alone(eng, const, sem, value):
    eng.wait_ge(sem, value)
    eng.sem_inc(const.waits_passed, 1)


def semaphore(nc, const, name):
    s = nc.alloc_semaphore(name=name)
    const.semaphores.append(s)
    return s


def end_stage(nc, const):
    nc.clear_and_free_semaphores(const.semaphores)
    nc.all_engine_barrier()
    const.semaphores = []


def twice(ap):
    return every(ap, 2)


def every(ap, n):
    return ap.unsqueeze(1).broadcast_to([ap.shape[0], n, ap.shape[1]])


def both(ap):
    return every(ap, 2)


def spread(ap, n):
    return ap.unsqueeze(2).broadcast_to([ap.shape[0], ap.shape[1], n])


Q_BANK = (1, 2, 0, 1)


def q_columns(bank, m):
    return bank[:, m * GT:(m + 1) * GT].rearrange("p (b s) -> p b s", s=S)


def patch_columns(bank, k):
    n = NPH * IPG * NPH
    return bank[:, (k % 2) * n:(k % 2 + 1) * n].rearrange("p (w b t) -> p w b t", w=NPH, b=IPG)


def patch_slots(patT, k):
    return patT[:, k, :].rearrange("p (b s) -> p b s", s=S)[:, :, 1:S].rearrange("p b (t w) -> p w b t", w=NPH)


_INS = ['x', 'L0_tok_W', 'L0_tok_b', 'L0_tok_cls_token', 'L0_tok_pos_embed', 'L0_attn_Wq', 'L0_attn_bq', 'L0_attn_Wk',
        'L0_attn_bk', 'L0_attn_Wv', 'L0_attn_bv', 'L0_attn_Wo', 'L0_attn_bo', 'L0_ffn_gate_w', 'L0_ffn_ln_w',
        'L0_ffn_ln_b', 'L0_ffn_fc1s', 'L0_ffn_b1s', 'L0_ffn_fc2s', 'L0_ffn_b2s', 'L1_attn_Wq', 'L1_attn_Wk',
        'L1_attn_Wv', 'L1_attn_Wg', 'L1_attn_Wo', 'L1_attn_gn_gamma', 'L1_attn_gn_beta', 'L1_ffn_W_gate_router',
        'L1_ffn_expert_bias', 'L1_ffn_Wg', 'L1_ffn_Wu', 'L1_ffn_Wd', 'L1_ffn_Wg_s', 'L1_ffn_Wu_s', 'L1_ffn_Wd_s']
_OUTS = [((NB, S, D), 'float32')]


def kernel(**inputs):
    import numpy as _np
    import concourse.bacc as _bacc
    from concourse import mybir as _mybir
    from concourse.bass_utils import run_bass_kernel_spmd as _run

    nc = _bacc.Bacc("TRN2", target_bir_lowering=False, num_devices=1)
    arrays, args = {}, []
    for name in _INS:
        a = _np.ascontiguousarray(inputs[name])
        arrays[f"in_{name}_dram"] = a
        args.append(nc.dram_tensor(f"in_{name}_dram", a.shape, _mybir.dt.from_np(a.dtype), kind="ExternalInput").ap())
    for i, (shape, dtype) in enumerate(_OUTS):
        dt = _mybir.dt.from_np(_np.dtype(dtype))
        args.append(nc.dram_tensor(f"out_{i}_dram", shape, dt, kind="ExternalOutput").ap())
    program(nc, *args)
    r = _run(nc, [arrays], core_ids=[0])
    got = tuple(r.results[0][f"out_{i}_dram"] for i in range(len(_OUTS)))
    return got[0]
```

```python
from contextlib import ExitStack

import concourse.bass as bass
from concourse import mybir

ALU = mybir.AluOpType
ACT = mybir.ActivationFunctionType
F32 = mybir.dt.float32
BF16 = mybir.dt.bfloat16
I32 = mybir.dt.int32
AX_X = mybir.AxisListType.X

P = 128
D = 256
NB = 64
C, IMG, PATCH = 3, 96, 16
NPH = IMG // PATCH
S = NPH * NPH + 1
KP = C * PATCH * PATCH // P
H0, DK = 16, 64
NPAIR = H0 // 2
IPT = 3
R = IPT * S
IPG = 2 * IPT
GT = 2 * R
NT = -(-NB // IPG) * 2
NG = NT // 2
TOK = NB * S
NE = 8
CAP = TOK // NE
TOPK = 2
NTILE = (TOK * TOPK + NE * (P - 1)) // P
YW = D + NE
LN_EPS = 1e-5
GN_EPS = 1e-3
SCALE0 = DK ** -0.5


def program(nc, x, tok_W, tok_b, cls_token, pos_embed, Wq, bq, Wk, bk, Wv, bv, Wo, bo, gate_w, ln_w, ln_b,
            fc1s, b1s, fc2s, b2s, rWq, rWk, rWv, rWg, rWo, gn_gamma, gn_beta, router_w, expert_bias,
            eWg, eWu, eWd, sWg, sWu, sWd, out):
    with ExitStack() as ctx:
        acc_rows = nc.dram_tensor("acc_rows", (NT * R, D), F32, kind="Internal").ap()
        y_rows = nc.dram_tensor("y_rows", (NT * R, YW), F32, kind="Internal").ap()
        scores = ctx.enter_context(nc.sbuf_tensor("scores", [P, NT, NE], F32))
        pair_rows = nc.dram_tensor("pair_rows", (TOPK * NT * R + NTILE * P, D), F32, kind="Internal").ap()
        x3_rows = nc.dram_tensor("x3_rows", (NT * R, D), F32, kind="Internal").ap()
        logits = ctx.enter_context(nc.sbuf_tensor("logits", [P, NT, NE], F32))
        const = constants(nc, ctx)
        with ExitStack() as stage:
            embed_and_attend(nc, stage, const, x, tok_W, tok_b, cls_token, pos_embed, Wq, bq, Wk, bk, Wv, bv,
                             Wo, bo, gate_w, ln_w, ln_b, acc_rows, y_rows, scores)
        end_stage(nc, const)
        with ExitStack() as stage:
            expert_choice(nc, stage, const, scores, fc1s, b1s, fc2s, b2s, acc_rows, y_rows)
        end_stage(nc, const)
        h = ctx.enter_context(nc.sbuf_tensor("h", [R, NT, D], F32))
        with ExitStack() as stage:
            retention(nc, stage, const, acc_rows, rWq, rWk, rWv, rWg, rWo, gn_gamma, gn_beta, router_w, sWg, sWu, sWd,
                      h, x3_rows, logits)
        end_stage(nc, const)
        with ExitStack() as stage:
            token_choice(nc, stage, const, logits, expert_bias, eWg, eWu, eWd, h, pair_rows, x3_rows, out)


class Const:
    pass


def constants(nc, ctx):
    c = Const()
    c.semaphores = []
    sb = lambda n, s, d: ctx.enter_context(nc.sbuf_tensor(n, s, d))
    c.ident = sb("ident", [P, P], F32)
    c.zero = sb("zero", [P, P], F32)
    c.neg_half = sb("neg_half", [P, 2], F32)
    made = c.made = ctx.enter_context(nc.semaphore("const_made"))
    c.waits_passed = ctx.enter_context(nc.semaphore("waits_passed"))
    with nc.Block() as block:
        @block.gpsimd
        def _(pool):
            nc.gpsimd.memset(c.neg_half[:, :], -0.5).then_inc(made, 1)
            nc.gpsimd.memset(c.zero[:, :], 0.0).then_inc(made, 1)
            pool.wait_ge(made, 2)
            nc.gpsimd.affine_select(out=c.ident[:, :], in_=c.zero[:, :], compare_op=ALU.not_equal, fill=1.0,
                                    base=0, pattern=[[-1, P]], channel_multiplier=1).then_inc(made, 1)
            pool.wait_ge(made, 3)
    return c


def embed_and_attend(nc, ctx, const, x, tok_W, tok_b, cls_token, pos_embed, Wq, bq, Wk, bk, Wv, bv,
                     Wo, bo, gate_w, ln_w, ln_b, acc_rows, y_rows, scores):
    sb = lambda n, s, d=F32: ctx.enter_context(nc.sbuf_tensor(n, s, d))
    sem = lambda n: semaphore(nc, const, "a_" + n)

    w_rows = sb("w_rows", [P, D // P, KP * P])
    w_tok = sb("w_tok", [P, KP, D])
    w_q = sb("w_q", [P, 2, H0 * DK])
    w_k2 = sb("w_k2", [P, 2, 2, DK])
    w_v2 = sb("w_v2", [P, 2, 2, DK])
    w_o = sb("w_o", [P, NPAIR, D])
    gate_rows = sb("gate_rows", [NE, D])
    w_gate = sb("w_gate", [P, 2, P])
    bq_rows = sb("bq_rows", [NPAIR, P])
    b_q = sb("b_q", [P, NPAIR])
    b_k2 = sb("b_k2", [P, 1])
    b_v2 = sb("b_v2", [P, 1])
    b_o = sb("b_o", [R, D])
    pos = sb("pos", [R, D])
    base = sb("base", [R, D])
    table = sb("table", [R, D])
    lnw = sb("lnw", [R, D])
    lnb = sb("lnb", [R, D])
    vmask = sb("vmask", [2 * S, P])
    ones_s = sb("ones_s", [2 * S, P])

    x_in = [sb(f"x_in{i}", [IPG * NPH, C, PATCH * IMG]) for i in range(2)]
    x_pat = sb("x_pat", [IPG * NPH, C, NPH, PATCH * PATCH])
    patT = sb("patT", [P, KP, GT])
    h0 = sb("h0", [R, 2, D])
    h0b = [sb(f"h0b{i}", [R, 2, D]) for i in range(2)]
    stats0 = sb("stats0", [R, 2, 6])
    mv0 = sb("mv0", [R, 2, 2])
    ve0 = sb("ve0", [R, 2])
    rstd0 = sb("rstd0", [R, 2])
    xn = sb("xn", [R, 2, D])
    xnT = sb("xnT", [P, 2, GT])
    QT = [sb(f"QT{i}", [P, IPG, NPAIR, S]) for i in range(2)]
    Kbd = [sb(f"Kbd{i}", [P, IPG + 1, 2, S]) for i in range(2)]
    VT = sb("VT", [P, IPG, 2, S])
    Vbd = [sb(f"Vbd{i}", [2 * S, IPG, P]) for i in range(2)]
    NCH = 3
    SUB = 2 * NCH * 2
    W3 = 2 * NCH * 2 * S
    smax = sb("smax", [R, 3, SUB])
    ssum = sb("ssum", [R, 3, SUB])
    sinv = sb("sinv", [R, 3, SUB])
    prob = sb("prob", [R, 3, W3])
    PT = [sb(f"PT{i}", [2 * S, NPAIR * S]) for i in range(2)]
    OT = sb("OT", [P, NPAIR, GT])
    h1 = [sb(f"h1_{i}", [R, 2, D]) for i in range(2)]
    stats1 = sb("stats1", [R, 2, 6])
    mv1 = sb("mv1", [R, 2, 2])
    ve1 = sb("ve1", [R, 2])
    rstd1 = sb("rstd1", [R, 2])
    xn1 = sb("xn1", [R, 2, D])
    res = sb("res", [R, 2, D])
    xn1T = sb("xn1T", [P, 2, GT])
    lmax = sb("lmax", [R, 2])
    lexp = sb("lexp", [R, 2, NE])
    lsum = sb("lsum", [R, 2])
    linv = sb("linv", [R, 2])
    stats2 = sb("stats2", [R, 2, 6])
    mv2 = sb("mv2", [R, 2, 2])
    ve2 = sb("ve2", [R, 2])
    rstd2 = sb("rstd2", [R, 2])
    yn = sb("yn", [R, 2, D])
    ym = sb("ym", [R, 2, D])
    yo = sb("yo", [R, 2, YW])

    ring = [ctx.enter_context(nc.psum_tensor(f"a_ring{i}", [P, 512], F32)) for i in range(3)]
    pS = [ctx.enter_context(nc.psum_tensor(f"a_score{i}", [P, 512], F32)) for i in range(3)]
    pPT = ctx.enter_context(nc.psum_tensor("a_pt", [P, 512], F32))
    pO = ctx.enter_context(nc.psum_tensor("a_o", [P, 512], F32))

    loaded = sem("loaded")
    base_in, cls_in = sem("base_in"), sem("cls_in")
    cleared, masked = sem("cleared"), sem("masked")
    wT_done, wT_out = sem("wT_done"), sem("wT_out")
    table_made = sem("table_made")
    x_here = [sem(f"x_here{i}") for i in range(2)]
    x_sorted = [sem(f"x_sorted{c}") for c in range(C)]
    xt_done, xt_act, xt_dve = sem("xt_done"), sem("xt_act"), sem("xt_dve")
    emb_done, emb_out, h0b_made = sem("emb_done"), sem("emb_out"), sem("h0b_made")
    ln0_stat, ln0_var, ln0_eps, ln0_rstd, xn_made = (sem(n) for n in ("ln0_stat", "ln0_var", "ln0_eps", "ln0_rstd", "xn_made"))
    xnT_done, xnT_out = sem("xnT_done"), sem("xnT_out")
    q_done, q_act, q_dve = sem("q_done"), sem("q_act"), sem("q_dve")
    kv_done, k_out, v_out = sem("kv_done"), sem("k_out"), sem("v_out")
    vt_done, vt_out = sem("vt_done"), sem("vt_out")
    s_done, s_max, s_sub, s_exp, s_sum, s_inv, s_prob = (sem(n) for n in ("s_done", "s_max", "s_sub", "s_exp", "s_sum", "s_inv", "s_prob"))
    pt_done, pt_out, o_done, o_out = sem("pt_done"), sem("pt_out"), sem("o_done"), sem("o_out")
    wo_done, h1_made = sem("wo_done"), sem("h1_made")
    ln1_stat, ln1_var, ln1_eps, ln1_rstd, xn1_made = (sem(n) for n in ("ln1_stat", "ln1_var", "ln1_eps", "ln1_rstd", "xn1_made"))
    res_made, res_stored = sem("res_made"), sem("res_stored")
    xn1T_done, xn1T_out = sem("xn1T_done"), sem("xn1T_out")
    lg_done, lg_max, lg_sub, lg_exp, lg_sum, lg_inv, lg_out, lg_kept = (
        sem(n) for n in ("lg_done", "lg_max", "lg_sub", "lg_exp", "lg_sum", "lg_inv", "lg_out", "lg_kept"))
    ln2_stat, ln2_var, ln2_eps, ln2_rstd, yn_made, ym_made, y_made, y_stored = (
        sem(n) for n in ("ln2_stat", "ln2_var", "ln2_eps", "ln2_rstd", "yn_made", "ym_made", "y_made", "y_stored"))

    x_dram = x.rearrange("b c (t y) w -> b t c (y w)", t=NPH)
    def sort_pixels(eng, copy, c, f, half, par):
        eng.wait_ge(x_here[1 - par], 16 * IPG * (half + 1 + par))
        wait_alone(eng, const, xt_done, 3 * f)
        src = x_in[1 - par][:, c, :].rearrange("p (y w u) -> p w y u", y=PATCH, w=NPH)
        copy(x_pat[:, c, :, :].rearrange("p w (y u) -> p w y u", y=PATCH), src).then_inc(x_sorted[c], 1)

    acc_t = acc_rows.rearrange("(t p) d -> p t d", p=R)
    y_t = y_rows.rearrange("(t p) d -> p t d", p=R)
    N_LOADS = 20

    def steps(eng, step):
        step(eng, -1, -1, 1, attend=False, front=True, tail=False)
        step(eng, 0, 0, 0, attend=True, front=True, tail=False)
        step(eng, 1, 0, 1, attend=True, front=True, tail=True)
        with eng.Fori(1, NG // 2) as i:
            step(eng, 2 * i, i, 0, attend=True, front=True, tail=True)
            step(eng, 2 * i + 1, i, 1, attend=True, front=True, tail=True)
        step(eng, NG - 1, NG // 2, 0, attend=True, front=False, tail=True)
        step(eng, NG, NG // 2, 1, attend=False, front=False, tail=True)

    with nc.Block() as block:

        @block.sync
        def _(sp):
            loads = 0
            for dst, src in [
                (w_rows[:, :, :], tok_W.rearrange("(a p) k -> p a k", p=P)),
                (w_q[:, :, :], Wq.rearrange("(a p) n -> p a n", p=P)),
                (w_k2[:, :, 0, :], Wk.rearrange("(a p) n -> p a n", p=P)),
                (w_k2[:, :, 1, :], Wk.rearrange("(a p) n -> p a n", p=P)),
                (w_v2[:, :, 0, :], Wv.rearrange("(a p) n -> p a n", p=P)),
                (w_v2[:, :, 1, :], Wv.rearrange("(a p) n -> p a n", p=P)),
                (w_o[:, :, :], Wo.rearrange("(j p) n -> p j n", p=P)),
                (gate_rows[:, :], gate_w),
                (bq_rows[:, :], bq.rearrange("(j p) -> j p", p=P)),
                (b_k2[0:DK, :], bk.rearrange("(p a) -> p a", a=1)),
                (b_k2[DK:P, :], bk.rearrange("(p a) -> p a", a=1)),
                (b_v2[0:DK, :], bv.rearrange("(p a) -> p a", a=1)),
                (b_v2[DK:P, :], bv.rearrange("(p a) -> p a", a=1)),
                (b_o[:, :], bo.rearrange("(a d) -> a d", a=1).broadcast_to([R, D])),
                (lnw[:, :], ln_w.rearrange("(a d) -> a d", a=1).broadcast_to([R, D])),
                (lnb[:, :], ln_b.rearrange("(a d) -> a d", a=1).broadcast_to([R, D])),
                (pos[0:S, :], pos_embed[0]),
                (pos[S:2 * S, :], pos_embed[0]),
                (pos[2 * S:3 * S, :], pos_embed[0]),
            ]:
                sp.dma_start(dst, src).then_inc(loaded, 16)
                loads += 1
            assert loads == N_LOADS - 1
            sp.dma_start(base[:, :], tok_b.rearrange("(a d) -> a d", a=1).broadcast_to([R, D])).then_inc(base_in, 16)
            sp.wait_ge(base_in, 16)
            for i in range(IPT):
                sp.dma_start(base[i * S:i * S + 1, :], cls_token[0]).then_inc(cls_in, 16)

            def images(g, parity):
                for b in range(IPG):
                    n = min(IPG * g + b, NB - 1) if isinstance(g, int) else IPG * g + b
                    sp.dma_start(x_in[parity][b * NPH:(b + 1) * NPH, :, :], x_dram[n]).then_inc(x_here[parity], 16)

            images(0, 0)
            images(1, 1)

            def store(g):
                sp.wait_ge(res_made, g + 1)
                sp.dma_start(acc_t[:, bass.ds(2 * g, 2), :], res[:, :, :]).then_inc(res_stored, 16)
                sp.wait_ge(y_made, g + 1)
                sp.wait_ge(lg_out, g + 1)
                sp.dma_start(y_t[:, bass.ds(2 * g, 2), :], yo[:, :, :]).then_inc(y_stored, 16)

            def x_free(g):
                for c in range(C):
                    sp.wait_ge(x_sorted[c], g + 1)

            for g in range(2):
                x_free(g)
                images(g + 2, g)
            with sp.Fori(1, NG // 2 - 1) as i:
                for u in range(2):
                    x_free(2 * i + u)
                    images(2 * i + u + 2, u)
                    store(2 * i + u - 2)
            x_free(NG - 3)
            images(NG - 1, 0)
            for g in range(NG - 5, NG):
                store(g)
            sp.wait_ge(res_stored, 16 * NG)
            sp.wait_ge(y_stored, 16 * NG)

        @block.tensor
        def _(pe):
            pe.wait_ge(loaded, 16 * (N_LOADS - 1))
            n = 0
            for k in range(0, KP, 2):
                for kk in (k, k + 1):
                    for a in range(2):
                        n += 1
                        mm = nc.tensor.transpose(ring[k // 2][:, (kk - k) * D + a * P:(kk - k) * D + (a + 1) * P],
                                                 w_rows[:, a, kk * P:(kk + 1) * P], const.ident[:, :])
                mm.then_inc(wT_done, 1)
            for a in range(2):
                mm = nc.tensor.transpose(pS[0][:, a * NE:(a + 1) * NE], gate_rows[:, a * P:(a + 1) * P],
                                         const.ident[0:NE, 0:NE])
            mm = nc.tensor.transpose(pS[0][:, 2 * NE:2 * NE + NPAIR], bq_rows[:, :], const.ident[0:NPAIR, 0:NPAIR])
            mm.then_inc(wT_done, 1)
            pe.wait_ge(wT_out, 5)
            pe.wait_ge(cleared, 1)

            def step(pe, g, half, par, attend, front, tail):
                f = g + 1
                fp = 1 - par
                t = g - 1
                def patch_transposes(j):
                    wait_alone(pe, const, x_sorted[j], f + 1)
                    for k in (2 * j, 2 * j + 1):
                        for w in range(NPH):
                            o = (k % 2) * NPH * IPG * NPH + w * IPG * NPH
                            mm = nc.tensor.transpose(ring[j][:, o:o + IPG * NPH],
                                                     x_pat[:, k // 2, w, (k % 2) * P:(k % 2 + 1) * P],
                                                     const.ident[0:IPG * NPH, 0:IPG * NPH])
                    mm.then_inc(xt_done, 1)

                def scores_of(j):
                    pe.wait_ge(s_sub, 3 * g + j - 2) if not isinstance(g, int) or g > 0 else None
                    for b in (2 * j, 2 * j + 1):
                        for c in range(NCH):
                            pair = min(NCH * c, NPAIR - NCH)
                            o = ((b % 2) * NCH + c) * 2 * S
                            mm = nc.tensor.matmul(
                                pS[j][0:R, o:o + R],
                                QT[par][:, b, pair:pair + NCH, :].rearrange("p j s -> p (j s)"),
                                Kbd[par][:, b:b + 2, :, :].rearrange("p b e s -> p (b e s)")[:, 0:R],
                                start=True, stop=True)
                    mm.then_inc(s_done, 1)

                def prob_transposes(b):
                    if b % 2 == 0:
                        pe.wait_ge(s_prob, 3 * g + b // 2 + 1)
                    pe.wait_ge(pt_out, 6 * g + b)
                    for c in range(NCH):
                        pair = min(NCH * c, NPAIR - NCH)
                        o = ((b % 2) * NCH + c) * 2 * S
                        mm = nc.tensor.transpose(pPT[0:2 * S, pair * S:pair * S + R], prob[:, b // 2, o:o + 2 * S],
                                                 const.ident[0:R, 0:R])
                    mm.then_inc(pt_done, 1)

                def values_of(b):
                    pe.wait_ge(pt_out, 6 * g + b + 1)
                    pe.wait_ge(o_out, 6 * g + b)
                    nc.tensor.matmul(pO[:, 0:NPAIR * S], Vbd[par][:, b, :], PT[b % 2][:, :],
                                     start=True, stop=True).then_inc(o_done, 1)

                def q_pairs(j, bank):
                    for m in (2 * j, 2 * j + 1):
                        for k in range(2):
                            mm = nc.tensor.matmul(ring[bank][:, (m % 2) * GT:(m % 2 + 1) * GT],
                                                  w_q[:, k, m * P:(m + 1) * P], xnT[:, k, :],
                                                  start=(k == 0), stop=(k == 1))
                    mm.then_inc(q_done, 1)

                if attend:
                    pe.wait_ge(q_act, 2 * (g + 1))
                    pe.wait_ge(q_dve, 2 * (g + 1))
                    pe.wait_ge(k_out, 2 * (g + 1))
                    for j in range(3):
                        scores_of(j)
                if front:
                    pe.wait_ge(vt_out, 2 * f)
                    patch_transposes(0)
                    patch_transposes(1)
                    if attend:
                        pe.wait_ge(h1_made, g)
                    patch_transposes(2)
                    pe.wait_ge(xt_act, 2 * (f + 1))
                    pe.wait_ge(xt_dve, f + 1)
                    for tile in range(2):
                        for k in range(KP):
                            mm = nc.tensor.matmul(ring[0][0:R, tile * D:(tile + 1) * D],
                                                  patT[:, k, tile * R:(tile + 1) * R], w_tok[:, k, :],
                                                  start=(k == 0), stop=(k == KP - 1))
                    mm.then_inc(emb_done, 1)
                if tail:
                    if not front:
                        pe.wait_ge(vt_out, 2 * NG)
                        pe.wait_ge(h1_made, min(g, NG))
                    pe.wait_ge(xn1_made, 2 * (t + 1))
                    for tile in range(2):
                        for k in range(2):
                            mm = nc.tensor.transpose(ring[1][:, k * GT + tile * R:k * GT + (tile + 1) * R],
                                                     xn1[:, tile, k * P:(k + 1) * P], const.ident[0:R, 0:R])
                    mm.then_inc(xn1T_done, 1)
                if attend:
                    prob_transposes(0)
                    prob_transposes(1)
                    values_of(0)
                if tail:
                    pe.wait_ge(xn1T_out, t + 1)
                    for tile in range(2):
                        for k in range(2):
                            mm = nc.tensor.matmul(ring[2][0:R, tile * P:(tile + 1) * P],
                                                  xn1T[:, k, tile * R:(tile + 1) * R], w_gate[:, k, :],
                                                  start=(k == 0), stop=(k == 1))
                    mm.then_inc(lg_done, 1)
                if attend:
                    values_of(1)
                if front:
                    pe.wait_ge(emb_out, f + 1)
                    pe.wait_ge(xn_made, 2 * (f + 1))
                    for tile in range(2):
                        for k in range(2):
                            mm = nc.tensor.transpose(ring[0][:, k * GT + tile * R:k * GT + (tile + 1) * R],
                                                     xn[:, tile, k * P:(k + 1) * P], const.ident[0:R, 0:R])
                    mm.then_inc(xnT_done, 1)
                if attend:
                    prob_transposes(2)
                if front:
                    pe.wait_ge(xnT_out, f + 1)
                    if tail:
                        pe.wait_ge(xn1T_out, t + 1)
                    q_pairs(0, 1)
                if attend:
                    values_of(2)
                    prob_transposes(3)
                if front:
                    if tail:
                        pe.wait_ge(lg_sub, t + 1)
                    q_pairs(1, 2)
                    q_pairs(2, 0)
                if attend:
                    values_of(3)
                    prob_transposes(4)
                if front:
                    pe.wait_ge(q_act, 2 * f + 1)
                    q_pairs(3, 1)
                if attend:
                    values_of(4)
                    prob_transposes(5)
                if front:
                    pe.wait_ge(q_dve, 2 * f + 1)
                    for n, w in ((0, w_k2), (1, w_v2)):
                        for k in range(2):
                            mm = nc.tensor.matmul(ring[2][:, n * GT:(n + 1) * GT],
                                                  w[:, k, :, :], xnT[:, k, :], start=(k == 0), stop=(k == 1))
                    mm.then_inc(kv_done, 1)
                if attend:
                    values_of(5)
                if front:
                    pe.wait_ge(v_out, f + 1)
                    pe.wait_ge(q_act, 2 * f + 2)
                    for b in range(4):
                        mm = nc.tensor.transpose(ring[0][0:2 * S, b * P:(b + 1) * P], VT[:, b, :, :].rearrange("p e s -> p (e s)"),
                                                 const.ident[:, :])
                    mm.then_inc(vt_done, 1)
                    pe.wait_ge(q_dve, 2 * f + 2)
                    for b in range(4, IPG):
                        mm = nc.tensor.transpose(ring[1][0:2 * S, (b - 4) * P:(b - 3) * P], VT[:, b, :, :].rearrange("p e s -> p (e s)"),
                                                 const.ident[:, :])
                    mm.then_inc(vt_done, 1)
                if attend:
                    if front:
                        pe.wait_ge(k_out, 2 * (f + 1))
                    elif tail:
                        pe.wait_ge(lg_sub, t + 1)
                    pe.wait_ge(o_out, 6 * (g + 1))
                    for tile in range(2):
                        for j in range(NPAIR):
                            mm = nc.tensor.matmul(ring[2][0:R, tile * D:(tile + 1) * D],
                                                  OT[:, j, tile * R:(tile + 1) * R], w_o[:, j, :],
                                                  start=(j == 0), stop=(j == NPAIR - 1))
                    mm.then_inc(wo_done, 1)

            steps(pe, step)

        @block.scalar
        def _(act):
            for j in range(3):
                act.wait_ge(wT_done, j + 1)
                nc.scalar.activation(w_tok[:, 2 * j:2 * j + 2, :].rearrange("p k e -> p (k e)"), ring[j][:, :],
                                     ACT.Copy).then_inc(wT_out, 1)
            act.wait_ge(wT_done, 4)
            act.wait_ge(cleared, 1)
            nc.scalar.activation(w_gate[:, :, 0:NE], pS[0][:, 0:2 * NE].rearrange("p (k e) -> p k e", k=2),
                                 ACT.Copy).then_inc(wT_out, 1)
            nc.scalar.activation(b_q[:, :], pS[0][:, 2 * NE:2 * NE + NPAIR], ACT.Copy).then_inc(wT_out, 1)
            act.wait_ge(wT_out, 5)
            act.wait_ge(loaded, 16 * (N_LOADS - 1))

            def step(act, g, half, par, attend, front, tail):
                f, fp, t = g + 1, 1 - par, g - 1

                def exp_of(j):
                    act.wait_ge(s_sub, 3 * g + j + 1)
                    nc.scalar.activation(prob[:, j, :], prob[:, j, :], ACT.Exp, scale=SCALE0).then_inc(s_exp, 1)

                def patch_out(j):
                    act.wait_ge(xt_done, 3 * f + j + 1)
                    act.wait_ge(emb_done, f)
                    nc.scalar.activation(patch_slots(patT, 2 * j), patch_columns(ring[j], 0), ACT.Copy)
                    nc.scalar.activation(patch_slots(patT, 2 * j + 1), patch_columns(ring[j], 1), ACT.Copy).then_inc(xt_act, 1)

                def q_out(j):
                    act.wait_ge(q_done, 4 * f + j + 1)
                    for m in range(2):
                        last = nc.scalar.activation(QT[fp][:, :, 2 * j + m, :], q_columns(ring[Q_BANK[j]], m), ACT.Identity,
                                                    bias=b_q[:, 2 * j + m:2 * j + m + 1])
                    last.then_inc(q_act, 1)

                def pt_copy(b):
                    act.wait_ge(pt_done, 6 * g + b + 1)
                    if b >= 2:
                        act.wait_ge(o_done, 6 * g + b - 1)
                    else:
                        act.wait_ge(o_done, 6 * g)
                    nc.scalar.activation(PT[b % 2][:, :], pPT[0:2 * S, 0:NPAIR * S], ACT.Copy).then_inc(pt_out, 1)

                if front:
                    sort_pixels(act, lambda o, i: nc.scalar.activation(o, i, ACT.Copy), 0, f, half, par)
                if attend:
                    exp_of(0)
                if front:
                    patch_out(0)
                if attend:
                    exp_of(1)
                if front:
                    patch_out(2)
                if attend:
                    exp_of(2)
                if tail:
                    act.wait_ge(xn1T_done, t + 1)
                    nc.scalar.activation(xn1T[:, :, :].rearrange("p k t -> p (k t)"), ring[1][:, 0:2 * GT],
                                         ACT.Copy).then_inc(xn1T_out, 1)
                if attend:
                    pt_copy(0)
                    pt_copy(1)
                if tail:
                    act.wait_ge(lg_sub, t + 1)
                    nc.scalar.activation(lexp[:, :, :], lexp[:, :, :], ACT.Exp).then_inc(lg_exp, 1)
                if front:
                    act.wait_ge(xnT_done, f + 1)
                    act.wait_ge(kv_done, f)
                    nc.scalar.activation(xnT[:, :, :].rearrange("p k t -> p (k t)"), ring[0][:, 0:2 * GT],
                                         ACT.Copy).then_inc(xnT_out, 1)
                if attend:
                    pt_copy(2)
                if front:
                    q_out(0)
                if attend:
                    pt_copy(3)
                if front:
                    q_out(2)
                if attend:
                    pt_copy(4)
                    pt_copy(5)
                if front:
                    act.wait_ge(kv_done, f + 1)
                    nc.scalar.activation(VT[:, :, :, :], ring[2][:, GT:2 * GT].rearrange("p (b s) -> p b s", s=S).unsqueeze(2).broadcast_to([P, IPG, 2, S]), ACT.Identity, bias=b_v2[:, 0:1]).then_inc(v_out, 1)

            steps(act, step)

        @block.gpsimd
        def _(pool):
            nc.gpsimd.memset(w_gate[:, :, :], 0.0)
            for i in range(2):
                nc.gpsimd.memset(Kbd[i][:, :, :, :], 0.0)
            for b in range(IPG):
                last = nc.gpsimd.memset(patT[:, :, b * S:b * S + 1], 0.0)
            last = nc.gpsimd.memset(ones_s[:, :], 1.0)
            last.then_inc(cleared, 1)
            pool.wait_ge(cleared, 1)
            nc.gpsimd.affine_select(out=vmask[:, 0:DK], in_=ones_s[:, 0:DK], compare_op=ALU.is_gt, fill=0.0,
                                    base=S, pattern=[[0, DK]], channel_multiplier=-1)
            nc.gpsimd.affine_select(out=vmask[:, DK:P], in_=ones_s[:, DK:P], compare_op=ALU.is_ge, fill=0.0,
                                    base=-S, pattern=[[0, DK]], channel_multiplier=1).then_inc(masked, 1)
            pool.wait_ge(loaded, 16 * (N_LOADS - 1))
            pool.wait_ge(cls_in, 16 * IPT)
            nc.gpsimd.tensor_tensor(table[:, :], base[:, :], pos[:, :], ALU.add).then_inc(table_made, 1)

            def rstd_of(mv, ve, rstd, stat, eps, done, n):
                wait_alone(pool, const, stat, 2 * (n + 1))
                nc.gpsimd.tensor_scalar(ve[:, :], mv[:, :, 1], LN_EPS, None, ALU.add).then_inc(eps, 1)
                pool.wait_ge(eps, n + 1)
                nc.gpsimd.tensor_tensor(rstd[:, :], ve[:, :], const.neg_half[0:R, :], ALU.pow).then_inc(done, 1)

            def step(pool, g, half, par, attend, front, tail):
                f, fp, t = g + 1, 1 - par, g - 1
                if tail:
                    rstd_of(mv1, ve1, rstd1, ln1_var, ln1_eps, ln1_rstd, t)

                def scale(j):
                    pool.wait_ge(s_inv, 3 * g + j + 1)
                    pool.wait_ge(s_exp, 3 * g + j + 1)
                    v = prob[:, j, :].rearrange("p (n s) -> p n s", s=S)
                    nc.gpsimd.tensor_tensor(v, v, spread(sinv[:, j, :], S), ALU.mult).then_inc(s_prob, 1)

                if attend:
                    scale(0)
                    scale(1)
                    scale(2)
                if front:
                    rstd_of(mv0, ve0, rstd0, ln0_var, ln0_eps, ln0_rstd, f)
                if tail:
                    rstd_of(mv2, ve2, rstd2, ln2_var, ln2_eps, ln2_rstd, t)
                    pool.wait_ge(xn1_made, 2 * (t + 1))
                    pool.wait_ge(res_stored, 16 * t)
                    nc.gpsimd.tensor_tensor(res[:, :, :], h1[fp][:, :, :], xn1[:, :, :], ALU.add).then_inc(res_made, 1)
                if front:
                    pool.wait_ge(emb_out, f + 1)
                    nc.gpsimd.tensor_tensor(h0b[fp][:, :, :], h0[:, :, :], both(b_o[:, :]), ALU.add).then_inc(h0b_made, 1)
                if tail:
                    pool.wait_ge(yn_made, 2 * (t + 1))
                    nc.gpsimd.tensor_tensor(ym[:, :, :], yn[:, :, :], both(lnw[:, :]), ALU.mult).then_inc(ym_made, 1)
                    pool.wait_ge(ym_made, t + 1)
                    pool.wait_ge(y_stored, 16 * t)
                    nc.gpsimd.tensor_tensor(yo[:, :, 0:D], ym[:, :, :], both(lnb[:, :]), ALU.add).then_inc(y_made, 1)

            steps(pool, step)

        @block.vector
        def _(dve):
            def norm_stats(src, stats, mv, stat, var, n):
                for tile in range(2):
                    nc.vector.bn_stats(stats[:, tile, :], src[:, tile, :]).then_inc(stat, 1)
                for tile in range(2):
                    wait_alone(dve, const, stat, 2 * n + tile + 1)
                    nc.vector.bn_aggr(mv[:, tile, :], stats[:, tile, :]).then_inc(var, 1)

            def normalise(dst, src, mv, rstd, rstd_made, made, n):
                dve.wait_ge(rstd_made, n + 1)
                for tile in range(2):
                    nc.vector.tensor_scalar(dst[:, tile, :], src[:, tile, :], mv[:, tile, 0:1], rstd[:, tile:tile + 1],
                                            ALU.subtract, ALU.mult).then_inc(made, 1)

            dve.wait_ge(masked, 1)
            dve.wait_ge(table_made, 1)
            dve.wait_ge(wT_out, 5)
            dve.wait_ge(loaded, 16 * (N_LOADS - 1))

            def step(dve, g, half, par, attend, front, tail):
                f, fp, t = g + 1, 1 - par, g - 1

                def patch_out(j):
                    dve.wait_ge(xt_done, 3 * f + j + 1)
                    dve.wait_ge(emb_done, f)
                    nc.vector.tensor_copy(patch_slots(patT, 2 * j), patch_columns(ring[j], 0))
                    nc.vector.tensor_copy(patch_slots(patT, 2 * j + 1), patch_columns(ring[j], 1)).then_inc(xt_dve, 1)

                def shift(j):
                    dve.wait_ge(s_done, 3 * g + j + 1)
                    if j == 0:
                        dve.wait_ge(pt_done, 6 * g)
                    v = pS[j][0:R, 0:W3].rearrange("p (n s) -> p n s", s=S)
                    nc.vector.tensor_reduce(smax[:, j, :], v, AX_X, ALU.max).then_inc(s_max, 1)
                    dve.wait_ge(s_max, 3 * g + j + 1)
                    nc.vector.tensor_tensor(prob[:, j, :].rearrange("p (n s) -> p n s", s=S), v,
                                            spread(smax[:, j, :], S), ALU.subtract).then_inc(s_sub, 1)

                def inverse(j):
                    dve.wait_ge(s_exp, 3 * g + j + 1)
                    if j == 0:
                        dve.wait_ge(s_prob, 3 * g)
                    v = prob[:, j, :].rearrange("p (n s) -> p n s", s=S)
                    nc.vector.tensor_reduce(ssum[:, j, :], v, AX_X, ALU.add).then_inc(s_sum, 1)
                    dve.wait_ge(s_sum, 3 * g + j + 1)
                    nc.vector.reciprocal(sinv[:, j, :], ssum[:, j, :]).then_inc(s_inv, 1)

                def o_copy(b):
                    dve.wait_ge(o_done, 6 * g + b + 1)
                    if b == 0:
                        dve.wait_ge(wo_done, g)
                    nc.vector.tensor_copy(OT[:, :, b * S:(b + 1) * S],
                                          pO[:, 0:NPAIR * S].rearrange("p (j s) -> p j s", s=S)).then_inc(o_out, 1)

                def q_out(j):
                    dve.wait_ge(q_done, 4 * f + j + 1)
                    for m in range(2):
                        last = nc.vector.tensor_scalar(QT[fp][:, :, 2 * j + m, :], q_columns(ring[Q_BANK[j]], m),
                                                       b_q[:, 2 * j + m:2 * j + m + 1], None, ALU.add)
                    last.then_inc(q_dve, 1)

                if front:
                    sort_pixels(dve, nc.vector.tensor_copy, 1, f, half, par)
                    sort_pixels(dve, nc.vector.tensor_copy, 2, f, half, par)
                if tail:
                    dve.wait_ge(h1_made, t + 1)
                    norm_stats(h1[fp], stats1, mv1, ln1_stat, ln1_var, t)
                if attend:
                    shift(0)
                if tail:
                    dve.wait_ge(xn1T_done, t)
                    dve.wait_ge(res_made, t)
                    normalise(xn1, h1[fp], mv1, rstd1, ln1_rstd, xn1_made, t)
                if attend:
                    shift(1)
                    inverse(0)
                if front:
                    patch_out(1)
                if attend:
                    shift(2)
                    inverse(1)
                if attend:
                    inverse(2)
                if front:
                    dve.wait_ge(emb_done, f + 1)
                    dve.wait_ge(h0b_made, f)
                    nc.vector.tensor_tensor(h0[:, :, :], ring[0][0:R, :].rearrange("p (t d) -> p t d", t=2),
                                            both(table[:, :]), ALU.add).then_inc(emb_out, 1)
                    dve.wait_ge(emb_out, f + 1)
                    norm_stats(h0, stats0, mv0, ln0_stat, ln0_var, f)
                if tail:
                    dve.wait_ge(xn1_made, 2 * (t + 1))
                    norm_stats(xn1, stats2, mv2, ln2_stat, ln2_var, t)
                if attend:
                    o_copy(0)
                if tail:
                    dve.wait_ge(lg_done, t + 1)
                    dve.wait_ge(lg_exp, t)
                    lv = ring[2][0:R, 0:2 * P].rearrange("p (t e) -> p t e", t=2)[:, :, 0:NE]
                    nc.vector.tensor_reduce(lmax[:, :], lv, AX_X, ALU.max).then_inc(lg_max, 1)
                    dve.wait_ge(lg_max, t + 1)
                    nc.vector.tensor_tensor(lexp[:, :, :], lv, spread(lmax[:, :], NE), ALU.subtract).then_inc(lg_sub, 1)
                if front:
                    dve.wait_ge(xnT_done, f)
                    normalise(xn, h0, mv0, rstd0, ln0_rstd, xn_made, f)
                if attend:
                    o_copy(1)
                if tail:
                    dve.wait_ge(ym_made, t)
                    normalise(yn, xn1, mv2, rstd2, ln2_rstd, yn_made, t)
                    dve.wait_ge(lg_exp, t + 1)
                    nc.vector.tensor_reduce(lsum[:, :], lexp[:, :, :], AX_X, ALU.add).then_inc(lg_sum, 1)
                    dve.wait_ge(lg_sum, t + 1)
                    nc.vector.reciprocal(linv[:, :], lsum[:, :]).then_inc(lg_inv, 1)
                    dve.wait_ge(lg_inv, t + 1)
                    dve.wait_ge(y_stored, 16 * t)
                    nc.vector.tensor_tensor(yo[:, :, D:YW], lexp[:, :, :], spread(linv[:, :], NE), ALU.mult).then_inc(lg_out, 1)
                    nc.vector.tensor_tensor(scores[0:R, bass.ds(2 * t, 2), :], lexp[:, :, :], spread(linv[:, :], NE),
                                            ALU.mult).then_inc(lg_kept, 1)
                    dve.wait_ge(lg_kept, t + 1)
                if attend:
                    o_copy(2)
                if front:
                    q_out(1)
                if attend:
                    o_copy(3)
                if front:
                    q_out(3)
                if attend:
                    o_copy(4)
                if front:
                    dve.wait_ge(v_out, f + 1)
                    for e in range(2):
                        rows = slice(e * DK, (e + 1) * DK)
                        nc.vector.tensor_scalar(Kbd[fp][rows, 0:IPG, e, :],
                                                ring[2][rows, 0:GT].rearrange("p (b s) -> p b s", s=S),
                                                b_k2[rows, 0:1], None, ALU.add).then_inc(k_out, 1)
                if attend:
                    o_copy(5)
                if front:
                    for n, (b0, b1) in enumerate(((0, 4), (4, IPG))):
                        dve.wait_ge(vt_done, 2 * f + n + 1)
                        nc.vector.tensor_tensor(Vbd[fp][:, b0:b1, :],
                                                ring[n][0:2 * S, 0:(b1 - b0) * P].rearrange("p (b d) -> p b d", d=P),
                                                every(vmask[:, :], b1 - b0), ALU.mult).then_inc(vt_out, 1)
                if attend:
                    dve.wait_ge(wo_done, g + 1)
                    dve.wait_ge(h0b_made, g + 1)
                    nc.vector.tensor_tensor(h1[par][:, :, :], ring[2][0:R, :].rearrange("p (t d) -> p t d", t=2),
                                            h0b[par][:, :, :], ALU.add).then_inc(h1_made, 1)

            steps(dve, step)


def expert_choice(nc, ctx, const, scores, fc1s, b1s, fc2s, b2s, acc_rows, y_rows):
    sb = lambda n, s, d=F32: ctx.enter_context(nc.sbuf_tensor(n, s, d))
    sem = lambda n: semaphore(nc, const, "c_" + n)
    ps = lambda n, d=F32: ctx.enter_context(nc.psum_tensor(n, [P, 512], d))
    NF = 8
    F = NF * P
    NST = -(-CAP // P)
    LAST = CAP - (NST - 1) * P
    rows_in = [P] * (NST - 1) + [LAST]
    FAR = 4095.0
    BITS = 30

    valid = sb("valid", [R, NT])
    valid1 = sb("valid1", [R, NT])
    sc = sb("sc", [R, NE, NT])
    cur = sb("cur", [R, NE])
    bit = sb("bit", [R, NE], I32)
    cand = sb("cand", [R, NE])
    over = sb("over", [R, NE, NT], BF16)
    cnt = sb("cnt", [R, NE], BF16)
    kept = sb("kept", [R, NE])
    ones_b = sb("ones_b", [R, P], BF16)
    tri = sb("tri", [R, R], BF16)
    sel = sb("sel", [R, 2, NE, NT], BF16)
    reset = sb("reset", [R, 2 * NE * NT])
    incl = sb("incl", [R, 2, NE, NT])
    excl = sb("excl", [R, 2, NE, NT])
    posn = sb("posn", [R, 2, NE, NT])
    slot_g = sb("slot_g", [R, NE, NT])
    slot_q = sb("slot_q", [R, NE, NT])
    slot_e = sb("slot_e", [R, NE, NT])
    slot = sb("slot", [R, NE, NT], I32)
    hi_i = sb("hi_i", [R, NE, NT], I32)
    lo_i = sb("lo_i", [R, NE, NT], I32)
    hi = sb("hi", [R, NE * NT])
    lo = sb("lo", [R, NE, NT])
    iota_s = sb("iota_s", [R, P], BF16)
    iota_j = sb("iota_j", [R, NST], F32)
    tile_no = sb("tile_no", [R, NE, NT], F32)
    row_no = sb("row_no", [R, 1], F32)
    in_tile = sb("in_tile", [R, NE * NT, NST], F32)
    marks = sb("marks", [R, NE, NT, 2, NST], BF16)
    hot = [sb(f"hot{i}", [R, NT, P], BF16) for i in range(2)]
    idx_f = sb("idx_f", [P, NE, NST])
    idx = sb("idx", [P, NE, NST], I32)
    tokens = [sb(f"tokens{i}", [P, NST], I32) for i in range(2)]

    fc1_rows = [sb(f"fc1_rows{i}", [P, NF, D]) for i in range(2)]
    fc2_rows = [sb(f"fc2_rows{i}", [P, 2, F]) for i in range(2)]
    fc1T = [sb(f"fc1T{i}", [P, 2, F]) for i in range(2)]
    fc2T = [sb(f"fc2T{i}", [P, NF, D]) for i in range(2)]
    b1_rows = sb("b1_rows", [NE, F])
    b1T = sb("b1T", [P, NF, NE])
    b2 = [sb(f"b2_{i}", [P, D]) for i in range(2)]
    yg = [sb(f"yg{i}", [P, NST, YW]) for i in range(2)]
    yT = [sb(f"yT{i}", [P, 2, CAP]) for i in range(2)]
    hT = sb("hT", [P, NF, CAP])
    ob = sb("ob", [P, NST, D])
    ow = sb("ow", [P, NST, D])

    pW = [ps(f"c_w{i}") for i in range(2)]
    pY = [ps(f"c_y{i}") for i in range(2)]
    pH = [ps(f"c_h{i}") for i in range(2)]
    pO = [ps(f"c_o{i}") for i in range(2)]

    made, init = sem("made"), sem("init")
    counted, reduced, summed, kept_made, cur_made, bit_made, cand_made = (
        sem(n) for n in ("counted", "reduced", "summed", "kept_made", "cur_made", "bit_made", "cand_made"))
    routed = sem("routed")
    prefix_done, hot_made, ids_done, idx_made = sem("prefix_done"), sem("hot_made"), sem("ids_done"), sem("idx_made")
    w_here = [sem(f"w_here{i}") for i in range(2)]
    b2_here = [sem(f"b2_here{i}") for i in range(2)]
    b1_here, b1_done, b1_out = sem("b1_here"), sem("b1_done"), sem("b1_out")
    wt_done, wt_act, wt_dve = sem("wt_done"), sem("wt_act"), sem("wt_dve")
    y_here = [sem(f"y_here{i}") for i in range(2)]
    yt_done, yt_out = sem("yt_done"), sem("yt_out")
    h_done, h_out = sem("h_done"), sem("h_out")
    o_done, ob_made, ow_made = sem("o_done"), sem("ob_made"), sem("ow_made")
    scattered, tokens_made = sem("scattered"), sem("tokens_made")

    def steps(eng, step):
        with eng.Fori(0, NE // 2 - 1) as i:
            step(eng, 2 * i, i, 0, prepare=True)
            step(eng, 2 * i + 1, i, 1, prepare=True)
        step(eng, NE - 2, NE // 2 - 1, 0, prepare=True)
        step(eng, NE - 1, NE // 2 - 1, 1, prepare=False)

    with nc.Block() as block:

        @block.sync
        def _(sp):
            fc1_d = fc1s.rearrange("e (j p) d -> e p j d", p=P)
            fc2_d = fc2s.rearrange("e (a p) f -> e p a f", p=P)

            def weights(e, par):
                sp.dma_start(fc1_rows[par][:, :, :], fc1_d[e]).then_inc(w_here[par], 16)
                sp.dma_start(fc2_rows[par][:, :, :], fc2_d[e]).then_inc(w_here[par], 16)

            def bias2(e, par):
                sp.dma_start(b2[par][:, :], b2s[bass.ds(e, 1), :].broadcast_to([P, D])).then_inc(b2_here[par], 16)

            sp.dma_start(b1_rows[:, :], b1s).then_inc(b1_here, 16)
            for e in range(2):
                weights(e, e)
                bias2(e, e)
            with sp.Fori(0, NE // 2 - 1) as i:
                for u in range(2):
                    sp.wait_ge(wt_done, NF * (2 * i + u + 1))
                    weights(2 * i + u + 2, u)
                    sp.wait_ge(ob_made, 2 * (2 * i + u + 1))
                    bias2(2 * i + u + 2, u)

        @block.gpsimd
        def _(pool):
            nc.gpsimd.memset(ones_b[:, :], 1.0)
            nc.gpsimd.memset(valid[:, :], 1.0).then_inc(made, 1)
            pool.wait_ge(made, 1)
            nc.gpsimd.affine_select(out=tri[:, :], in_=ones_b[:, 0:R], compare_op=ALU.is_gt, fill=0.0,
                                    base=0, pattern=[[1, R]], channel_multiplier=-1)
            nc.gpsimd.affine_select(out=valid[:, NT - 1:NT], in_=ones_b[:, 0:1], compare_op=ALU.is_gt, fill=0.0,
                                    base=TOK - (NT - 1) * R, pattern=[[0, 1]], channel_multiplier=-1)
            nc.gpsimd.iota(iota_s[:, :], pattern=[[1, P]], base=0, channel_multiplier=0,
                           allow_small_or_imprecise_dtypes=True)
            nc.gpsimd.iota(iota_j[:, :], pattern=[[1, NST]], base=0, channel_multiplier=0,
                           allow_small_or_imprecise_dtypes=True)
            nc.gpsimd.iota(tile_no[:, :, :], pattern=[[0, NE], [1, NT]], base=0, channel_multiplier=0,
                           allow_small_or_imprecise_dtypes=True)
            nc.gpsimd.iota(row_no[:, :], pattern=[[0, 1]], base=0, channel_multiplier=1,
                           allow_small_or_imprecise_dtypes=True).then_inc(made, 1)

            def gather(e, par):
                nc.gpsimd.tensor_copy(tokens[par][:, :], idx[:, e, :]).then_inc(tokens_made, 1)
                wait_alone(pool, const, tokens_made, e + 1)
                for j in range(NST):
                    n = rows_in[j]
                    nc.gpsimd.indirect_dma_start(
                        out=yg[par][0:n, j, :], out_offset=None, in_=y_rows[:, :],
                        in_offset=bass.IndirectOffsetOnAxis(ap=tokens[par][0:n, j:j + 1], axis=0)).then_inc(y_here[par], 16)

            pool.wait_ge(idx_made, 1)
            gather(0, 0)

            def step(pool, e, half, par, prepare):
                if prepare:
                    pool.wait_ge(yt_done, 2 * e)
                    pool.wait_ge(scattered, 16 * NST * e)
                    gather(e + 1, 1 - par)
                for j in range(NST):
                    wait_alone(pool, const, ow_made, NST * e + j + 1)
                    if j == 0:
                        wait_alone(pool, const, scattered, 16 * NST * e)
                    n = rows_in[j]
                    nc.gpsimd.indirect_dma_start(
                        out=acc_rows[:, :], out_offset=bass.IndirectOffsetOnAxis(ap=tokens[par][0:n, j:j + 1], axis=0),
                        in_=ow[0:n, j, :], in_offset=None, compute_op=ALU.add).then_inc(scattered, 16)

            steps(pool, step)
            pool.wait_ge(scattered, 16 * NST * NE)

        @block.tensor
        def _(pe):
            def weight_transposes(e, half, par, n):
                if n == 0:
                    pe.wait_ge(w_here[par], 32 * (half + 1))
                k = NF * e + n
                if n % 2 == 0:
                    pe.wait_ge(wt_act, NF // 2 * e + n // 2)
                else:
                    pe.wait_ge(wt_dve, NF // 2 * e + n // 2)
                bank = pW[n % 2]
                for q in range(4):
                    if n < 4:
                        src = fc1_rows[par][:, 4 * (n % 2) + q, (n // 2) * P:(n // 2 + 1) * P]
                    else:
                        j, a = 2 * (n - 4) + q // 2, q % 2
                        src = fc2_rows[par][:, a, j * P:(j + 1) * P]
                    mm = nc.tensor.transpose(bank[:, q * P:(q + 1) * P], src, const.ident[:, :])
                mm.then_inc(wt_done, 1)

            pe.wait_ge(b1_here, 16)
            for j in range(NF):
                mm = nc.tensor.transpose(pO[0][:, j * NE:(j + 1) * NE], b1_rows[:, j * P:(j + 1) * P],
                                         const.ident[0:NE, 0:NE])
            mm.then_inc(b1_done, 1)
            for n in range(NF):
                weight_transposes(0, 0, 0, n)

            pe.wait_ge(made, 2)
            with pe.Fori(0, BITS) as i:
                pe.wait_ge(reduced, i + 1)
                nc.tensor.matmul(pH[0][0:R, 0:NE], ones_b[:, 0:R], cnt[:, :], start=True, stop=True).then_inc(summed, 1)
            pe.wait_ge(routed, 4)
            nc.tensor.matmul(pH[0][0:R, 0:2 * NE * NT], tri[:, :], sel[:, :, :, :].rearrange("p a e t -> p (a e t)"),
                             start=True, stop=True)
            nc.tensor.matmul(pH[1][0:R, 0:2 * NE * NT], ones_b[:, 0:R], sel[:, :, :, :].rearrange("p a e t -> p (a e t)"),
                             start=True, stop=True).then_inc(prefix_done, 1)
            with pe.Fori(0, NE // 2) as i:
                for u in range(2):
                    e = 2 * i + u
                    pe.wait_ge(hot_made, e + 1)
                    for t in range(NT):
                        mm = nc.tensor.matmul(pY[0][:, bass.ds(e * 2 * NST, 2 * NST)], hot[u][:, t, :],
                                              marks[:, e, t, :, :].rearrange("p v j -> p (v j)"),
                                              start=(t == 0), stop=(t == NT - 1))
                    mm.then_inc(ids_done, 1)

            def row_transposes(e, half, par):
                pe.wait_ge(y_here[par], 16 * NST * (half + 1))
                pe.wait_ge(yt_out, 2 * e)
                for k in range(2):
                    for j in range(NST):
                        n = rows_in[j]
                        mm = nc.tensor.transpose(pY[k][:, j * P:j * P + n], yg[par][0:n, j, k * P:(k + 1) * P],
                                                 const.ident[0:n, 0:n])
                    mm.then_inc(yt_done, 1)

            pe.wait_ge(idx_made, 1)
            row_transposes(0, 0, 0)

            def step(pe, e, half, par, prepare):
                pe.wait_ge(yt_out, 2 * (e + 1))
                pe.wait_ge(wt_act, NF // 2 * (e + 1))
                pe.wait_ge(wt_dve, NF // 2 * (e + 1))
                for j in range(NF):
                    pe.wait_ge(h_out, NF * e + max(j - 1, 0))
                    for k in range(2):
                        mm = nc.tensor.matmul(pH[j % 2][:, 0:CAP], fc1T[par][:, k, j * P:(j + 1) * P], yT[par][:, k, :],
                                              start=(k == 0), stop=(k == 1))
                    mm.then_inc(h_done, 1)
                    if prepare:
                        weight_transposes(e + 1, half + par, 1 - par, j)
                if prepare:
                    row_transposes(e + 1, half + par, 1 - par)
                pe.wait_ge(h_out, NF * (e + 1))
                pe.wait_ge(ob_made, 2 * e)
                for j in range(NST):
                    n = rows_in[j]
                    for f in range(NF):
                        mm = nc.tensor.matmul(pO[j // 2][0:n, (j % 2) * D:(j % 2 + 1) * D], hT[:, f, j * P:j * P + n],
                                              fc2T[par][:, f, :], start=(f == 0), stop=(f == NF - 1))
                    if j:
                        mm.then_inc(o_done, 1)

            steps(pe, step)

        @block.scalar
        def _(act):
            act.wait_ge(b1_done, 1)
            nc.scalar.activation(b1T[:, :, :].rearrange("p j e -> p (j e)"), pO[0][:, 0:NF * NE], ACT.Copy).then_inc(b1_out, 1)
            act.wait_ge(b1_out, 1)

            def weights_out(e, par, n):
                act.wait_ge(wt_done, NF * e + n + 1)
                nc.scalar.activation(*weight_bank(par, n), ACT.Copy).then_inc(wt_act, 1)

            def weight_bank(par, n):
                if n < 4:
                    return fc1T[par][:, n // 2, (n % 2) * 4 * P:(n % 2 + 1) * 4 * P], pW[n % 2][:, :]
                return fc2T[par][:, 2 * (n - 4):2 * (n - 3), :].rearrange("p j d -> p (j d)"), pW[n % 2][:, :]

            for n in range(0, NF, 2):
                weights_out(0, 0, n)

            def step(act, e, half, par, prepare):
                for j in range(NF):
                    act.wait_ge(h_done, NF * e + j + 1)
                    if j == 0:
                        act.wait_ge(o_done, 2 * e)
                    nc.scalar.activation(hT[:, j, :], pH[j % 2][:, 0:CAP], ACT.Gelu_apprx_tanh,
                                         bias=b1T[:, j, bass.ds(e, 1)]).then_inc(h_out, 1)
                    if prepare and j % 2 == 0:
                        weights_out(e + 1, 1 - par, j)

            steps(act, step)

        @block.vector
        def _(dve):
            def weights_out(e, par, n):
                dve.wait_ge(wt_done, NF * e + n + 1)
                if n < 4:
                    dst = fc1T[par][:, n // 2, (n % 2) * 4 * P:(n % 2 + 1) * 4 * P]
                else:
                    dst = fc2T[par][:, 2 * (n - 4):2 * (n - 3), :].rearrange("p j d -> p (j d)")
                nc.vector.tensor_copy(dst, pW[n % 2][:, :]).then_inc(wt_dve, 1)

            for n in range(1, NF, 2):
                weights_out(0, 0, n)
            link = [0]

            def chained(ins):
                link[0] += 1
                ins.then_inc(init, 1)
                dve.wait_ge(init, link[0])

            dve.wait_ge(made, 2)
            nc.vector.memset(cur[:, :], 0.0)
            nc.vector.memset(bit[:, :], 1 << (BITS - 1))
            nc.vector.memset(reset[:, :], 1.0)
            chained(nc.vector.tensor_scalar(valid1[:, :], valid[:, :], -1.0, None, ALU.add))
            nc.vector.memset(reset[:, :].rearrange("p (n t) -> p n t", t=NT)[:, :, 0:1], 0.0)
            chained(nc.vector.tensor_tensor(sc[:, :, :], scores[0:R, :, :].rearrange("p t e -> p e t"),
                                            every(valid[:, :], NE), ALU.mult))
            chained(nc.vector.tensor_tensor(sc[:, :, :], sc[:, :, :], every(valid1[:, :], NE), ALU.add))
            cur_i, cand_i = cur[:, :].bitcast(I32), cand[:, :].bitcast(I32)
            with dve.Fori(0, BITS) as i:
                dve.wait_ge(cur_made, i)
                dve.wait_ge(bit_made, i)
                nc.vector.tensor_tensor(cand_i, cur_i, bit[:, :], ALU.bitwise_or).then_inc(cand_made, 1)
                dve.wait_ge(cand_made, i + 1)
                nc.vector.tensor_tensor(over[:, :, :], sc[:, :, :], spread(cand[:, :], NT), ALU.is_ge).then_inc(counted, 1)
                dve.wait_ge(counted, i + 1)
                with nc.allow_low_precision("counts up to NT are exact in bfloat16"):
                    nc.vector.tensor_reduce(cnt[:, :], over[:, :, :], AX_X, ALU.add).then_inc(reduced, 1)
                nc.vector.tensor_scalar(bit[:, :], bit[:, :], 1, None, ALU.logical_shift_right).then_inc(bit_made, 1)
                dve.wait_ge(summed, i + 1)
                nc.vector.scalar_tensor_tensor(kept[:, :], pH[0][0:R, 0:NE], float(CAP), cand[:, :],
                                               ALU.is_ge, ALU.mult).then_inc(kept_made, 1)
                dve.wait_ge(kept_made, i + 1)
                nc.vector.tensor_tensor(cur[:, :], cur[:, :], kept[:, :], ALU.max).then_inc(cur_made, 1)
            dve.wait_ge(cur_made, BITS)
            nc.vector.tensor_tensor(sel[:, 0, :, :], sc[:, :, :], spread(cur[:, :], NT), ALU.is_gt).then_inc(routed, 2)
            nc.vector.tensor_tensor(sel[:, 1, :, :], sc[:, :, :], spread(cur[:, :], NT), ALU.is_equal).then_inc(routed, 2)
            flat = lambda t: t[:, :, :, :].rearrange("p a e t -> p (a e t)")
            dve.wait_ge(prefix_done, 1)
            chained(nc.vector.tensor_tensor_scan(flat(incl), reset[:, :], pH[1][0:R, 0:2 * NE * NT], 0.0, ALU.mult, ALU.add))
            chained(nc.vector.tensor_tensor(flat(excl), flat(incl), pH[1][0:R, 0:2 * NE * NT], ALU.subtract))
            chained(nc.vector.tensor_tensor(flat(posn), flat(excl), pH[0][0:R, 0:2 * NE * NT], ALU.add))
            over_count = incl[:, 0, :, NT - 1]
            nc.vector.scalar_tensor_tensor(slot_g[:, :, :], posn[:, 0, :, :], -FAR, sel[:, 0, :, :], ALU.add, ALU.mult)
            chained(nc.vector.tensor_tensor(slot_q[:, :, :], posn[:, 1, :, :], spread(over_count, NT), ALU.add))
            chained(nc.vector.scalar_tensor_tensor(slot_e[:, :, :], slot_q[:, :, :], -FAR, sel[:, 1, :, :], ALU.add, ALU.mult))
            chained(nc.vector.scalar_tensor_tensor(slot[:, :, :], slot_g[:, :, :], FAR, slot_e[:, :, :], ALU.add, ALU.add))
            nc.vector.tensor_scalar(hi_i[:, :, :], slot[:, :, :], 7, None, ALU.logical_shift_right)
            chained(nc.vector.tensor_scalar(lo_i[:, :, :], slot[:, :, :], P - 1, None, ALU.bitwise_and))
            nc.vector.tensor_copy(hi[:, :], hi_i[:, :, :].rearrange("p e t -> p (e t)"))
            chained(nc.vector.tensor_copy(lo[:, :, :], lo_i[:, :, :]))
            chained(nc.vector.tensor_tensor(in_tile[:, :, :], spread(hi[:, :], NST), every(iota_j[:, :], NE * NT), ALU.is_equal))
            m = marks[:, :, :, :, :].rearrange("p e t v j -> p (e t) v j")
            nc.vector.tensor_tensor(m[:, :, 0, :], in_tile[:, :, :],
                                    spread(tile_no[:, :, :].rearrange("p e t -> p (e t)"), NST), ALU.mult)
            chained(nc.vector.tensor_scalar(m[:, :, 1, :], in_tile[:, :, :], row_no[:, 0:1], None, ALU.mult))
            with dve.Fori(0, NE // 2) as i:
                for u in range(2):
                    e = 2 * i + u
                    if u == 0:
                        dve.wait_ge(ids_done, e)
                    for t in range(NT):
                        last = nc.vector.tensor_scalar(hot[u][:, t, :], iota_s[:, :], lo[:, e, t:t + 1], None, ALU.is_equal)
                    last.then_inc(hot_made, 1)
            dve.wait_ge(ids_done, NE)
            ids = pY[0][:, 0:NE * 2 * NST].rearrange("p (e v j) -> p e v j", v=2, j=NST)
            chained(nc.vector.tensor_scalar(idx_f[:, :, :], ids[:, :, 0, :], float(R), None, ALU.mult))
            nc.vector.tensor_tensor(idx[:, :, :], idx_f[:, :, :], ids[:, :, 1, :], ALU.add).then_inc(idx_made, 1)

            def rows_out(e, par):
                for k in range(2):
                    dve.wait_ge(yt_done, 2 * e + k + 1)
                    nc.vector.tensor_copy(yT[par][:, k, :], pY[k][:, 0:CAP]).then_inc(yt_out, 1)

            rows_out(0, 0)

            def step(dve, e, half, par, prepare):
                if prepare:
                    for n in range(1, NF, 2):
                        weights_out(e + 1, 1 - par, n)
                    rows_out(e + 1, 1 - par)
                dve.wait_ge(b2_here[par], 16 * (half + 1))
                dve.wait_ge(ow_made, NST * e)
                for bank, j0, nt, n in ((0, 0, 2, P), (1, 2, 1, LAST)):
                    dve.wait_ge(o_done, 2 * e + bank + 1)
                    nc.vector.tensor_tensor(ob[0:n, j0:j0 + nt, :],
                                            pO[bank][0:n, 0:nt * D].rearrange("p (t d) -> p t d", t=nt),
                                            every(b2[par][0:n, :], nt), ALU.add).then_inc(ob_made, 1)
                dve.wait_ge(ob_made, 2 * (e + 1))
                dve.wait_ge(scattered, 16 * NST * e)
                for j in range(NST):
                    n = rows_in[j]
                    nc.vector.tensor_scalar(ow[0:n, j, :], ob[0:n, j, :], yg_score(par, n, j, e), None,
                                            ALU.mult).then_inc(ow_made, 1)

            def yg_score(par, n, j, e):
                return yg[par][0:n, j, bass.ds(D + e, 1)]

            steps(dve, step)


def retention(nc, ctx, const, acc_rows, rWq, rWk, rWv, rWg, rWo, gn_gamma, gn_beta, router_w, sWg, sWu, sWd,
              h, x3_rows, logits):
    sb = lambda n, s, d=F32: ctx.enter_context(nc.sbuf_tensor("r_" + n, s, d))
    sem = lambda n: semaphore(nc, const, "r_" + n)
    H1 = rWq.shape[0]
    FS = sWg.shape[1]
    FB = FS - P
    PER = IPG * H1

    w_q = sb("w_q", [P, H1, P])
    w_k = sb("w_k", [P, H1, P])
    w_v = sb("w_v", [P, H1, P])
    w_g = sb("w_g", [P, 2, D])
    w_o = sb("w_o", [P, 2, D])
    w_r = sb("w_r", [P, 2, P])
    w_sg = sb("w_sg", [P, 2, FS])
    w_su = sb("w_su", [P, 2, FS])
    w_sd0 = sb("w_sd0", [P, D])
    w_sd1 = sb("w_sd1", [FB, D])
    gam_rows = sb("gam_rows", [2, P])
    bet_rows = sb("bet_rows", [2, P])
    gam_bet = sb("gam_bet", [P, 4])
    gap = sb("gap", [R, R])
    gammas = sb("gammas", [R, R])
    power = sb("power", [R, H1, R])
    decay_a = sb("decay_a", [R, H1, R])
    decay = sb("decay", [R, H1, R])
    pair_a = sb("pair_a", [P, P])
    pair_b = sb("pair_b", [P, P])
    pair = sb("pair", [P, P])
    half_neg = sb("half_neg", [P, PER])

    stats2 = sb("stats2", [R, 2, 6])
    mv2 = sb("mv2", [R, 2, 2])
    ve2 = sb("ve2", [R, 2])
    rstd2 = sb("rstd2", [R, 2])
    xn = sb("xn", [R, 2, D])
    xnT = sb("xnT", [P, 2, GT])
    QT = [sb(f"QT{i}", [P, H1, GT]) for i in range(2)]
    KT = [sb(f"KT{i}", [P, H1, GT]) for i in range(2)]
    V = [sb(f"V{i}", [R, 2, H1, P]) for i in range(2)]
    gate = [sb(f"gate{i}", [P, 2, GT]) for i in range(2)]
    dec = sb("dec", [R, 2, H1, R])
    ysum = sb("ysum", [P, PER])
    ymean = sb("ymean", [P, PER])
    yc = [sb(f"yc{i}", [P, PER, S]) for i in range(2)]
    ysq = sb("ysq", [P, PER, S])
    ysum2 = sb("ysum2", [P, PER])
    yvar = sb("yvar", [P, PER])
    yrstd = sb("yrstd", [P, PER])
    z1 = sb("z1", [P, 2, GT])
    z2 = sb("z2", [P, 2, GT])
    zT = sb("zT", [P, 2, GT])
    stats3 = sb("stats3", [R, 2, 6])
    mv3 = sb("mv3", [R, 2, 2])
    ve3 = sb("ve3", [R, 2])
    rstd3 = sb("rstd3", [R, 2])
    x3 = sb("x3", [R, 2, D])
    x3T = sb("x3T", [P, 2, GT])
    sg0 = sb("sg0", [P, GT])
    sg1 = sb("sg1", [FB, GT])
    hid0 = sb("hid0", [P, GT])
    hid1 = sb("hid1", [FB, GT])

    bank = [ctx.enter_context(nc.psum_tensor(f"r_bank{i}", [P, 512], F32)) for i in range(8)]
    pS, pY, pM, pF0, pF1, pT0, pT1, pT2 = bank

    loaded, made, setup = sem("loaded"), sem("made"), sem("setup")
    gb_done, gb_out = sem("gb_done"), sem("gb_out")
    h2_here = [sem(f"h2_here{i}") for i in range(2)]
    ln2_stat, ln2_var, ln2_eps, ln2_rstd, xn_made = (sem(n) for n in ("ln2_stat", "ln2_var", "ln2_eps", "ln2_rstd", "xn_made"))
    xnT_done, xnT_out = sem("xnT_done"), sem("xnT_out")
    q_done, q_out, k_done, k_out, v_done, v_out, g_done, g_out = (
        sem(n) for n in ("q_done", "q_out", "k_done", "k_out", "v_done", "v_out", "g_done", "g_out"))
    s_done, s_out, y_done, y_sum, m_done, m_out, y_cent, y_sq, y_sum2, v2_done, y_var, y_rstd = (
        sem(n) for n in ("s_done", "s_out", "y_done", "y_sum", "m_done", "m_out", "y_cent", "y_sq", "y_sum2",
                         "v2_done", "y_var", "y_rstd"))
    z1_made, z2_made, z_made, wo_done, h3_made = (sem(n) for n in ("z1_made", "z2_made", "z_made", "wo_done", "h3_made"))
    ln3_stat, ln3_var, ln3_eps, ln3_rstd, x3_made, x3_stored = (
        sem(n) for n in ("ln3_stat", "ln3_var", "ln3_eps", "ln3_rstd", "x3_made", "x3_stored"))
    x3T_done, x3T_out, lg_done, lg_out = sem("x3T_done"), sem("x3T_out"), sem("lg_done"), sem("lg_out")
    sh_done, silu_done, hid_made, dn_done, h4_made = (
        sem(n) for n in ("sh_done", "silu_done", "hid_made", "dn_done", "h4_made"))

    acc_t = acc_rows.rearrange("(t p) d -> p t d", p=R)
    pair_of = lambda n: h[:, bass.ds(2 * n, 2), :]
    x3_t = x3_rows.rearrange("(t p) d -> p t d", p=R)
    N_LOADS = 12

    def steps(eng, step):
        for g in range(-1, 2):
            step(eng, g, g % 2)
        with eng.Fori(1, NG // 2 - 1) as i:
            for par in range(2):
                step(eng, 2 * i + par, par)
        for g in range(NG - 3, NG + 2):
            step(eng, g, g % 2)

    def there(n):
        return not isinstance(n, int) or 0 <= n < NG

    def later(n, first=1):
        return not isinstance(n, int) or n >= first

    with nc.Block() as block:

        @block.sync
        def _(sp):
            for n, (t0, t1) in enumerate(((0, 4), (4, NT))):
                sp.dma_start(h[:, t0:t1, :], acc_t[:, t0:t1, :]).then_inc(h2_here[n], 16)
            for dst, src in [
                (gam_rows[:, :], gn_gamma.rearrange("(k p) -> k p", p=P)),
                (bet_rows[:, :], gn_beta.rearrange("(k p) -> k p", p=P)),
                (w_q[:, :, :], rWq.rearrange("h p n -> p h n")),
                (w_k[:, :, :], rWk.rearrange("h p n -> p h n")),
                (w_v[:, :, :], rWv.rearrange("h p n -> p h n")),
                (w_g[:, :, :], rWg.rearrange("(k p) n -> p k n", p=P)),
                (w_o[:, :, :], rWo.rearrange("(k p) n -> p k n", p=P)),
                (w_sg[:, :, :], sWg.rearrange("(k p) n -> p k n", p=P)),
                (w_su[:, :, :], sWu.rearrange("(k p) n -> p k n", p=P)),
                (w_sd0[:, :], sWd[0:P, :]),
                (w_sd1[:, :], sWd[P:FS, :]),
            ]:
                sp.dma_start(dst, src).then_inc(loaded, 16)
            sp.wait_ge(made, 1)
            sp.dma_start(w_r[:, :, 0:NE], router_w.rearrange("(k p) e -> p k e", p=P)).then_inc(loaded, 16)

            def store(g):
                sp.wait_ge(x3_made, 2 * (g + 1))
                sp.dma_start(x3_t[:, bass.ds(2 * g, 2), :], x3[:, :, :]).then_inc(x3_stored, 16)

            store(0)
            with sp.Fori(1, NG) as g:
                store(g)
            sp.wait_ge(x3_stored, 16 * NG)

        @block.tensor
        def _(pe):
            pe.wait_ge(loaded, 16 * N_LOADS)
            nc.tensor.transpose(pS[:, 0:2], gam_rows[:, :], const.ident[0:2, 0:2])
            nc.tensor.transpose(pS[:, 2:4], bet_rows[:, :], const.ident[0:2, 0:2]).then_inc(gb_done, 1)
            pe.wait_ge(gb_out, 1)
            pe.wait_ge(made, 4)

            def transposes(dst, src, done):
                for tile in range(2):
                    for k in range(2):
                        mm = nc.tensor.transpose(dst[:, k * GT + tile * R:k * GT + (tile + 1) * R],
                                                 src[:, tile, k * P:(k + 1) * P], const.ident[0:R, 0:R])
                mm.then_inc(done, 1)

            def step(pe, g, par):
                f, b, t = g + 1, g - 1, g - 2
                attend, front, back, tail = there(g), there(f), there(b), there(t)
                if back:
                    pe.wait_ge(y_sum2, b + 1)
                    pe.wait_ge(h3_made, b)
                    nc.tensor.matmul(pM[:, 0:PER], pair[:, :], ysum2[:, :], start=True, stop=True).then_inc(v2_done, 1)
                if front:
                    pe.wait_ge(xn_made, 2 * (f + 1))
                    pe.wait_ge(g_out, f)
                    transposes(pF0, xn, xnT_done)
                if attend:
                    pe.wait_ge(q_out, g + 1)
                    pe.wait_ge(k_out, g + 1)
                    pe.wait_ge(s_out, g)
                    for tile in range(2):
                        for hd in range(H1):
                            cols = slice(tile * R, (tile + 1) * R)
                            mm = nc.tensor.matmul(pS[0:R, (tile * H1 + hd) * R:(tile * H1 + hd + 1) * R],
                                                  KT[par][:, hd, cols], QT[par][:, hd, cols], start=True, stop=True)
                    mm.then_inc(s_done, 1)
                if front:
                    pe.wait_ge(xnT_out, f + 1)
                    pe.wait_ge(v_out, f)
                    for hd in range(H1):
                        mm = nc.tensor.matmul(pF1[:, hd * GT:(hd + 1) * GT], w_q[:, hd, :], xnT[:, hd, :], start=True, stop=True)
                    mm.then_inc(q_done, 1)
                    for hd in range(H1):
                        mm = nc.tensor.matmul(pF0[:, hd * GT:(hd + 1) * GT], w_k[:, hd, :], xnT[:, hd, :], start=True, stop=True)
                    mm.then_inc(k_done, 1)
                if attend:
                    pe.wait_ge(s_out, g + 1)
                    pe.wait_ge(v_out, g + 1)
                    pe.wait_ge(y_cent, g)
                    for tile in range(2):
                        for hd in range(H1):
                            mm = nc.tensor.matmul(pY[:, hd * GT + tile * R:hd * GT + (tile + 1) * R], V[par][:, tile, hd, :],
                                                  dec[:, tile, hd, :], start=True, stop=True)
                    mm.then_inc(y_done, 1)
                if tail:
                    pe.wait_ge(x3_made, 2 * (t + 1))
                    pe.wait_ge(lg_out, t)
                    transposes(pT0, x3, x3T_done)
                if front:
                    pe.wait_ge(q_out, f + 1)
                    for tile in range(2):
                        for hd in range(H1):
                            mm = nc.tensor.matmul(pF1[0:R, (tile * H1 + hd) * P:(tile * H1 + hd + 1) * P],
                                                  xnT[:, hd, tile * R:(tile + 1) * R], w_v[:, hd, :], start=True, stop=True)
                    mm.then_inc(v_done, 1)
                if attend:
                    pe.wait_ge(y_sum, g + 1)
                    pe.wait_ge(y_var, b + 1) if back else None
                    nc.tensor.matmul(pM[:, 0:PER], pair[:, :], ysum[:, :], start=True, stop=True).then_inc(m_done, 1)
                if front:
                    pe.wait_ge(k_out, f + 1)
                    for m in range(2):
                        for k in range(2):
                            mm = nc.tensor.matmul(pF0[:, m * GT:(m + 1) * GT], w_g[:, k, m * P:(m + 1) * P], xnT[:, k, :],
                                                  start=(k == 0), stop=(k == 1))
                    mm.then_inc(g_done, 1)
                if tail:
                    pe.wait_ge(x3T_out, t + 1)
                    pe.wait_ge(h4_made, t)
                    for n, w in ((0, w_sg), (1, w_su)):
                        for k in range(2):
                            nc.tensor.matmul(pT1[:, n * GT:(n + 1) * GT], w[:, k, 0:P], x3T[:, k, :],
                                             start=(k == 0), stop=(k == 1))
                    for n, w in ((0, w_sg), (1, w_su)):
                        for k in range(2):
                            mm = nc.tensor.matmul(pT2[0:FB, n * GT:(n + 1) * GT], w[:, k, P:FS], x3T[:, k, :],
                                                  start=(k == 0), stop=(k == 1))
                    mm.then_inc(sh_done, 1)
                    for tile in range(2):
                        for k in range(2):
                            mm = nc.tensor.matmul(pT0[0:R, tile * P:(tile + 1) * P], x3T[:, k, tile * R:(tile + 1) * R],
                                                  w_r[:, k, :], start=(k == 0), stop=(k == 1))
                    mm.then_inc(lg_done, 1)
                if back:
                    pe.wait_ge(z_made, b + 1)
                    pe.wait_ge(m_out, g + 1) if attend else None
                    for tile in range(2):
                        for k in range(2):
                            mm = nc.tensor.matmul(pM[0:R, tile * D:(tile + 1) * D], zT[:, k, tile * R:(tile + 1) * R],
                                                  w_o[:, k, :], start=(k == 0), stop=(k == 1))
                    mm.then_inc(wo_done, 1)
                if tail:
                    pe.wait_ge(hid_made, 2 * (t + 1))
                    for tile in range(2):
                        cols = slice(tile * R, (tile + 1) * R)
                        nc.tensor.matmul(pT1[0:R, tile * D:(tile + 1) * D], hid0[:, cols], w_sd0[:, :], start=True, stop=False)
                        mm = nc.tensor.matmul(pT1[0:R, tile * D:(tile + 1) * D], hid1[:, cols], w_sd1[:, :],
                                              start=False, stop=True)
                    mm.then_inc(dn_done, 1)

            steps(pe, step)

        @block.scalar
        def _(act):
            act.wait_ge(gb_done, 1)
            nc.scalar.activation(gam_bet[:, :], pS[:, 0:4], ACT.Copy).then_inc(gb_out, 1)
            act.wait_ge(gb_out, 1)

            def out_of(dst, src, func, done, out, n):
                act.wait_ge(done, n + 1)
                nc.scalar.activation(dst, src, func).then_inc(out, 1)

            flat = lambda a: a[:, :, :].rearrange("p a b -> p (a b)")

            def step(act, g, par):
                f, b, t, other = g + 1, g - 1, g - 2, 1 - par
                attend, front, back, tail = there(g), there(f), there(b), there(t)
                if front:
                    act.wait_ge(g_done, f)
                    out_of(flat(xnT), pF0[:, 0:2 * GT], ACT.Copy, xnT_done, xnT_out, f)
                    out_of(flat(QT[other]), pF1[:, 0:2 * GT], ACT.Copy, q_done, q_out, f)
                    out_of(flat(KT[other]), pF0[:, 0:2 * GT], ACT.Copy, k_done, k_out, f)
                if tail:
                    act.wait_ge(lg_done, t)
                    out_of(flat(x3T), pT0[:, 0:2 * GT], ACT.Copy, x3T_done, x3T_out, t)
                if attend:
                    act.wait_ge(y_cent, g + 1)
                    act.wait_ge(y_sum2, g)
                    nc.scalar.activation(ysq[:, :, :], yc[par][:, :, :], ACT.Square).then_inc(y_sq, 1)
                if back:
                    act.wait_ge(z1_made, b + 1)
                    act.wait_ge(z_made, b)
                    for k in range(2):
                        last = nc.scalar.activation(z2[:, k, :], z1[:, k, :], ACT.Identity, bias=gam_bet[:, 2 + k:3 + k],
                                                    scale=gam_bet[:, k:k + 1])
                    last.then_inc(z2_made, 1)
                if tail:
                    act.wait_ge(sh_done, t + 1)
                    act.wait_ge(hid_made, 2 * t)
                    nc.scalar.activation(sg0[:, :], pT1[:, 0:GT], ACT.Silu)
                    nc.scalar.activation(sg1[:, :], pT2[0:FB, 0:GT], ACT.Silu).then_inc(silu_done, 1)
                if front:
                    act.wait_ge(z_made, f - 1) if later(f, 2) else None
                    out_of(flat(gate[other]), pF0[:, 0:2 * GT], ACT.Relu, g_done, g_out, f)

            steps(act, step)

        @block.gpsimd
        def _(pool):
            nc.gpsimd.memset(w_r[:, :, :], 0.0).then_inc(made, 1)
            nc.gpsimd.memset(half_neg[:, :], -0.5)
            nc.gpsimd.iota(gap[:, :], pattern=[[1, R]], base=0, channel_multiplier=-1, allow_small_or_imprecise_dtypes=True)
            for h in range(H1):
                nc.gpsimd.memset(gammas[:, :], 1.0 - 2.0 ** (-5 - h)).then_inc(setup, 1)
                pool.wait_ge(setup, 2 * h + 1)
                nc.gpsimd.tensor_tensor(power[:, h, :], gammas[:, :], gap[:, :], ALU.pow).then_inc(setup, 1)
                pool.wait_ge(setup, 2 * h + 2)
            for b in range(IPT):
                cols = slice(b * S, (b + 1) * S)
                last = nc.gpsimd.affine_select(out=decay_a[:, :, cols], in_=power[:, :, cols], compare_op=ALU.is_ge, fill=0.0,
                                               base=-b * S, pattern=[[0, H1], [0, S]], channel_multiplier=1)
            nc.gpsimd.memset(pair_a[:, :], 1.0 / (2 * S)).then_inc(setup, 1)
            pool.wait_ge(setup, 2 * H1 + 1)
            for b in range(IPT):
                cols = slice(b * S, (b + 1) * S)
                nc.gpsimd.affine_select(out=decay[:, :, cols], in_=decay_a[:, :, cols], compare_op=ALU.is_gt, fill=0.0,
                                        base=(b + 1) * S, pattern=[[0, H1], [0, S]], channel_multiplier=-1)
            pa, pb, pc = (x[:, :].rearrange("p (g e) -> p g e", e=2) for x in (pair_a, pair_b, pair))
            nc.gpsimd.affine_select(out=pb, in_=pa, compare_op=ALU.is_ge, fill=0.0, base=0,
                                    pattern=[[-2, P // 2], [0, 2]], channel_multiplier=1).then_inc(made, 1)
            pool.wait_ge(made, 2)
            nc.gpsimd.affine_select(out=pc, in_=pb, compare_op=ALU.is_ge, fill=0.0, base=1,
                                    pattern=[[2, P // 2], [0, 2]], channel_multiplier=-1).then_inc(made, 2)
            pool.wait_ge(made, 4)

            def rstd_of(mv, ve, rstd, stat, eps, done, n):
                wait_alone(pool, const, stat, 2 * (n + 1))
                nc.gpsimd.tensor_scalar(ve[:, :], mv[:, :, 1], LN_EPS, None, ALU.add).then_inc(eps, 1)
                pool.wait_ge(eps, n + 1)
                nc.gpsimd.tensor_tensor(rstd[:, :], ve[:, :], const.neg_half[0:R, :], ALU.pow).then_inc(done, 1)

            def step(pool, g, par):
                b, t, n, other = g - 1, g - 2, g + 2, 1 - par
                if there(t):
                    rstd_of(mv3, ve3, rstd3, ln3_var, ln3_eps, ln3_rstd, t)
                if there(b):
                    pool.wait_ge(y_var, b + 1)
                    nc.gpsimd.tensor_tensor(yrstd[:, :], yvar[:, :], half_neg[:, :], ALU.pow).then_inc(y_rstd, 1)
                    pool.wait_ge(y_rstd, b + 1)
                    pool.wait_ge(z2_made, b)
                    nc.gpsimd.tensor_tensor(z1[:, :, :].rearrange("p k (b s) -> p (k b) s", s=S), yc[other][:, :, :],
                                            spread(yrstd[:, :], S), ALU.mult).then_inc(z1_made, 1)
                if there(n):
                    rstd_of(mv2, ve2, rstd2, ln2_var, ln2_eps, ln2_rstd, n)
                if there(b):
                    pool.wait_ge(z2_made, b + 1)
                    pool.wait_ge(g_out, b + 1)
                    pool.wait_ge(wo_done, b)
                    nc.gpsimd.tensor_tensor(zT[:, :, :], z2[:, :, :], gate[other][:, :, :], ALU.mult).then_inc(z_made, 1)

            rstd_of(mv2, ve2, rstd2, ln2_var, ln2_eps, ln2_rstd, 0)
            steps(pool, step)

        @block.vector
        def _(dve):
            def norm_stats(stats, mv, stat, var, n):
                for tile in range(2):
                    nc.vector.bn_stats(stats[:, tile, :], h[:, bass.ds(2 * n + tile, 1), :].rearrange("p a d -> p (a d)")
                                       ).then_inc(stat, 1)
                for tile in range(2):
                    wait_alone(dve, const, stat, 2 * n + tile + 1)
                    nc.vector.bn_aggr(mv[:, tile, :], stats[:, tile, :]).then_inc(var, 1)

            def normalise(dst, mv, rstd, rstd_made, made_, n):
                dve.wait_ge(rstd_made, n + 1)
                for tile in range(2):
                    nc.vector.tensor_scalar(dst[:, tile, :], h[:, bass.ds(2 * n + tile, 1), :].rearrange("p a d -> p (a d)"),
                                            mv[:, tile, 0:1], rstd[:, tile:tile + 1], ALU.subtract, ALU.mult).then_inc(made_, 1)

            def first_stats(n):
                if isinstance(n, int) and n in (0, 2):
                    dve.wait_ge(h2_here[n // 2], 16)
                norm_stats(stats2, mv2, ln2_stat, ln2_var, n)

            def first_norm(n):
                dve.wait_ge(xnT_done, n)
                normalise(xn, mv2, rstd2, ln2_rstd, xn_made, n)

            first_stats(0)
            first_norm(0)
            dve.wait_ge(made, 4)

            def step(dve, g, par):
                f, b, t, n, other = g + 1, g - 1, g - 2, g + 2, 1 - par
                attend, front, back, tail, ahead = there(g), there(f), there(b), there(t), there(n)
                if tail:
                    wait_alone(dve, const, h3_made, t + 1)
                    norm_stats(stats3, mv3, ln3_stat, ln3_var, t)
                if back:
                    dve.wait_ge(v2_done, b + 1)
                    dve.wait_ge(y_rstd, b)
                    nc.vector.tensor_scalar(yvar[:, :], pM[:, 0:PER], GN_EPS, None, ALU.add).then_inc(y_var, 1)
                if attend:
                    dve.wait_ge(s_done, g + 1)
                    dve.wait_ge(y_done, g)
                    nc.vector.tensor_tensor(dec[:, :, :, :].rearrange("p a b c -> p a (b c)"),
                                            pS[0:R, 0:2 * GT].rearrange("p (a b) -> p a b", a=2),
                                            every(decay[:, :, :].rearrange("p h s -> p (h s)"), 2), ALU.mult).then_inc(s_out, 1)
                if tail:
                    dve.wait_ge(x3T_done, t)
                    dve.wait_ge(x3_stored, 16 * t)
                    normalise(x3, mv3, rstd3, ln3_rstd, x3_made, t)
                if ahead:
                    first_stats(n)
                if attend:
                    dve.wait_ge(y_done, g + 1)
                    dve.wait_ge(m_done, g)
                    yv = pY[:, 0:2 * GT].rearrange("p (n s) -> p n s", s=S)
                    nc.vector.tensor_reduce(ysum[:, :], yv, AX_X, ALU.add).then_inc(y_sum, 1)
                if front:
                    dve.wait_ge(v_done, f + 1)
                    nc.vector.tensor_copy(V[other][:, :, :, :].rearrange("p a b c -> p (a b c)"), pF1[0:R, :]).then_inc(v_out, 1)
                if attend:
                    dve.wait_ge(m_done, g + 1)
                    nc.vector.tensor_copy(ymean[:, :], pM[:, 0:PER]).then_inc(m_out, 1)
                    dve.wait_ge(m_out, g + 1)
                    if later(g, 2):
                        dve.wait_ge(z1_made, g - 1)
                        dve.wait_ge(y_sq, g - 1)
                    nc.vector.tensor_tensor(yc[par][:, :, :], yv, spread(ymean[:, :], S), ALU.subtract).then_inc(y_cent, 1)
                if ahead:
                    first_norm(n)
                if attend:
                    dve.wait_ge(y_sq, g + 1)
                    dve.wait_ge(v2_done, g)
                    nc.vector.tensor_reduce(ysum2[:, :], ysq[:, :, :], AX_X, ALU.add).then_inc(y_sum2, 1)
                if tail:
                    dve.wait_ge(silu_done, t + 1)
                    dve.wait_ge(dn_done, t)
                    nc.vector.tensor_tensor(hid0[:, :], sg0[:, :], pT1[:, GT:2 * GT], ALU.mult).then_inc(hid_made, 1)
                    nc.vector.tensor_tensor(hid1[:, :], sg1[:, :], pT2[0:FB, GT:2 * GT], ALU.mult).then_inc(hid_made, 1)
                    dve.wait_ge(lg_done, t + 1)
                    nc.vector.tensor_copy(logits[0:R, bass.ds(2 * t, 2), :],
                                          pT0[0:R, 0:2 * P].rearrange("p (t e) -> p t e", t=2)[:, :, 0:NE]).then_inc(lg_out, 1)
                if back:
                    dve.wait_ge(wo_done, b + 1)
                    nc.vector.tensor_tensor(pair_of(b), pM[0:R, :].rearrange("p (t d) -> p t d", t=2), pair_of(b),
                                            ALU.add).then_inc(h3_made, 1)
                if tail:
                    dve.wait_ge(dn_done, t + 1)
                    nc.vector.tensor_tensor(pair_of(t), pT1[0:R, :].rearrange("p (t d) -> p t d", t=2), pair_of(t),
                                            ALU.add).then_inc(h4_made, 1)

            steps(dve, step)


def token_choice(nc, ctx, const, logits, expert_bias, eWg, eWu, eWd, h, pair_rows, x3_rows, out):
    sb = lambda n, s, d=F32: ctx.enter_context(nc.sbuf_tensor("t_" + n, s, d))
    sem = lambda n: semaphore(nc, const, "t_" + n)
    ps = lambda n, d=F32: ctx.enter_context(nc.psum_tensor("t_" + n, [P, 512], d))
    F = eWg.shape[2]
    FB = F - P
    DUMP = TOPK * NT * R
    FULL = TOK // R
    CHUNKS = [(c, min(c + 4, FULL), R) for c in range(0, FULL, 4)] + [(FULL, NT, TOK - FULL * R)]
    NV = 6
    BIG = 1.0e30

    bias = sb("bias", [R, NE])
    valid = sb("valid", [R, NT])
    sig = sb("sig", [R, NT, NE])
    tot = sb("tot", [R, NT, NE])
    best = sb("best", [R, NT])
    tie = sb("tie", [R, NT, NE])
    rank = sb("rank", [R, NT, NE])
    first = sb("first", [R, NT])
    pick = [sb(f"pick{k}", [R, NT, NE]) for k in range(TOPK)]
    rest = sb("rest", [R, NT, NE])
    prod = sb("prod", [R, NT, NE])
    w = sb("w", [R, TOPK, NT])
    wsum = sb("wsum", [R, NT])
    winv = sb("winv", [R, NT])
    wn = sb("wn", [R, TOPK, NT])
    w_left = sb("w_left", [R, TOPK, NT])
    chosen = sb("chosen", [R, NE, NT], BF16)
    ones_b = sb("ones_b", [R, P], BF16)
    tri = sb("tri", [R, R], BF16)
    reset = sb("reset", [R, NE * NT])
    incl = sb("incl", [R, NE, NT])
    excl = sb("excl", [R, NE, NT])
    posn = sb("posn", [R, NE, NT])
    tiles_i = sb("tiles_i", [R, NE], I32)
    tiles_s = sb("tiles_s", [R, NE], I32)
    tiles = sb("tiles", [R, NE])
    one8 = sb("one8", [R, NE])
    upto = sb("upto", [R, NE])
    start = sb("start", [R, NE])
    slot_all = sb("slot_all", [R, NE, NT])
    slot_f = sb("slot_f", [R, TOPK, NT])
    slot = sb("slot", [R, TOPK, NT], I32)
    hi_i = sb("hi_i", [R, TOPK, NT], I32)
    lo_i = sb("lo_i", [R, TOPK, NT], I32)
    hi = sb("hi", [R, TOPK * NT])
    lo = sb("lo", [R, TOPK * NT])
    iota_s = sb("iota_s", [R, P], BF16)
    iota_j = sb("iota_j", [R, NTILE])
    iota_w = sb("iota_w", [R, NE])
    values = sb("values", [R, NV, TOPK * NT], BF16)
    in_tile = sb("in_tile", [R, TOPK * NT, NTILE], BF16)
    marks = [sb(f"marks{i}", [R, TOPK * NT // 2, NV, NTILE], BF16) for i in range(2)]
    hot = sb("hot", [R, TOPK * NT, P], BF16)
    told = sb("told", [P, NV, NTILE])
    tok_a = sb("tok_a", [P, NTILE])
    tok_b = sb("tok_b", [P, NTILE])
    free = sb("free", [P, NTILE])
    second = sb("second", [P, NTILE])
    dump = sb("dump", [P, NTILE])
    src_idx = sb("src_idx", [P, NTILE], I32)
    dst_idx = sb("dst_idx", [P, NTILE], I32)
    w_a = sb("w_a", [P, NTILE])
    w_slot = sb("w_slot", [P, NTILE])
    owner_m = sb("owner_m", [1, NTILE, NE])
    owner_f = sb("owner_f", [1, NTILE])
    owner = sb("owner", [1, NTILE], I32)

    w_gu = sb("w_gu", [P, NE, 2, 2 * F])
    w_d0 = sb("w_d0", [P, NE, D])
    w_d1 = sb("w_d1", [FB, NE, D])
    tok_in = [sb(f"tok_in{i}", [P, 1], I32) for i in range(2)]
    tok_out = [sb(f"tok_out{i}", [P, 1], I32) for i in range(2)]
    xg = [sb(f"xg{i}", [P, D]) for i in range(2)]
    xT = [sb(f"xT{i}", [P, 2, P]) for i in range(2)]
    sg = [sb(f"sg{i}", [P, F]) for i in range(2)]
    hid = [sb(f"hid{i}", [P, F]) for i in range(2)]
    hT = [sb(f"hT{i}", [P, 2, P]) for i in range(2)]
    ow = [sb(f"ow{i}", [P, D]) for i in range(2)]
    picks = sb("picks", [R, TOPK, NT, D])

    pX = [ps(f"x{i}") for i in range(2)]
    pG = [ps(f"g{i}") for i in range(2)]
    pT = [ps(f"t{i}") for i in range(2)]
    pD = [ps(f"d{i}") for i in range(2)]

    def steps(eng, parts):
        def step(half, par):
            for lead, part in parts.items():
                n = 2 * half + par + lead
                if not isinstance(n, int) or 0 <= n < NTILE:
                    shift, parity = divmod(par + lead, 2)
                    part(n, half + shift, parity)

        for j in range(-2, 2):
            step(j // 2, j % 2)
        with eng.Fori(1, NTILE // 2 - 2) as i:
            for par in range(2):
                step(i, par)
        for j in range(NTILE - 4, NTILE + 1):
            step(j // 2, j % 2)

    def follows(nth):
        return not isinstance(nth, int) or nth > 0

    loaded, w_here, made, link, sig_made = sem("loaded"), sem("w_here"), sem("made"), sem("link"), sem("sig_made")
    chosen_made, prefix_done, marks_made, told_done, idx_made = (
        sem(n) for n in ("chosen_made", "prefix_done", "marks_made", "told_done", "idx_made"))
    tok_in_made, tok_out_made = sem("tok_in_made"), sem("tok_out_made")
    scattered = [sem(f"scattered{i}") for i in range(2)]
    picked = [sem(f"picked{c}") for c in range(len(CHUNKS))]
    x_here = [sem(f"x_here{i}") for i in range(2)]
    xT_done, xT_out, g_done, silu_done, hid_made, hT_done, hT_out, d_done, ow_made = (
        sem(n) for n in ("xT_done", "xT_out", "g_done", "silu_done", "hid_made", "hT_done", "hT_out", "d_done", "ow_made"))
    first_added, out_made, out_done = sem("first_added"), sem("out_made"), sem("out_done")

    with nc.Block() as block:

        @block.sync
        def _(sp):
            sp.dma_start(bias[:, :], expert_bias.rearrange("(a e) -> a e", a=1).broadcast_to([R, NE])).then_inc(loaded, 16)
            for dst, src in [
                (w_gu[:, :, 0, 0:F], eWg[:, 0:P, :].rearrange("e p f -> p e f")),
                (w_gu[:, :, 1, 0:F], eWg[:, P:D, :].rearrange("e p f -> p e f")),
                (w_gu[:, :, 0, F:2 * F], eWu[:, 0:P, :].rearrange("e p f -> p e f")),
                (w_gu[:, :, 1, F:2 * F], eWu[:, P:D, :].rearrange("e p f -> p e f")),
                (w_d0[:, :, :], eWd[:, 0:P, :].rearrange("e p d -> p e d")),
                (w_d1[:, :, :], eWd[:, P:F, :].rearrange("e p d -> p e d")),
            ]:
                sp.dma_start(dst, src).then_inc(w_here, 16)
            for par in range(2):
                sp.wait_ge(scattered[par], 16 * NTILE // 2)
            pair_t = pair_rows[0:TOPK * NT * R, :].rearrange("(k t p) d -> p k t d", k=TOPK, p=R)
            for c, (t0, t1, rows) in enumerate(CHUNKS):
                for k in range(TOPK):
                    sp.dma_start(picks[0:rows, k, t0:t1, :], pair_t[0:rows, k, t0:t1, :]).then_inc(picked[c], 16)
            for c, (t0, t1, rows) in enumerate(CHUNKS):
                sp.wait_ge(out_made, c + 1)
                o = out.rearrange("b s d -> (b s) d")[t0 * R:t0 * R + (t1 - t0) * rows, :]
                sp.dma_start(o.rearrange("(t p) d -> p t d", p=rows), picks[0:rows, 1, t0:t1, :]).then_inc(out_done, 16)
            sp.wait_ge(out_done, 16 * len(CHUNKS))

        @block.gpsimd
        def _(pool):
            nc.gpsimd.memset(ones_b[:, :], 1.0)
            nc.gpsimd.memset(valid[:, :], 1.0)
            nc.gpsimd.memset(one8[:, :], 1.0)
            nc.gpsimd.memset(values[:, NV - 1, :], 1.0)
            nc.gpsimd.memset(reset[:, :], 1.0).then_inc(made, 1)
            pool.wait_ge(made, 1)
            nc.gpsimd.memset(reset[:, :].rearrange("p (n t) -> p n t", t=NT)[:, :, 0:1], 0.0)
            nc.gpsimd.affine_select(out=tri[:, :], in_=ones_b[:, 0:R], compare_op=ALU.is_gt, fill=0.0,
                                    base=0, pattern=[[1, R]], channel_multiplier=-1)
            nc.gpsimd.affine_select(out=valid[:, NT - 1:NT], in_=ones_b[:, 0:1], compare_op=ALU.is_gt, fill=0.0,
                                    base=TOK - (NT - 1) * R, pattern=[[0, 1]], channel_multiplier=-1)
            iota = lambda o, pattern, base=0, mult=0: nc.gpsimd.iota(
                o, pattern=pattern, base=base, channel_multiplier=mult, allow_small_or_imprecise_dtypes=True)
            iota(iota_s[:, :], [[1, P]])
            iota(iota_j[:, :], [[1, NTILE]])
            iota(iota_w[:, :], [[-1, NE]], base=NE)
            iota(values[:, 0, :], [[1, TOPK * NT]])
            iota(values[:, 1, :], [[0, TOPK * NT]], mult=1)
            iota(dump[:, :], [[P, NTILE]], base=DUMP, mult=1).then_inc(made, 1)

            def gather(n, nth, par):
                pool.wait_ge(xT_done, n - 1) if follows(nth) else None
                nc.gpsimd.tensor_copy(tok_in[par][:, :], src_idx[:, bass.ds(n, 1)]).then_inc(tok_in_made, 1)
                wait_alone(pool, const, tok_in_made, n + 1)
                nc.gpsimd.indirect_dma_start(out=xg[par][:, :], out_offset=None, in_=x3_rows[:, :],
                                             in_offset=bass.IndirectOffsetOnAxis(ap=tok_in[par][:, 0:1], axis=0)
                                             ).then_inc(x_here[par], 16)

            def scatter(n, nth, par):
                pool.wait_ge(scattered[par], 16 * nth)
                nc.gpsimd.tensor_copy(tok_out[par][:, :], dst_idx[:, bass.ds(n, 1)]).then_inc(tok_out_made, 1)
                pool.wait_ge(tok_out_made, n + 1)
                wait_alone(pool, const, ow_made, n + 1)
                nc.gpsimd.indirect_dma_start(out=pair_rows[:, :],
                                             out_offset=bass.IndirectOffsetOnAxis(ap=tok_out[par][:, 0:1], axis=0),
                                             in_=ow[par][:, :], in_offset=None).then_inc(scattered[par], 16)

            pool.wait_ge(idx_made, 2)
            for n in range(2):
                gather(n, 0, n)
            steps(pool, {4: gather, -1: scatter})

        @block.tensor
        def _(pe):
            pe.wait_ge(chosen_made, 1)
            pe.wait_ge(made, 2)
            c = chosen[:, :, :].rearrange("p e t -> p (e t)")
            nc.tensor.matmul(pX[0][0:R, 0:NE * NT], tri[:, :], c, start=True, stop=True)
            nc.tensor.matmul(pX[1][0:R, 0:NE * NT], ones_b[:, 0:R], c, start=True, stop=True).then_inc(prefix_done, 1)
            for n in range(TOPK * NT):
                if n % NT == 0:
                    pe.wait_ge(marks_made, n // NT + 1)
                mm = nc.tensor.matmul(pG[0][:, 0:NV * NTILE], hot[:, n, :],
                                      marks[n // NT][:, n % NT, :, :].rearrange("p v j -> p (v j)"),
                                      start=(n == 0), stop=(n == TOPK * NT - 1))
            mm.then_inc(told_done, 1)
            pe.wait_ge(w_here, 16 * 6)
            pe.wait_ge(idx_made, 2)

            def expert(n):
                return pe.value_load(owner[0:1, bass.ds(n, 1)], min_val=0, max_val=NE - 1)

            def transpose_rows(n, nth, par):
                pe.wait_ge(x_here[par], 16 * (nth + 1))
                pe.wait_ge(xT_out, n - 1) if follows(nth) else None
                for k in range(2):
                    mm = nc.tensor.transpose(pX[par][:, k * P:(k + 1) * P], xg[par][:, k * P:(k + 1) * P], const.ident[:, :])
                mm.then_inc(xT_done, 1)

            def gate_up(n, nth, par):
                e = expert(n)
                pe.wait_ge(xT_out, n + 1)
                pe.wait_ge(hid_made, n - 1) if follows(nth) else None
                for k in range(2):
                    mm = nc.tensor.matmul(pG[par][:, 0:2 * F], xT[par][:, k, :], w_gu[:, bass.ds(e, 1), k, :],
                                          start=(k == 0), stop=(k == 1))
                mm.then_inc(g_done, 1)

            def hidden_transposes(n, nth, par):
                pe.wait_ge(hid_made, n + 1)
                pe.wait_ge(hT_out, n - 1) if follows(nth) else None
                nc.tensor.transpose(pT[par][:, 0:P], hid[par][:, 0:P], const.ident[:, :])
                nc.tensor.transpose(pT[par][0:FB, P:2 * P], hid[par][:, P:F], const.ident[:, :]).then_inc(hT_done, 1)

            def down(n, nth, par):
                e = expert(n)
                pe.wait_ge(hT_out, n + 1)
                pe.wait_ge(ow_made, n - 1) if follows(nth) else None
                nc.tensor.matmul(pD[par][:, 0:D], hT[par][:, 0, :], w_d0[:, bass.ds(e, 1), :], start=True, stop=False)
                nc.tensor.matmul(pD[par][:, 0:D], hT[par][0:FB, 1, :], w_d1[:, bass.ds(e, 1), :],
                                 start=False, stop=True).then_inc(d_done, 1)

            steps(pe, {2: transpose_rows, 1: gate_up, 0: hidden_transposes, -1: down})

        @block.scalar
        def _(act):
            nc.scalar.activation(sig[:, :, :], logits[0:R, :, :], ACT.Sigmoid).then_inc(sig_made, 1)

            def silu(n, nth, par):
                act.wait_ge(g_done, n + 1)
                act.wait_ge(hid_made, n - 1) if follows(nth) else None
                nc.scalar.activation(sg[par][:, :], pG[par][:, 0:F], ACT.Silu).then_inc(silu_done, 1)

            def hidden_out(n, nth, par):
                act.wait_ge(hT_done, n + 1)
                act.wait_ge(d_done, n - 1) if follows(nth) else None
                nc.scalar.activation(hT[par][:, 0, :], pT[par][:, 0:P], ACT.Copy)
                nc.scalar.activation(hT[par][0:FB, 1, :], pT[par][0:FB, P:2 * P], ACT.Copy).then_inc(hT_out, 1)

            steps(act, {1: silu, 0: hidden_out})

        @block.vector
        def _(dve):
            links = [0]

            def chained(ins):
                links[0] += 1
                ins.then_inc(link, 1)
                dve.wait_ge(link, links[0])

            dve.wait_ge(loaded, 16)
            dve.wait_ge(sig_made, 1)
            dve.wait_ge(made, 2)
            chained(nc.vector.tensor_tensor(tot[:, :, :], sig[:, :, :], every(bias[:, :], NT), ALU.add))
            for k in range(TOPK):
                src = (tot, rest)[k]
                chained(nc.vector.tensor_reduce(best[:, :], src[:, :, :], AX_X, ALU.max))
                chained(nc.vector.tensor_tensor(tie[:, :, :], src[:, :, :], spread(best[:, :], NE), ALU.is_equal))
                chained(nc.vector.tensor_tensor(rank[:, :, :], tie[:, :, :], every(iota_w[:, :], NT), ALU.mult))
                chained(nc.vector.tensor_reduce(first[:, :], rank[:, :, :], AX_X, ALU.max))
                chained(nc.vector.tensor_tensor(pick[k][:, :, :], rank[:, :, :], spread(first[:, :], NE), ALU.is_equal))
                if k == 0:
                    chained(nc.vector.scalar_tensor_tensor(rest[:, :, :], pick[0][:, :, :], -BIG, tot[:, :, :],
                                                           ALU.mult, ALU.add))
                chained(nc.vector.tensor_tensor(prod[:, :, :], pick[k][:, :, :], sig[:, :, :], ALU.mult))
                chained(nc.vector.tensor_reduce(w[:, k, :], prod[:, :, :], AX_X, ALU.add))
            chained(nc.vector.tensor_tensor(prod[:, :, :], pick[0][:, :, :], pick[1][:, :, :], ALU.add))
            nc.vector.tensor_tensor(chosen[:, :, :], prod[:, :, :].rearrange("p t e -> p e t"), every(valid[:, :], NE),
                                    ALU.mult).then_inc(chosen_made, 1)
            chained(nc.vector.tensor_tensor(wsum[:, :], w[:, 0, :], w[:, 1, :], ALU.add))
            chained(nc.vector.tensor_scalar(wsum[:, :], wsum[:, :], 1e-20, None, ALU.add))
            chained(nc.vector.reciprocal(winv[:, :], wsum[:, :]))
            chained(nc.vector.tensor_tensor(wn[:, :, :], w[:, :, :], every(winv[:, :], TOPK), ALU.mult))
            vw = lambda n: values[:, 2 + n, :].rearrange("p (k t) -> p k t", k=TOPK)
            chained(nc.vector.tensor_copy(vw(0), wn[:, :, :]))
            chained(nc.vector.tensor_tensor(w_left[:, :, :], wn[:, :, :], vw(0), ALU.subtract))
            chained(nc.vector.tensor_copy(vw(1), w_left[:, :, :]))
            chained(nc.vector.tensor_tensor(vw(2), w_left[:, :, :], vw(1), ALU.subtract))
            dve.wait_ge(prefix_done, 1)
            fl = lambda a: a[:, :, :].rearrange("p a b -> p (a b)")
            counts = pX[1][0:R, 0:NE * NT]
            chained(nc.vector.tensor_tensor_scan(fl(incl), reset[:, :], counts, 0.0, ALU.mult, ALU.add))
            chained(nc.vector.tensor_tensor(fl(excl), fl(incl), counts, ALU.subtract))
            nc.vector.tensor_tensor(fl(posn), fl(excl), pX[0][0:R, 0:NE * NT], ALU.add)
            chained(nc.vector.tensor_scalar(tiles_i[:, :], incl[:, :, NT - 1], float(P - 1), None, ALU.add))
            chained(nc.vector.tensor_scalar(tiles_s[:, :], tiles_i[:, :], 7, None, ALU.logical_shift_right))
            chained(nc.vector.tensor_copy(tiles[:, :], tiles_s[:, :]))
            chained(nc.vector.tensor_tensor_scan(upto[:, :], one8[:, :], tiles[:, :], 0.0, ALU.mult, ALU.add))
            chained(nc.vector.tensor_tensor(start[:, :], upto[:, :], tiles[:, :], ALU.subtract))
            chained(nc.vector.tensor_scalar(start[:, :], start[:, :], float(P), None, ALU.mult))
            chained(nc.vector.tensor_tensor(slot_all[:, :, :], posn[:, :, :], spread(start[:, :], NT), ALU.add))
            for k in range(TOPK):
                chained(nc.vector.tensor_tensor(prod[:, :, :], pick[k][:, :, :],
                                                slot_all[:, :, :].rearrange("p e t -> p t e"), ALU.mult))
                chained(nc.vector.tensor_reduce(slot_f[:, k, :], prod[:, :, :], AX_X, ALU.add))
            far = float(P * 127)
            chained(nc.vector.scalar_tensor_tensor(slot_f[:, :, :], slot_f[:, :, :], -far, every(valid[:, :], TOPK),
                                                   ALU.add, ALU.mult))
            chained(nc.vector.tensor_scalar(slot[:, :, :], slot_f[:, :, :], far, None, ALU.add))
            nc.vector.tensor_scalar(hi_i[:, :, :], slot[:, :, :], 7, None, ALU.logical_shift_right)
            chained(nc.vector.tensor_scalar(lo_i[:, :, :], slot[:, :, :], P - 1, None, ALU.bitwise_and))
            nc.vector.tensor_copy(hi[:, :], fl(hi_i))
            chained(nc.vector.tensor_copy(lo[:, :], fl(lo_i)))
            nc.vector.tensor_tensor(owner_m[:, :, :], every(upto[0:1, :], NTILE), spread(iota_j[0:1, :], NE), ALU.is_le)
            chained(nc.vector.tensor_tensor(in_tile[:, :, :], spread(hi[:, :], NTILE), every(iota_j[:, :], TOPK * NT),
                                            ALU.is_equal))
            chained(nc.vector.tensor_reduce(owner_f[:, :], owner_m[:, :, :], AX_X, ALU.add))
            nc.vector.tensor_scalar(owner[:, :], owner_f[:, :], float(NE - 1), None, ALU.min).then_inc(idx_made, 1)
            for k in range(TOPK):
                cols = slice(k * NT, (k + 1) * NT)
                for v in range(NV):
                    nc.vector.tensor_tensor(marks[k][:, :, v, :], in_tile[:, cols, :], spread(values[:, v, cols], NTILE), ALU.mult)
                for n in range(k * NT, (k + 1) * NT):
                    last = nc.vector.tensor_scalar(hot[:, n, :], iota_s[:, :], lo[:, n:n + 1], None, ALU.is_equal)
                last.then_inc(marks_made, 1)
            dve.wait_ge(told_done, 1)
            chained(nc.vector.tensor_copy(told[:, :, :], pG[0][:, 0:NV * NTILE].rearrange("p (v j) -> p v j", v=NV)))
            nc.vector.scalar_tensor_tensor(tok_a[:, :], told[:, 0, :], float(R), told[:, 1, :], ALU.mult, ALU.add)
            chained(nc.vector.tensor_scalar(second[:, :], told[:, 0, :], float(NT), -float(NT * R), ALU.is_ge, ALU.mult))
            nc.vector.tensor_tensor(src_idx[:, :], tok_a[:, :], second[:, :], ALU.add)
            chained(nc.vector.tensor_scalar(free[:, :], told[:, 5, :], -1.0, 1.0, ALU.mult, ALU.add))
            chained(nc.vector.tensor_tensor(tok_b[:, :], free[:, :], dump[:, :], ALU.mult))
            chained(nc.vector.tensor_tensor(dst_idx[:, :], tok_a[:, :], tok_b[:, :], ALU.add))
            chained(nc.vector.tensor_tensor(w_a[:, :], told[:, 3, :], told[:, 4, :], ALU.add))
            nc.vector.tensor_tensor(w_slot[:, :], w_a[:, :], told[:, 2, :], ALU.add).then_inc(idx_made, 1)
            dve.wait_ge(idx_made, 2)

            def rows_out(n, nth, par):
                dve.wait_ge(xT_done, n + 1)
                dve.wait_ge(g_done, n - 1) if follows(nth) else None
                nc.vector.tensor_copy(xT[par][:, :, :].rearrange("p k s -> p (k s)"), pX[par][:, 0:2 * P]).then_inc(xT_out, 1)

            def hidden(n, nth, par):
                dve.wait_ge(silu_done, n + 1)
                dve.wait_ge(hT_done, n - 1) if follows(nth) else None
                nc.vector.tensor_tensor(hid[par][:, :], sg[par][:, :], pG[par][:, F:2 * F], ALU.mult).then_inc(hid_made, 1)

            def weigh(n, nth, par):
                dve.wait_ge(d_done, n + 1)
                dve.wait_ge(scattered[par], 16 * nth)
                nc.vector.tensor_scalar(ow[par][:, :], pD[par][:, 0:D], w_slot[:, bass.ds(n, 1)], None, ALU.mult).then_inc(ow_made, 1)

            steps(dve, {2: rows_out, 1: hidden, -1: weigh})

            for c, (t0, t1, rows) in enumerate(CHUNKS):
                dve.wait_ge(picked[c], 32)
                a, b = (picks[0:rows, k, t0:t1, :] for k in range(TOPK))
                nc.vector.tensor_tensor(a, a, h[0:rows, t0:t1, :], ALU.add).then_inc(first_added, 1)
                dve.wait_ge(first_added, c + 1)
                nc.vector.tensor_tensor(b, a, b, ALU.add).then_inc(out_made, 1)


def wait_alone(eng, const, sem, value):
    eng.wait_ge(sem, value)
    eng.sem_inc(const.waits_passed, 1)


def semaphore(nc, const, name):
    s = nc.alloc_semaphore(name=name)
    const.semaphores.append(s)
    return s


def end_stage(nc, const):
    nc.clear_and_free_semaphores(const.semaphores)
    nc.all_engine_barrier()
    const.semaphores = []


def twice(ap):
    return every(ap, 2)


def every(ap, n):
    return ap.unsqueeze(1).broadcast_to([ap.shape[0], n, ap.shape[1]])


def both(ap):
    return every(ap, 2)


def spread(ap, n):
    return ap.unsqueeze(2).broadcast_to([ap.shape[0], ap.shape[1], n])


Q_BANK = (1, 2, 0, 1)


def q_columns(bank, m):
    return bank[:, m * GT:(m + 1) * GT].rearrange("p (b s) -> p b s", s=S)


def patch_columns(bank, k):
    n = NPH * IPG * NPH
    return bank[:, (k % 2) * n:(k % 2 + 1) * n].rearrange("p (w b t) -> p w b t", w=NPH, b=IPG)


def patch_slots(patT, k):
    return patT[:, k, :].rearrange("p (b s) -> p b s", s=S)[:, :, 1:S].rearrange("p b (t w) -> p w b t", w=NPH)


_INS = ['x', 'L0_tok_W', 'L0_tok_b', 'L0_tok_cls_token', 'L0_tok_pos_embed', 'L0_attn_Wq', 'L0_attn_bq', 'L0_attn_Wk',
        'L0_attn_bk', 'L0_attn_Wv', 'L0_attn_bv', 'L0_attn_Wo', 'L0_attn_bo', 'L0_ffn_gate_w', 'L0_ffn_ln_w',
        'L0_ffn_ln_b', 'L0_ffn_fc1s', 'L0_ffn_b1s', 'L0_ffn_fc2s', 'L0_ffn_b2s', 'L1_attn_Wq', 'L1_attn_Wk',
        'L1_attn_Wv', 'L1_attn_Wg', 'L1_attn_Wo', 'L1_attn_gn_gamma', 'L1_attn_gn_beta', 'L1_ffn_W_gate_router',
        'L1_ffn_expert_bias', 'L1_ffn_Wg', 'L1_ffn_Wu', 'L1_ffn_Wd', 'L1_ffn_Wg_s', 'L1_ffn_Wu_s', 'L1_ffn_Wd_s']
_OUTS = [((NB, S, D), 'float32')]


def kernel(**inputs):
    import numpy as _np
    import concourse.bacc as _bacc
    from concourse import mybir as _mybir
    from concourse.bass_utils import run_bass_kernel_spmd as _run

    nc = _bacc.Bacc("TRN2", target_bir_lowering=False, num_devices=1)
    arrays, args = {}, []
    for name in _INS:
        a = _np.ascontiguousarray(inputs[name])
        arrays[f"in_{name}_dram"] = a
        args.append(nc.dram_tensor(f"in_{name}_dram", a.shape, _mybir.dt.from_np(a.dtype), kind="ExternalInput").ap())
    for i, (shape, dtype) in enumerate(_OUTS):
        dt = _mybir.dt.from_np(_np.dtype(dtype))
        args.append(nc.dram_tensor(f"out_{i}_dram", shape, dt, kind="ExternalOutput").ap())
    program(nc, *args)
    r = _run(nc, [arrays], core_ids=[0])
    got = tuple(r.results[0][f"out_{i}_dram"] for i in range(len(_OUTS)))
    return got[0]
```

```python
import math
from contextlib import ExitStack

import concourse.bass as bass
from concourse import mybir

ALU = mybir.AluOpType
ACT = mybir.ActivationFunctionType
F32 = mybir.dt.float32
F32R = mybir.dt.float32r
BF16 = mybir.dt.bfloat16
I32 = mybir.dt.int32
AX_X = mybir.AxisListType.X

P = 128
D = 256
NB = 64
C, IMG, PATCH = 3, 96, 16
NPH = IMG // PATCH
S = NPH * NPH + 1
KP = C * PATCH * PATCH // P
H0, DK = 16, 64
NPAIR = H0 // 2
IPT = 3
R = IPT * S
IPG = 2 * IPT
GT = 2 * R
NT = -(-NB // IPG) * 2
NG = NT // 2
TOK = NB * S
IROWS = C * NPH
XR = IPG * IROWS
NE = 8
CAP = TOK // NE
TOPK = 2
NTILE = (TOK * TOPK + NE * (P - 1)) // P
YW = D + NE
LN_EPS = 1e-5
GN_EPS = 1e-3
SCALE0 = DK ** -0.5


def program(nc, x, tok_W, tok_b, cls_token, pos_embed, Wq, bq, Wk, bk, Wv, bv, Wo, bo, gate_w, ln_w, ln_b,
            fc1s, b1s, fc2s, b2s, rWq, rWk, rWv, rWg, rWo, gn_gamma, gn_beta, router_w, expert_bias,
            eWg, eWu, eWd, sWg, sWu, sWd, out):
    with ExitStack() as ctx:
        acc_rows = nc.dram_tensor("acc_rows", (NT * R, D), F32, kind="Internal").ap()
        y_rows = nc.dram_tensor("y_rows", (NT * R, YW), F32, kind="Internal").ap()
        x3_rows = nc.dram_tensor("x3_rows", (NT * R, D), F32, kind="Internal").ap()
        pair_rows = nc.dram_tensor("pair_rows", (TOPK * NT * R + NTILE * P, D), F32, kind="Internal").ap()
        scores = ctx.enter_context(nc.sbuf_tensor("scores", [P, NT, NE], F32))
        logits = ctx.enter_context(nc.sbuf_tensor("logits", [P, NT, NE], F32))
        const = constants(nc, ctx)
        with ExitStack() as stage:
            embed_and_attend(nc, stage, const, x, tok_W, tok_b, cls_token, pos_embed, Wq, bq, Wk, bk, Wv, bv,
                             Wo, bo, gate_w, ln_w, ln_b, acc_rows, y_rows, scores)
        end_stage(nc, const)
        ready = RetentionReady(nc, ctx, rWq, rWk, rWv, rWg, rWo, gn_gamma, gn_beta, router_w, sWg, sWu, sWd)
        with ExitStack() as stage:
            expert_choice(nc, stage, const, ready, scores, fc1s, b1s, fc2s, b2s, acc_rows, y_rows)
        end_stage(nc, const)
        h = ctx.enter_context(nc.sbuf_tensor("h", [R, NT, D], F32))
        with ExitStack() as stage:
            retention(nc, stage, const, ready, acc_rows, h, x3_rows, logits)
        end_stage(nc, const)
        with ExitStack() as stage:
            token_choice(nc, stage, const, logits, expert_bias, eWg, eWu, eWd, h, pair_rows, x3_rows, out)


class Const:
    pass


def constants(nc, ctx):
    c = Const()
    c.semaphores = []
    sb = lambda n, s, d: ctx.enter_context(nc.sbuf_tensor(n, s, d))
    c.ident = sb("ident", [P, P], F32)
    c.zero = sb("zero", [P, P], F32)
    c.neg_half = sb("neg_half", [P, 2], F32)
    made = c.made = ctx.enter_context(nc.semaphore("const_made"))
    c.waits_passed = ctx.enter_context(nc.semaphore("waits_passed"))
    with nc.Block() as block:
        @block.gpsimd
        def _(pool):
            nc.gpsimd.memset(c.neg_half[:, :], -0.5).then_inc(made, 1)
            nc.gpsimd.memset(c.zero[:, :], 0.0).then_inc(made, 1)
            pool.wait_ge(made, 2)
            nc.gpsimd.affine_select(out=c.ident[:, :], in_=c.zero[:, :], compare_op=ALU.not_equal, fill=1.0,
                                    base=0, pattern=[[-1, P]], channel_multiplier=1).then_inc(made, 1)
            pool.wait_ge(made, 3)
    return c


def embed_and_attend(nc, ctx, const, x, tok_W, tok_b, cls_token, pos_embed, Wq, bq, Wk, bk, Wv, bv,
                     Wo, bo, gate_w, ln_w, ln_b, acc_rows, y_rows, scores):
    sb = lambda n, s, d=F32: ctx.enter_context(nc.sbuf_tensor(n, s, d))
    sem = lambda n: semaphore(nc, const, "a_" + n)

    shared = sb("shared", [P, 13 * 512])
    used = {"weights": 0, "activations": 0}

    def view(kind, rows, *sizes):
        n = math.prod(sizes)
        start = used[kind]
        used[kind] += n
        assert used[kind] <= shared.shape[1]
        names = "abcd"[:len(sizes)]
        return shared[0:rows, start:start + n].rearrange(f"p ({' '.join(names)}) -> p {' '.join(names)}",
                                                         **dict(zip(names[1:], sizes[1:])))

    w_rows = view("weights", P, D // P, KP * P)
    two = lambda n, s: [sb(f"{n}_{part}", s, F32R) for part in ("high", "low")]
    w_tok = two("w_tok", [P, KP, D])
    w_q_in = view("weights", P, 2, H0 * DK)
    w_q = two("w_q", [P, 2, H0 * DK])
    w_kv_in = view("weights", P, 2, 2, 2, DK)
    w_kv = two("w_kv", [P, 2, 2, 2, DK])
    w_o_in = view("weights", P, NPAIR, D)
    w_o = two("w_o", [P, NPAIR, D])
    gate_rows = sb("gate_rows", [NE, D])
    w_gate = sb("w_gate", [P, 2, P])
    bq_rows = sb("bq_rows", [NPAIR, P])
    b_q = sb("b_q", [P, NPAIR])
    b_k2 = sb("b_k2", [P, 1])
    b_v2 = sb("b_v2", [P, 1])
    b_o = sb("b_o", [R, D])
    pos = sb("pos", [R, D])
    base = sb("base", [R, D])
    table = sb("table", [R, D])
    lnw = sb("lnw", [R, D])
    lnb = sb("lnb", [R, D])
    vmask = sb("vmask", [2 * S, P])
    ones_s = sb("ones_s", [2 * S, P])

    x_in = [sb(f"x_in{i}", [XR, PATCH * IMG]) for i in range(2)]
    x_pat = sb("x_pat", [XR, NPH, PATCH * PATCH])
    patT = two("patT", [P, KP, GT])
    h0 = sb("h0", [R, 2, D])
    h0b = [sb(f"h0b{i}", [R, 2, D]) for i in range(2)]
    stats0 = sb("stats0", [R, 2, 6])
    mv0 = sb("mv0", [R, 2, 2])
    ve0 = sb("ve0", [R, 2])
    rstd0 = sb("rstd0", [R, 2])
    xn = sb("xn", [R, 2, D])
    xnT = two("xnT", [P, 2, GT])
    QT = [sb(f"QT{i}", [P, IPG, NPAIR, S]) for i in range(2)]
    Kbd = [sb(f"Kbd{i}", [P, IPG + 1, 2, S]) for i in range(2)]
    VT = sb("VT", [P, IPG, 2, S])
    Vbd = [sb(f"Vbd{i}", [2 * S, IPG, P]) for i in range(2)]
    NCH = 3
    SUB = 2 * NCH * 2
    W3 = 2 * NCH * 2 * S
    smax = sb("smax", [R, 3, SUB])
    ssum = sb("ssum", [R, 3, SUB])
    sinv = sb("sinv", [R, 3, SUB])
    prob = view("activations", R, 3, W3)
    PT = [sb(f"PT{i}", [2 * S, NPAIR * S]) for i in range(2)]
    OT = two("OT", [P, NPAIR, GT])
    h1 = [view("activations", R, 2, D) for _ in range(2)]
    stats1 = sb("stats1", [R, 2, 6])
    mv1 = sb("mv1", [R, 2, 2])
    ve1 = sb("ve1", [R, 2])
    rstd1 = sb("rstd1", [R, 2])
    xn1 = view("activations", R, 2, D)
    res = view("activations", R, 2, D)
    xn1T = view("activations", P, 2, GT)
    lmax = sb("lmax", [R, 2])
    lexp = sb("lexp", [R, 2, NE])
    lsum = sb("lsum", [R, 2])
    linv = sb("linv", [R, 2])
    stats2 = sb("stats2", [R, 2, 6])
    mv2 = sb("mv2", [R, 2, 2])
    ve2 = sb("ve2", [R, 2])
    rstd2 = sb("rstd2", [R, 2])
    yn = view("activations", R, 2, D)
    ym = view("activations", R, 2, D)
    yo = view("activations", R, 2, YW)

    ring = [ctx.enter_context(nc.psum_tensor(f"a_ring{i}", [P, 512], F32)) for i in range(3)]
    pS = [ctx.enter_context(nc.psum_tensor(f"a_score{i}", [P, 512], F32)) for i in range(3)]
    pPT = ctx.enter_context(nc.psum_tensor("a_pt", [P, 512], F32))
    pO = ctx.enter_context(nc.psum_tensor("a_o", [P, 512], F32))

    rows_in, base_in, cls_in, early_in, late_in = (
        sem(n) for n in ("rows_in", "base_in", "cls_in", "early_in", "late_in"))
    w_q_here, w_kv_here, w_o_here = sem("w_q_here"), sem("w_kv_here"), sem("w_o_here")
    cleared, masked = sem("cleared"), sem("masked")
    wT_done, wT_out, w_tok_low = sem("wT_done"), sem("wT_out"), sem("w_tok_low")
    w_in_high, w_in_low, w_o_high, w_o_low = sem("w_in_high"), sem("w_in_low"), sem("w_o_high"), sem("w_o_low")
    table_made = sem("table_made")
    x_here = [sem(f"x_here{i}") for i in range(2)]
    x_sorted = [sem(f"x_sorted{j}") for j in range(3)]
    xt_done, xt_out, xt_low = sem("xt_done"), sem("xt_out"), sem("xt_low")
    emb_done, emb_out, h0b_made = sem("emb_done"), sem("emb_out"), sem("h0b_made")
    ln0_stat, ln0_var, ln0_eps, ln0_rstd, xn_made = (
        sem(n) for n in ("ln0_stat", "ln0_var", "ln0_eps", "ln0_rstd", "xn_made"))
    xnT_done, xnT_out, xnT_low = sem("xnT_done"), sem("xnT_out"), sem("xnT_low")
    q_done, q_act, q_dve = sem("q_done"), sem("q_act"), sem("q_dve")
    kv_done, k_out, v_out = sem("kv_done"), sem("k_out"), sem("v_out")
    vt_done, vt_out = sem("vt_done"), sem("vt_out")
    s_done, s_max, s_sub, s_exp, s_sum, s_inv, s_prob = (
        sem(n) for n in ("s_done", "s_max", "s_sub", "s_exp", "s_sum", "s_inv", "s_prob"))
    pt_done, pt_out, o_done, o_high, o_out = sem("pt_done"), sem("pt_out"), sem("o_done"), sem("o_high"), sem("o_out")
    wo_done, h1_made = sem("wo_done"), sem("h1_made")
    ln1_stat, ln1_var, ln1_eps, ln1_rstd, xn1_made = (
        sem(n) for n in ("ln1_stat", "ln1_var", "ln1_eps", "ln1_rstd", "xn1_made"))
    res_made, res_stored = sem("res_made"), sem("res_stored")
    xn1T_done, xn1T_out = sem("xn1T_done"), sem("xn1T_out")
    lg_done, lg_max, lg_sub, lg_exp, lg_sum, lg_inv, lg_out, lg_kept = (
        sem(n) for n in ("lg_done", "lg_max", "lg_sub", "lg_exp", "lg_sum", "lg_inv", "lg_out", "lg_kept"))
    ln2_stat, ln2_var, ln2_eps, ln2_rstd, yn_made, ym_made, y_made, y_stored = (
        sem(n) for n in ("ln2_stat", "ln2_var", "ln2_eps", "ln2_rstd", "yn_made", "ym_made", "y_made", "y_stored"))

    x_rows = x.rearrange("b c (t y) w -> (b c t) (y w)", t=NPH)
    assert NPH == 6

    def sort_pixels(eng, copy, j, n, nth, par):
        loads = nth + (3 if isinstance(n, int) and n == NG - 1 else 1)
        eng.wait_ge(x_here[par], 16 * loads)
        wait_alone(eng, const, xt_done, 3 * n)
        cols = slice(2 * j, 2 * j + 2)
        src = x_in[par][:, :].rearrange("p (y w u) -> p w y u", y=PATCH, w=NPH)[:, cols, :, :]
        copy(x_pat[:, cols, :].rearrange("p w (y u) -> p w y u", y=PATCH), src).then_inc(x_sorted[j], 1)

    acc_t = acc_rows.rearrange("(t p) d -> p t d", p=R)
    y_t = y_rows.rearrange("(t p) d -> p t d", p=R)

    def steps(eng, step):
        step(eng, -1, -1, 1, attend=False, front=True, tail=False)
        step(eng, 0, 0, 0, attend=True, front=True, tail=False)
        step(eng, 1, 0, 1, attend=True, front=True, tail=True)
        with eng.Fori(1, NG // 2 - 1) as i:
            step(eng, 2 * i, i, 0, attend=True, front=True, tail=True)
            step(eng, 2 * i + 1, i, 1, attend=True, front=True, tail=True)
        step(eng, NG - 3, NG // 2 - 1, 0, attend=True, front=True, tail=True)
        step(eng, NG - 2, NG // 2 - 1, 1, attend=True, front=True, tail=True)
        step(eng, NG - 1, NG // 2, 0, attend=True, front=False, tail=True)
        step(eng, NG, NG // 2, 1, attend=False, front=False, tail=True)

    def there(n):
        return not isinstance(n, int) or n < NG

    with nc.Block() as block:

        @block.sync
        def _(sp):
            def load(signal, *pairs):
                for dst, src in pairs:
                    sp.dma_start(dst, src).then_inc(signal, 16)

            def images(g, parity):
                real = min(IPG, NB - IPG * g) if isinstance(g, int) else IPG
                rows = real * IROWS
                sp.dma_start(x_in[parity][0:rows, :], x_rows[bass.ds(XR * g, rows), :]).then_inc(x_here[parity], 16)
                for b in range(real, IPG):
                    sp.dma_start(x_in[parity][b * IROWS:(b + 1) * IROWS, :],
                                 x_rows[(NB - 1) * IROWS:NB * IROWS, :]).then_inc(x_here[parity], 16)

            row = lambda v: v.rearrange("(a d) -> a d", a=1).broadcast_to([R, D])
            column = lambda v: v.rearrange("(p a) -> p a", a=1)
            slices = lambda w: w.rearrange("(a p) n -> p a n", p=P)
            load(rows_in, (w_rows, slices(tok_W)), (gate_rows[:, :], gate_w),
                 (bq_rows[:, :], bq.rearrange("(j p) -> j p", p=P)))
            images(0, 0)
            load(base_in, (base[:, :], row(tok_b)))
            load(w_q_here, (w_q_in, slices(Wq)))
            load(w_kv_here, *((w_kv_in[:, n, :, e, :], slices(w)) for n, w in enumerate((Wk, Wv)) for e in range(2)))
            load(early_in, *((pos[i * S:(i + 1) * S, :], pos_embed[0]) for i in range(IPT)),
                 *((b[e * DK:(e + 1) * DK, :], column(v)) for b, v in ((b_k2, bk), (b_v2, bv)) for e in range(2)))
            sp.wait_ge(base_in, 16)
            load(cls_in, *((base[i * S:i * S + 1, :], cls_token[0]) for i in range(IPT)))
            load(w_o_here, (w_o_in, slices(Wo)))
            images(1, 1)
            load(late_in, (b_o[:, :], row(bo)), (lnw[:, :], row(ln_w)), (lnb[:, :], row(ln_b)))

            def store(g):
                sp.wait_ge(res_made, g + 1)
                sp.dma_start(acc_t[:, bass.ds(2 * g, 2), :], res[:, :, :]).then_inc(res_stored, 16)
                sp.wait_ge(y_made, g + 1)
                sp.wait_ge(lg_out, g + 1)
                sp.dma_start(y_t[:, bass.ds(2 * g, 2), :], yo[:, :, :]).then_inc(y_stored, 16)

            def x_free(g):
                for j in range(3):
                    sp.wait_ge(x_sorted[j], g + 1)

            for g in range(2):
                x_free(g)
                images(g + 2, g)
            with sp.Fori(1, NG // 2 - 1) as i:
                for u in range(2):
                    x_free(2 * i + u)
                    images(2 * i + u + 2, u)
                    store(2 * i + u - 2)
            x_free(NG - 3)
            images(NG - 1, 0)
            for g in range(NG - 5, NG):
                store(g)
            sp.wait_ge(res_stored, 16 * NG)
            sp.wait_ge(y_stored, 16 * NG)

        @block.tensor
        def _(pe):
            pe.wait_ge(rows_in, 16 * 3)
            for k in range(0, KP, 2):
                for kk in (k, k + 1):
                    for a in range(2):
                        mm = nc.tensor.transpose(ring[k // 2][:, (kk - k) * D + a * P:(kk - k) * D + (a + 1) * P],
                                                 w_rows[:, a, kk * P:(kk + 1) * P], const.ident[:, :])
                mm.then_inc(wT_done, 1)
            for a in range(2):
                mm = nc.tensor.transpose(pS[0][:, a * NE:(a + 1) * NE], gate_rows[:, a * P:(a + 1) * P],
                                         const.ident[0:NE, 0:NE])
            mm = nc.tensor.transpose(pS[0][:, 2 * NE:2 * NE + NPAIR], bq_rows[:, :], const.ident[0:NPAIR, 0:NPAIR])
            mm.then_inc(wT_done, 1)
            pe.wait_ge(wT_out, 5)
            pe.wait_ge(cleared, 1)
            pe.wait_ge(w_tok_low, 1)

            def step(pe, g, half, par, attend, front, tail):
                f, t = g + 1, g - 1

                def patch_transposes(j):
                    wait_alone(pe, const, x_sorted[j], f + 1)
                    for q in range(4):
                        half, w = divmod(q, 2)
                        mm = nc.tensor.transpose(ring[j][:, q * XR:(q + 1) * XR],
                                                 x_pat[:, 2 * j + w, half * P:(half + 1) * P], const.ident[0:XR, 0:XR])
                    mm.then_inc(xt_done, 1)

                def scores_of(j):
                    if not isinstance(g, int) or g > 0:
                        pe.wait_ge(s_sub, 3 * g + j - 2)
                    for b in (2 * j, 2 * j + 1):
                        for c in range(NCH):
                            pair = min(NCH * c, NPAIR - NCH)
                            o = ((b % 2) * NCH + c) * 2 * S
                            mm = nc.tensor.matmul(
                                pS[j][0:R, o:o + R],
                                QT[par][:, b, pair:pair + NCH, :].rearrange("p j s -> p (j s)"),
                                Kbd[par][:, b:b + 2, :, :].rearrange("p b e s -> p (b e s)")[:, 0:R],
                                start=True, stop=True)
                    mm.then_inc(s_done, 1)

                def prob_transposes(b):
                    if b % 2 == 0:
                        pe.wait_ge(s_prob, 3 * g + b // 2 + 1)
                    pe.wait_ge(pt_out, 6 * g + b)
                    for c in range(NCH):
                        pair = min(NCH * c, NPAIR - NCH)
                        o = ((b % 2) * NCH + c) * 2 * S
                        mm = nc.tensor.transpose(pPT[0:2 * S, pair * S:pair * S + R], prob[:, b // 2, o:o + 2 * S],
                                                 const.ident[0:R, 0:R])
                    mm.then_inc(pt_done, 1)

                def values_of(b):
                    pe.wait_ge(pt_out, 6 * g + b + 1)
                    pe.wait_ge(o_out, 6 * g + b)
                    nc.tensor.matmul(pO[:, 0:NPAIR * S], Vbd[par][:, b, :], PT[b % 2][:, :],
                                     start=True, stop=True).then_inc(o_done, 1)

                def q_pairs(j):
                    bank = Q_BANK[j]
                    for m in (2 * j, 2 * j + 1):
                        mm = split_product(nc, ring[bank][:, (m % 2) * GT:(m % 2 + 1) * GT],
                                           [([w[:, k, m * P:(m + 1) * P] for w in w_q], [v[:, k, :] for v in xnT])
                                            for k in range(2)],
                                           {(2, 0): lambda: pe.wait_ge(xnT_low, f + 1)} if m == 0 else {})
                    mm.then_inc(q_done, 1)

                if front:
                    pe.wait_ge(vt_out, 2 * f)
                    patch_transposes(0)
                    patch_transposes(1)
                if attend:
                    pe.wait_ge(q_act, 3 * (g + 1))
                    pe.wait_ge(q_dve, g + 1)
                    pe.wait_ge(k_out, 2 * (g + 1))
                    scores_of(0)
                if front:
                    if attend:
                        pe.wait_ge(h1_made, g)
                    patch_transposes(2)
                if attend:
                    scores_of(1)
                    scores_of(2)
                if front:
                    pe.wait_ge(xt_out, 3 * (f + 1))
                    pe.wait_ge(xt_low, 3 * f + 1)
                    for tile in range(2):
                        cols = slice(tile * R, (tile + 1) * R)
                        waits = {(2, 0): lambda: pe.wait_ge(xt_low, 3 * (f + 1))} if tile == 0 else {}
                        mm = split_product(nc, ring[0][0:R, tile * D:(tile + 1) * D],
                                           [([v[:, k, cols] for v in patT], [w[:, k, :] for w in w_tok])
                                            for k in range(KP)], waits, last=(1, 0))
                    mm.then_inc(emb_done, 1)
                if attend:
                    prob_transposes(0)
                if tail:
                    if not front:
                        pe.wait_ge(vt_out, 2 * NG)
                        pe.wait_ge(h1_made, min(g, NG))
                    pe.wait_ge(xn1_made, 2 * (t + 1))
                    for tile in range(2):
                        for k in range(2):
                            mm = nc.tensor.transpose(ring[1][:, k * GT + tile * R:k * GT + (tile + 1) * R],
                                                     xn1[:, tile, k * P:(k + 1) * P], const.ident[0:R, 0:R])
                    mm.then_inc(xn1T_done, 1)
                if attend:
                    prob_transposes(1)
                    values_of(0)
                if tail:
                    pe.wait_ge(xn1T_out, t + 1)
                    for tile in range(2):
                        for k in range(2):
                            mm = nc.tensor.matmul(ring[2][0:R, tile * P:(tile + 1) * P],
                                                  xn1T[:, k, tile * R:(tile + 1) * R], w_gate[:, k, :],
                                                  start=(k == 0), stop=(k == 1))
                    mm.then_inc(lg_done, 1)
                if attend:
                    prob_transposes(2)
                    values_of(1)
                if front:
                    pe.wait_ge(emb_out, f + 1)
                    pe.wait_ge(xn_made, 2 * (f + 1))
                    for tile in range(2):
                        for k in range(2):
                            mm = nc.tensor.transpose(ring[0][:, k * GT + tile * R:k * GT + (tile + 1) * R],
                                                     xn[:, tile, k * P:(k + 1) * P], const.ident[0:R, 0:R])
                    mm.then_inc(xnT_done, 1)
                if attend:
                    prob_transposes(3)
                    values_of(2)
                if front:
                    pe.wait_ge(xnT_out, f + 1)
                    if not attend:
                        pe.wait_ge(w_in_low, 2)
                    if tail:
                        pe.wait_ge(xn1T_out, t + 1)
                    q_pairs(0)
                    if tail:
                        pe.wait_ge(lg_sub, t + 1)
                    q_pairs(1)
                if attend:
                    values_of(3)
                    prob_transposes(4)
                if front:
                    q_pairs(2)
                    pe.wait_ge(q_act, 3 * f + 1)
                    for n in range(2):
                        mm = split_product(nc, ring[KV_BANK][:, n * GT:(n + 1) * GT],
                                           [([w[:, n, k, :, :].rearrange("p a b -> p (a b)") for w in w_kv],
                                             [v[:, k, :] for v in xnT]) for k in range(2)])
                    mm.then_inc(kv_done, 1)
                if attend:
                    values_of(4)
                    prob_transposes(5)
                if front:
                    pe.wait_ge(q_dve, f + 1)
                    q_pairs(3)
                if attend:
                    values_of(5)
                if front:
                    pe.wait_ge(v_out, f + 1)
                    pe.wait_ge(q_act, 3 * f + 2)
                    for b in range(4):
                        mm = nc.tensor.transpose(ring[0][0:2 * S, b * P:(b + 1) * P],
                                                 VT[:, b, :, :].rearrange("p e s -> p (e s)"), const.ident[:, :])
                    mm.then_inc(vt_done, 1)
                    pe.wait_ge(k_out, 2 * (f + 1))
                    for b in range(4, IPG):
                        mm = nc.tensor.transpose(ring[1][0:2 * S, (b - 4) * P:(b - 3) * P],
                                                 VT[:, b, :, :].rearrange("p e s -> p (e s)"), const.ident[:, :])
                    mm.then_inc(vt_done, 1)
                if attend:
                    if front:
                        pe.wait_ge(q_act, 3 * f + 3)
                    elif tail:
                        pe.wait_ge(lg_sub, t + 1)
                    pe.wait_ge(o_out, 6 * (g + 1))
                    if not tail:
                        pe.wait_ge(w_o_low, 1)
                    for tile in range(2):
                        cols = slice(tile * R, (tile + 1) * R)
                        mm = split_product(nc, ring[2][0:R, tile * D:(tile + 1) * D],
                                           [([v[:, j, cols] for v in OT], [w[:, j, :] for w in w_o])
                                            for j in range(NPAIR)])
                    mm.then_inc(wo_done, 1)

            steps(pe, step)

        @block.scalar
        def _(act):
            for j in range(3):
                act.wait_ge(wT_done, j + 1)
                nc.scalar.activation(w_tok[0][:, 2 * j:2 * j + 2, :].rearrange("p k e -> p (k e)"), ring[j][:, :],
                                     ACT.Copy).then_inc(wT_out, 1)
            act.wait_ge(wT_done, 4)
            act.wait_ge(cleared, 1)
            nc.scalar.activation(w_gate[:, :, 0:NE], pS[0][:, 0:2 * NE].rearrange("p (k e) -> p k e", k=2),
                                 ACT.Copy).then_inc(wT_out, 1)
            nc.scalar.activation(b_q[:, :], pS[0][:, 2 * NE:2 * NE + NPAIR], ACT.Copy).then_inc(wT_out, 1)
            act.wait_ge(wT_out, 5)

            def step(act, g, half, par, attend, front, tail):
                f, fp, t = g + 1, 1 - par, g - 1

                def exp_of(j):
                    act.wait_ge(s_sub, 3 * g + j + 1)
                    nc.scalar.activation(prob[:, j, :], prob[:, j, :], ACT.Exp, scale=SCALE0).then_inc(s_exp, 1)

                def patch_out(j):
                    act.wait_ge(xt_done, 3 * f + j + 1)
                    act.wait_ge(emb_done, f)
                    for q in range(4):
                        last = nc.scalar.activation(patch_slots(patT[0], j, q), patch_columns(ring[j], q), ACT.Copy)
                    last.then_inc(xt_out, 1)

                def q_out(j):
                    act.wait_ge(q_done, 4 * f + j + 1)
                    for m in range(2):
                        last = nc.scalar.activation(QT[fp][:, :, 2 * j + m, :], q_columns(ring[Q_BANK[j]], m),
                                                    ACT.Identity, bias=b_q[:, 2 * j + m:2 * j + m + 1])
                    last.then_inc(q_act, 1)

                def pt_copy(b):
                    act.wait_ge(pt_done, 6 * g + b + 1)
                    act.wait_ge(o_done, 6 * g + max(b - 1, 0))
                    nc.scalar.activation(PT[b % 2][:, :], pPT[0:2 * S, 0:NPAIR * S], ACT.Copy).then_inc(pt_out, 1)

                if front:
                    patch_out(0)
                    patch_out(1)
                if attend:
                    exp_of(0)
                if front:
                    patch_out(2)
                if attend:
                    exp_of(1)
                    exp_of(2)
                if attend:
                    pt_copy(0)
                if tail:
                    act.wait_ge(xn1T_done, t + 1)
                    nc.scalar.activation(xn1T[:, :, :].rearrange("p k t -> p (k t)"), ring[1][:, 0:2 * GT],
                                         ACT.Copy).then_inc(xn1T_out, 1)
                if attend:
                    pt_copy(1)
                    pt_copy(2)
                if tail:
                    act.wait_ge(lg_sub, t + 1)
                    nc.scalar.activation(lexp[:, :, :], lexp[:, :, :], ACT.Exp).then_inc(lg_exp, 1)
                if front:
                    act.wait_ge(xnT_done, f + 1)
                    act.wait_ge(q_done, 4 * f)
                    nc.scalar.activation(xnT[0][:, :, :].rearrange("p k t -> p (k t)"), ring[0][:, 0:2 * GT],
                                         ACT.Copy).then_inc(xnT_out, 1)
                if attend:
                    pt_copy(3)
                if front:
                    q_out(0)
                if attend:
                    pt_copy(4)
                if front:
                    q_out(2)
                    act.wait_ge(kv_done, f + 1)
                    v = ring[KV_BANK][:, GT:2 * GT].rearrange("p (b s) -> p b s", s=S)
                    nc.scalar.activation(VT[:, :, :, :], v.unsqueeze(2).broadcast_to([P, IPG, 2, S]), ACT.Identity,
                                         bias=b_v2[:, 0:1]).then_inc(v_out, 1)
                if attend:
                    pt_copy(5)
                if front:
                    q_out(3)
                if not attend and front:
                    act.wait_ge(w_o_here, 16)
                    nc.scalar.activation(w_o[0].ap(), w_o_in, ACT.Copy).then_inc(w_o_high, 1)
                if front and there(g + 2):
                    sort_pixels(act, lambda o, i: nc.scalar.activation(o, i, ACT.Copy), 0, g + 2, half + 1, par)

            sort_pixels(act, lambda o, i: nc.scalar.activation(o, i, ACT.Copy), 0, 0, 0, 0)
            for parts, whole, here, loads in ((w_q, w_q_in, w_q_here, 1), (w_kv, w_kv_in, w_kv_here, 4)):
                act.wait_ge(here, 16 * loads)
                nc.scalar.activation(parts[0].ap(), whole, ACT.Copy).then_inc(w_in_high, 1)
            act.wait_ge(early_in, 16 * (IPT + 4))
            steps(act, step)

        @block.gpsimd
        def _(pool):
            nc.gpsimd.memset(w_gate[:, :, :], 0.0)
            for i in range(2):
                nc.gpsimd.memset(Kbd[i][:, :, :, :], 0.0)
            for b in range(IPG):
                for v in patT:
                    nc.gpsimd.memset(v[:, :, b * S:b * S + 1].bitcast(F32), 0.0)
            nc.gpsimd.memset(ones_s[:, :], 1.0).then_inc(cleared, 1)
            pool.wait_ge(cleared, 1)
            nc.gpsimd.affine_select(out=vmask[:, 0:DK], in_=ones_s[:, 0:DK], compare_op=ALU.is_gt, fill=0.0,
                                    base=S, pattern=[[0, DK]], channel_multiplier=-1)
            nc.gpsimd.affine_select(out=vmask[:, DK:P], in_=ones_s[:, DK:P], compare_op=ALU.is_ge, fill=0.0,
                                    base=-S, pattern=[[0, DK]], channel_multiplier=1).then_inc(masked, 1)
            pool.wait_ge(early_in, 16 * (IPT + 4))
            pool.wait_ge(cls_in, 16 * IPT)
            nc.gpsimd.tensor_tensor(table[:, :], base[:, :], pos[:, :], ALU.add).then_inc(table_made, 1)
            pool.wait_ge(late_in, 16 * 3)

            def rstd_of(mv, ve, rstd, stat, eps, done, n):
                wait_alone(pool, const, stat, 2 * (n + 1))
                nc.gpsimd.tensor_scalar(ve[:, :], mv[:, :, 1], LN_EPS, None, ALU.add).then_inc(eps, 1)
                pool.wait_ge(eps, n + 1)
                nc.gpsimd.tensor_tensor(rstd[:, :], ve[:, :], const.neg_half[0:R, :], ALU.pow).then_inc(done, 1)

            def step(pool, g, half, par, attend, front, tail):
                f, fp, t = g + 1, 1 - par, g - 1
                if tail:
                    rstd_of(mv1, ve1, rstd1, ln1_var, ln1_eps, ln1_rstd, t)

                def scale(j):
                    pool.wait_ge(s_inv, 3 * g + j + 1)
                    pool.wait_ge(s_exp, 3 * g + j + 1)
                    v = prob[:, j, :].rearrange("p (n s) -> p n s", s=S)
                    nc.gpsimd.tensor_tensor(v, v, spread(sinv[:, j, :], S), ALU.mult).then_inc(s_prob, 1)

                if attend:
                    scale(0)
                    scale(1)
                if front:
                    rstd_of(mv0, ve0, rstd0, ln0_var, ln0_eps, ln0_rstd, f)
                if attend:
                    scale(2)
                if tail:
                    rstd_of(mv2, ve2, rstd2, ln2_var, ln2_eps, ln2_rstd, t)
                    pool.wait_ge(xn1_made, 2 * (t + 1))
                    pool.wait_ge(res_stored, 16 * t)
                    nc.gpsimd.tensor_tensor(res[:, :, :], h1[fp][:, :, :], xn1[:, :, :],
                                            ALU.add).then_inc(res_made, 1)
                if front:
                    pool.wait_ge(emb_out, f + 1)
                    nc.gpsimd.tensor_tensor(h0b[fp][:, :, :], h0[:, :, :], both(b_o[:, :]),
                                            ALU.add).then_inc(h0b_made, 1)
                if tail:
                    pool.wait_ge(yn_made, 2 * (t + 1))
                    nc.gpsimd.tensor_tensor(ym[:, :, :], yn[:, :, :], both(lnw[:, :]), ALU.mult).then_inc(ym_made, 1)
                    pool.wait_ge(ym_made, t + 1)
                    pool.wait_ge(y_stored, 16 * t)
                    nc.gpsimd.tensor_tensor(yo[:, :, 0:D], ym[:, :, :], both(lnb[:, :]), ALU.add).then_inc(y_made, 1)

            steps(pool, step)

        @block.vector
        def _(dve):
            def norm_stats(src, stats, mv, stat, var, n):
                for tile in range(2):
                    nc.vector.bn_stats(stats[:, tile, :], src[:, tile, :]).then_inc(stat, 1)
                for tile in range(2):
                    wait_alone(dve, const, stat, 2 * n + tile + 1)
                    nc.vector.bn_aggr(mv[:, tile, :], stats[:, tile, :]).then_inc(var, 1)

            def normalise(dst, src, mv, rstd, rstd_made, made, n):
                dve.wait_ge(rstd_made, n + 1)
                for tile in range(2):
                    nc.vector.tensor_scalar(dst[:, tile, :], src[:, tile, :], mv[:, tile, 0:1], rstd[:, tile:tile + 1],
                                            ALU.subtract, ALU.mult).then_inc(made, 1)

            dve.wait_ge(masked, 1)
            dve.wait_ge(wT_out, 5)
            for j in range(KP // 2):
                high, low = (w[:, 2 * j:2 * j + 2, :].rearrange("p k e -> p (k e)") for w in w_tok)
                last = nc.vector.tensor_tensor(low, ring[j][:, :], high, ALU.subtract)
            last.then_inc(w_tok_low, 1)

            def step(dve, g, half, par, attend, front, tail):
                f, fp, t = g + 1, 1 - par, g - 1

                def patch_low(j):
                    dve.wait_ge(xt_out, 3 * f + j + 1)
                    dve.wait_ge(emb_done, f)
                    for q in range(4):
                        low, high = (patch_slots(v, j, q) for v in (patT[1], patT[0]))
                        last = nc.vector.tensor_tensor(low, patch_columns(ring[j], q), high, ALU.subtract)
                    last.then_inc(xt_low, 1)

                def shift(j):
                    dve.wait_ge(s_done, 3 * g + j + 1)
                    if j == 0:
                        dve.wait_ge(pt_done, 6 * g)
                    v = pS[j][0:R, 0:W3].rearrange("p (n s) -> p n s", s=S)
                    nc.vector.tensor_reduce(smax[:, j, :], v, AX_X, ALU.max).then_inc(s_max, 1)
                    dve.wait_ge(s_max, 3 * g + j + 1)
                    nc.vector.tensor_tensor(prob[:, j, :].rearrange("p (n s) -> p n s", s=S), v,
                                            spread(smax[:, j, :], S), ALU.subtract).then_inc(s_sub, 1)

                def inverse(j):
                    dve.wait_ge(s_exp, 3 * g + j + 1)
                    if j == 0:
                        dve.wait_ge(s_prob, 3 * g)
                    v = prob[:, j, :].rearrange("p (n s) -> p n s", s=S)
                    nc.vector.tensor_reduce(ssum[:, j, :], v, AX_X, ALU.add).then_inc(s_sum, 1)
                    dve.wait_ge(s_sum, 3 * g + j + 1)
                    nc.vector.reciprocal(sinv[:, j, :], ssum[:, j, :]).then_inc(s_inv, 1)

                def o_copy(b):
                    dve.wait_ge(o_done, 6 * g + b + 1)
                    if b == 0:
                        dve.wait_ge(wo_done, g)
                    high, low = (v[:, :, b * S:(b + 1) * S] for v in OT)
                    o = pO[:, 0:NPAIR * S].rearrange("p (j s) -> p j s", s=S)
                    nc.vector.tensor_copy(high, o).then_inc(o_high, 1)
                    dve.wait_ge(o_high, 6 * g + b + 1)
                    nc.vector.tensor_tensor(low, o, high, ALU.subtract).then_inc(o_out, 1)

                def q_out(j):
                    dve.wait_ge(q_done, 4 * f + j + 1)
                    for m in range(2):
                        last = nc.vector.tensor_scalar(QT[fp][:, :, 2 * j + m, :], q_columns(ring[Q_BANK[j]], m),
                                                       b_q[:, 2 * j + m:2 * j + m + 1], None, ALU.add)
                    last.then_inc(q_dve, 1)

                if front:
                    patch_low(0)
                    patch_low(1)
                if attend:
                    for j in range(3):
                        shift(j)
                if front:
                    patch_low(2)
                if tail:
                    dve.wait_ge(h1_made, t + 1)
                    norm_stats(h1[fp], stats1, mv1, ln1_stat, ln1_var, t)
                if attend:
                    inverse(0)
                    inverse(1)
                if tail:
                    dve.wait_ge(xn1T_done, t)
                    dve.wait_ge(res_made, t)
                    normalise(xn1, h1[fp], mv1, rstd1, ln1_rstd, xn1_made, t)
                if front:
                    dve.wait_ge(emb_done, f + 1)
                    if not attend:
                        dve.wait_ge(table_made, 1)
                    dve.wait_ge(h0b_made, f)
                    nc.vector.tensor_tensor(h0[:, :, :], ring[0][0:R, :].rearrange("p (t d) -> p t d", t=2),
                                            both(table[:, :]), ALU.add).then_inc(emb_out, 1)
                    dve.wait_ge(emb_out, f + 1)
                    norm_stats(h0, stats0, mv0, ln0_stat, ln0_var, f)
                if attend:
                    o_copy(0)
                if front:
                    dve.wait_ge(xnT_done, f)
                    normalise(xn, h0, mv0, rstd0, ln0_rstd, xn_made, f)
                if tail:
                    dve.wait_ge(lg_done, t + 1)
                    dve.wait_ge(lg_exp, t)
                    lv = ring[2][0:R, 0:2 * P].rearrange("p (t e) -> p t e", t=2)[:, :, 0:NE]
                    nc.vector.tensor_reduce(lmax[:, :], lv, AX_X, ALU.max).then_inc(lg_max, 1)
                    dve.wait_ge(lg_max, t + 1)
                    nc.vector.tensor_tensor(lexp[:, :, :], lv, spread(lmax[:, :], NE),
                                            ALU.subtract).then_inc(lg_sub, 1)
                if attend:
                    o_copy(1)
                if front:
                    dve.wait_ge(xnT_out, f + 1)
                    dve.wait_ge(kv_done, f)
                    high, low = (v[:, :, :].rearrange("p k t -> p (k t)") for v in xnT)
                    nc.vector.tensor_tensor(low, ring[0][:, 0:2 * GT], high, ALU.subtract).then_inc(xnT_low, 1)
                if attend:
                    inverse(2)
                if tail:
                    dve.wait_ge(xn1_made, 2 * (t + 1))
                    norm_stats(xn1, stats2, mv2, ln2_stat, ln2_var, t)
                if attend:
                    o_copy(2)
                if front and there(g + 2):
                    for j in (1, 2):
                        sort_pixels(dve, nc.vector.tensor_copy, j, g + 2, half + 1, par)
                if front:
                    q_out(1)
                if attend:
                    o_copy(3)
                    o_copy(4)
                if front:
                    dve.wait_ge(v_out, f + 1)
                    for e in range(2):
                        rows = slice(e * DK, (e + 1) * DK)
                        nc.vector.tensor_scalar(Kbd[fp][rows, 0:IPG, e, :],
                                                ring[KV_BANK][rows, 0:GT].rearrange("p (b s) -> p b s", s=S),
                                                b_k2[rows, 0:1], None, ALU.add).then_inc(k_out, 1)
                if attend:
                    o_copy(5)
                if tail:
                    dve.wait_ge(ym_made, t)
                    normalise(yn, xn1, mv2, rstd2, ln2_rstd, yn_made, t)
                    dve.wait_ge(lg_exp, t + 1)
                    nc.vector.tensor_reduce(lsum[:, :], lexp[:, :, :], AX_X, ALU.add).then_inc(lg_sum, 1)
                    dve.wait_ge(lg_sum, t + 1)
                    nc.vector.reciprocal(linv[:, :], lsum[:, :]).then_inc(lg_inv, 1)
                    dve.wait_ge(lg_inv, t + 1)
                    dve.wait_ge(y_stored, 16 * t)
                    nc.vector.tensor_tensor(yo[:, :, D:YW], lexp[:, :, :], spread(linv[:, :], NE),
                                            ALU.mult).then_inc(lg_out, 1)
                    nc.vector.tensor_tensor(scores[0:R, bass.ds(2 * t, 2), :], lexp[:, :, :], spread(linv[:, :], NE),
                                            ALU.mult).then_inc(lg_kept, 1)
                    dve.wait_ge(lg_kept, t + 1)
                if front:
                    for n, (b0, b1) in enumerate(((0, 4), (4, IPG))):
                        dve.wait_ge(vt_done, 2 * f + n + 1)
                        nc.vector.tensor_tensor(Vbd[fp][:, b0:b1, :],
                                                ring[n][0:2 * S, 0:(b1 - b0) * P].rearrange("p (b d) -> p b d", d=P),
                                                every(vmask[:, :], b1 - b0), ALU.mult).then_inc(vt_out, 1)
                if not attend and front:
                    dve.wait_ge(w_o_high, 1)
                    nc.vector.tensor_tensor(w_o[1].ap(), w_o_in, w_o[0].ap(), ALU.subtract).then_inc(w_o_low, 1)
                if attend:
                    dve.wait_ge(wo_done, g + 1)
                    dve.wait_ge(h0b_made, g + 1)
                    nc.vector.tensor_tensor(h1[par][:, :, :], ring[2][0:R, :].rearrange("p (t d) -> p t d", t=2),
                                            h0b[par][:, :, :], ALU.add).then_inc(h1_made, 1)

            for j in (1, 2):
                sort_pixels(dve, nc.vector.tensor_copy, j, 0, 0, 0)
            for n, (parts, whole) in enumerate(((w_q, w_q_in), (w_kv, w_kv_in))):
                dve.wait_ge(w_in_high, n + 1)
                nc.vector.tensor_tensor(parts[1].ap(), whole, parts[0].ap(), ALU.subtract).then_inc(w_in_low, 1)
            dve.wait_ge(early_in, 16 * (IPT + 4))
            steps(dve, step)


def expert_choice(nc, ctx, const, ready, scores, fc1s, b1s, fc2s, b2s, acc_rows, y_rows):
    sb = lambda n, s, d=F32: ctx.enter_context(nc.sbuf_tensor(n, s, d))
    sem = lambda n: semaphore(nc, const, "c_" + n)
    ps = lambda n, d=F32: ctx.enter_context(nc.psum_tensor(n, [P, 512], d))
    NF = 8
    F = NF * P
    NST = -(-CAP // P)
    LAST = CAP - (NST - 1) * P
    rows_in = [P] * (NST - 1) + [LAST]
    FAR = 4095.0
    ROUNDS = 15
    NCAND = 3

    valid = sb("valid", [R, NT])
    valid1 = sb("valid1", [R, NT])
    sc = sb("sc", [R, NE, NT])
    cur = sb("cur", [R, NE])
    bits = sb("bits", [R, NCAND, NE], I32)
    cand = sb("cand", [R, NCAND, NE])
    over = sb("over", [R, NCAND * NE, NT], BF16)
    cnt = sb("cnt", [R, NCAND * NE], BF16)
    kept = sb("kept", [R, NCAND, NE])
    most = sb("most", [R, NE])
    ones_b = sb("ones_b", [R, P], BF16)
    tri = sb("tri", [R, R], BF16)
    sel = sb("sel", [R, 2, NE, NT], BF16)
    reset = sb("reset", [R, 2 * NE * NT])
    incl = sb("incl", [R, 2, NE, NT])
    excl = sb("excl", [R, 2, NE, NT])
    posn = sb("posn", [R, 2, NE, NT])
    slot_g = sb("slot_g", [R, NE, NT])
    slot_q = sb("slot_q", [R, NE, NT])
    slot_e = sb("slot_e", [R, NE, NT])
    slot = sb("slot", [R, NE, NT], I32)
    hi_i = sb("hi_i", [R, NE, NT], I32)
    lo_i = sb("lo_i", [R, NE, NT], I32)
    hi = sb("hi", [R, NE * NT])
    lo = sb("lo", [R, NE, NT])
    iota_s = sb("iota_s", [R, P], BF16)
    iota_j = sb("iota_j", [R, NST], F32)
    tile_no = sb("tile_no", [R, NE, NT], F32)
    row_no = sb("row_no", [R, 1], F32)
    in_tile = sb("in_tile", [R, NE * NT, NST], F32)
    marks = sb("marks", [R, NE, NT, 2, NST], BF16)
    hot = sb("hot", [R, NT, P], BF16)
    tile_rows = sb("tile_rows", [P, NST])
    to_gather = [sb(f"to_gather{i}", [P, NST], I32) for i in range(2)]
    to_scatter = [sb(f"to_scatter{i}", [P, NST], I32) for i in range(2)]

    fc1_rows = [sb(f"fc1_rows{i}", [P, NF, D]) for i in range(2)]
    fc2_rows = [sb(f"fc2_rows{i}", [P, 2, F]) for i in range(2)]
    two = lambda n, s: [sb(f"{n}_{part}", s, F32R) for part in ("high", "low")]
    fc1T = [two(f"fc1T{i}", [P, 2, F]) for i in range(2)]
    fc2T = [two(f"fc2T{i}", [P, NF, D]) for i in range(2)]
    w_whole = [sb(f"w_whole{i}", [P, 4 * P]) for i in range(2)]
    b1_rows = sb("b1_rows", [NE, F])
    b1T = sb("b1T", [P, NF, NE])
    b2 = [sb(f"b2_{i}", [P, D]) for i in range(2)]
    yg = [sb(f"yg{i}", [P, NST, YW]) for i in range(2)]
    yT = [two(f"yT{i}", [P, 2, CAP]) for i in range(2)]
    h_whole = [sb(f"h_whole{i}", [P, CAP]) for i in range(2)]
    hT = two("hT", [P, NF, NST * P])
    ob = sb("ob", [P, NST, D])
    ow = sb("ow", [P, NST, D])

    pW = [ps(f"c_w{i}") for i in range(2)]
    pY = [ps(f"c_y{i}") for i in range(2)]
    pH = [ps(f"c_h{i}") for i in range(2)]
    pO = [ps(f"c_o{i}") for i in range(2)]

    made, link = sem("made"), sem("link")
    counted, reduced, summed, kept_made, most_made, cur_made, bits_made, cand_made = (
        sem(n) for n in ("counted", "reduced", "summed", "kept_made", "most_made",
                         "cur_made", "bits_made", "cand_made"))
    routed = sem("routed")
    prefix_done, marks_made, hot_made, ids_done, tile_rows_made, to_gather_made, to_scatter_made = (
        sem(n) for n in ("prefix_done", "marks_made", "hot_made", "ids_done", "tile_rows_made", "to_gather_made",
                         "to_scatter_made"))
    w_here = [sem(f"w_here{i}") for i in range(2)]
    b2_here = [sem(f"b2_here{i}") for i in range(2)]
    b1_here, b1_done, b1_out = sem("b1_here"), sem("b1_done"), sem("b1_out")
    wt_done, wt_high, wt_out = sem("wt_done"), sem("wt_high"), sem("wt_out")
    w_whole_out = sem("w_whole_out")
    y_here = [sem(f"y_here{i}") for i in range(2)]
    yt_done, yt_high, yt_out = sem("yt_done"), sem("yt_high"), sem("yt_out")
    h_done, h_out, h_low = sem("h_done"), sem("h_out"), sem("h_low")
    h_high = [sem(f"h_high{i}") for i in range(2)]
    o_done, ob_made, ow_made = sem("o_done"), sem("ob_made"), sem("ow_made")
    scattered = sem("scattered")

    def steps(eng, step):
        for e in range(2):
            step(eng, e, e // 2, e % 2)
        with eng.Fori(1, NE // 2 - 1) as i:
            for par in range(2):
                step(eng, 2 * i + par, i, par)
        for e in range(NE - 2, NE):
            step(eng, e, e // 2, e % 2)

    def there(e):
        return not isinstance(e, int) or e < NE

    def weight_bank(par, n):
        if n < 4:
            return [w[:, n // 2, (n % 2) * 4 * P:(n % 2 + 1) * 4 * P] for w in fc1T[par]]
        return [w[:, 2 * (n - 4):2 * (n - 3), :].rearrange("p j d -> p (j d)") for w in fc2T[par]]

    ids = pH[1][:, CAP:CAP + 2 * NST]

    with nc.Block() as block:

        @block.sync
        def _(sp):
            fc1_d = fc1s.rearrange("e (j p) d -> e p j d", p=P)
            fc2_d = fc2s.rearrange("e (a p) f -> e p a f", p=P)

            def weights(e, par):
                sp.dma_start(fc1_rows[par][:, :, :], fc1_d[e]).then_inc(w_here[par], 16)
                sp.dma_start(fc2_rows[par][:, :, :], fc2_d[e]).then_inc(w_here[par], 16)

            def bias2(e, par):
                sp.dma_start(b2[par][:, :], b2s[bass.ds(e, 1), :].broadcast_to([P, D])).then_inc(b2_here[par], 16)

            sp.dma_start(b1_rows[:, :], b1s).then_inc(b1_here, 16)
            weights(0, 0)
            bias2(0, 0)
            sp.wait_ge(w_here[0], 32)
            weights(1, 1)
            bias2(1, 1)
            ready.load(sp)
            with sp.Fori(0, NE // 2 - 1) as i:
                for u in range(2):
                    sp.wait_ge(wt_done, NF * (2 * i + u + 1))
                    weights(2 * i + u + 2, u)
                    sp.wait_ge(ob_made, 2 * (2 * i + u + 1))
                    bias2(2 * i + u + 2, u)

        @block.gpsimd
        def _(pool):
            nc.gpsimd.memset(ones_b[:, :], 1.0)
            nc.gpsimd.memset(valid[:, :], 1.0).then_inc(made, 1)
            pool.wait_ge(made, 1)
            nc.gpsimd.affine_select(out=tri[:, :], in_=ones_b[:, 0:R], compare_op=ALU.is_gt, fill=0.0,
                                    base=0, pattern=[[1, R]], channel_multiplier=-1)
            nc.gpsimd.affine_select(out=valid[:, NT - 1:NT], in_=ones_b[:, 0:1], compare_op=ALU.is_gt, fill=0.0,
                                    base=TOK - (NT - 1) * R, pattern=[[0, 1]], channel_multiplier=-1)
            nc.gpsimd.iota(iota_s[:, :], pattern=[[1, P]], base=0, channel_multiplier=0,
                           allow_small_or_imprecise_dtypes=True)
            nc.gpsimd.iota(iota_j[:, :], pattern=[[1, NST]], base=0, channel_multiplier=0,
                           allow_small_or_imprecise_dtypes=True)
            nc.gpsimd.iota(tile_no[:, :, :], pattern=[[0, NE], [1, NT]], base=0, channel_multiplier=0,
                           allow_small_or_imprecise_dtypes=True)
            nc.gpsimd.iota(row_no[:, :], pattern=[[0, 1]], base=0, channel_multiplier=1,
                           allow_small_or_imprecise_dtypes=True).then_inc(made, 1)

            def gather(e, par):
                wait_alone(pool, const, to_gather_made, e + 1)
                for j in range(NST):
                    n = rows_in[j]
                    nc.gpsimd.indirect_dma_start(
                        out=yg[par][0:n, j, :], out_offset=None, in_=y_rows[:, :],
                        in_offset=bass.IndirectOffsetOnAxis(ap=to_gather[par][0:n, j:j + 1], axis=0)
                    ).then_inc(y_here[par], 16)

            for v in hT:
                last = nc.gpsimd.memset(v[:, :, CAP:NST * P].bitcast(F32), 0.0)
            last.then_inc(made, 1)

            ready.make_powers(pool, 0)
            for n in range(NF):
                pool.wait_ge(w_whole_out, n + 1)
                high, low = weight_bank(0, n)
                nc.gpsimd.tensor_tensor(low, w_whole[n % 2][:, :], high, ALU.subtract).then_inc(wt_out, 1)
            gather(0, 0)

            def scatter(e, par):
                wait_alone(pool, const, scattered, 16 * NST * e)
                for j in range(NST):
                    wait_alone(pool, const, ow_made, NST * e + j + 1)
                    if j == 0:
                        wait_alone(pool, const, to_scatter_made, e + 1)
                    n = rows_in[j]
                    nc.gpsimd.indirect_dma_start(
                        out=acc_rows[:, :],
                        out_offset=bass.IndirectOffsetOnAxis(ap=to_scatter[par][0:n, j:j + 1], axis=0),
                        in_=ow[0:n, j, :], in_offset=None, compute_op=ALU.add).then_inc(scattered, 16)

            def step(pool, e, half, par):
                if there(e + 1):
                    pool.wait_ge(yt_done, 2 * e)
                    wait_alone(pool, const, ow_made, NST * e)
                    gather(e + 1, 1 - par)
                if isinstance(e, int) and e == 0:
                    for head in range(1, ready.sizes[0]):
                        ready.make_powers(pool, head)
                    ready.make_decay(pool)
                if not isinstance(e, int) or e > 0:
                    scatter(e - 1, 1 - par)

            steps(pool, step)
            scatter(NE - 1, (NE - 1) % 2)
            pool.wait_ge(scattered, 16 * NST * NE)

        @block.tensor
        def _(pe):
            def weight_transposes(e, half, par, n):
                if n == 0:
                    pe.wait_ge(w_here[par], 32 * (half + 1))
                k = NF * e + n
                if not isinstance(e, int) or k >= 2:
                    pe.wait_ge(wt_out, k - 1)
                bank = pW[n % 2]
                for q in range(4):
                    if n < 4:
                        src = fc1_rows[par][:, 4 * (n % 2) + q, (n // 2) * P:(n // 2 + 1) * P]
                    else:
                        j, a = 2 * (n - 4) + q // 2, q % 2
                        src = fc2_rows[par][:, a, j * P:(j + 1) * P]
                    mm = nc.tensor.transpose(bank[:, q * P:(q + 1) * P], src, const.ident[:, :])
                mm.then_inc(wt_done, 1)

            def search_round(i):
                pe.wait_ge(reduced, i + 1)
                nc.tensor.matmul(pH[0][0:R, 0:NCAND * NE], ones_b[:, 0:R], cnt[:, :],
                                 start=True, stop=True).then_inc(summed, 1)

            pe.wait_ge(made, 2)
            with pe.Fori(0, ROUNDS - NF) as i:
                search_round(i)
            pe.wait_ge(b1_here, 16)
            for j in range(NF):
                mm = nc.tensor.transpose(pO[0][:, j * NE:(j + 1) * NE], b1_rows[:, j * P:(j + 1) * P],
                                         const.ident[0:NE, 0:NE])
            mm.then_inc(b1_done, 1)
            for n in range(NF):
                weight_transposes(0, 0, 0, n)
                search_round(ROUNDS - NF + n)
            pe.wait_ge(routed, 2)
            nc.tensor.matmul(pH[0][0:R, 0:2 * NE * NT], tri[:, :], sel[:, :, :, :].rearrange("p a e t -> p (a e t)"),
                             start=True, stop=True)
            nc.tensor.matmul(pH[1][0:R, 0:2 * NE * NT], ones_b[:, 0:R],
                             sel[:, :, :, :].rearrange("p a e t -> p (a e t)"),
                             start=True, stop=True).then_inc(prefix_done, 1)

            def find_tokens(e):
                pe.wait_ge(hot_made, e + 1)
                pe.wait_ge(to_gather_made, e)
                for t in range(NT):
                    mm = nc.tensor.matmul(ids, hot[:, t, :],
                                          marks[:, bass.ds(e, 1), t, :, :].rearrange("p a v j -> p (a v j)"),
                                          start=(t == 0), stop=(t == NT - 1))
                mm.then_inc(ids_done, 1)

            pe.wait_ge(marks_made, 1)
            for e in range(2):
                find_tokens(e)

            def row_transposes(e, half, par):
                pe.wait_ge(y_here[par], 16 * NST * (half + 1))
                pe.wait_ge(yt_out, 2 * e)
                for k in range(2):
                    for j in range(NST):
                        n = rows_in[j]
                        mm = nc.tensor.transpose(pY[k][:, j * P:j * P + n], yg[par][0:n, j, k * P:(k + 1) * P],
                                                 const.ident[0:n, 0:n])
                    mm.then_inc(yt_done, 1)

            row_transposes(0, 0, 0)
            pe.wait_ge(made, 3)

            def step(pe, e, half, par):
                def next_weights(n):
                    if there(e + 1):
                        weight_transposes(e + 1, half + par, 1 - par, n)

                pe.wait_ge(yt_out, 2 * (e + 1))
                pe.wait_ge(wt_out, NF * (e + 1))
                for j in range(NF):
                    pe.wait_ge(h_out, NF * e + max(j - 1, 0))
                    if j == 1:
                        found = min(e + 2, NE) if isinstance(e, int) else e + 2
                        pe.wait_ge(to_gather_made, found)
                    mm = split_product(nc, pH[j % 2][:, 0:CAP],
                                       [([w[:, k, j * P:(j + 1) * P] for w in fc1T[par]], [y[:, k, :] for y in yT[par]])
                                        for k in range(2)])
                    mm.then_inc(h_done, 1)
                    if j % 2 == 0:
                        next_weights(j // 2)
                next_weights(4)
                for i in range(2):
                    pe.wait_ge(h_high[i], NF // 2 * (e + 1))
                pe.wait_ge(ob_made, 2 * e)
                for j in range(NST):
                    waits = {(2, 0): lambda: pe.wait_ge(h_low, NF * (e + 1))} if j == 0 else {}
                    if j < 2:
                        waits[1, 0] = lambda: next_weights((5, 7)[j])
                    mm = split_product(nc, pO[j // 2][:, (j % 2) * D:(j % 2 + 1) * D],
                                       [([h[:, f, j * P:(j + 1) * P] for h in hT], [w[:, f, :] for w in fc2T[par]])
                                        for f in range(NF)], waits, last=(1, 0))
                    if j == 0:
                        next_weights(6)
                        if there(e + 1):
                            row_transposes(e + 1, half + par, 1 - par)
                    if j:
                        mm.then_inc(o_done, 1)
                if there(e + 2):
                    find_tokens(e + 2)

            steps(pe, step)

        @block.scalar
        def _(act):
            act.wait_ge(b1_done, 1)
            nc.scalar.activation(b1T[:, :, :].rearrange("p j e -> p (j e)"), pO[0][:, 0:NF * NE],
                                 ACT.Copy).then_inc(b1_out, 1)
            act.wait_ge(b1_out, 1)

            def weights_high(e, par, n):
                act.wait_ge(wt_done, NF * e + n + 1)
                nc.scalar.activation(weight_bank(par, n)[0], pW[n % 2][:, :], ACT.Copy).then_inc(wt_high, 1)

            for n in range(NF):
                weights_high(0, 0, n)
                if n >= 2:
                    act.wait_ge(wt_out, n - 1)
                nc.scalar.activation(w_whole[n % 2][:, :], pW[n % 2][:, :], ACT.Copy).then_inc(w_whole_out, 1)

            def step(act, e, half, par):
                for j in range(NF):
                    act.wait_ge(h_done, NF * e + j + 1)
                    if not isinstance(e, int) or e > 0 or j >= 2:
                        act.wait_ge(h_low, NF * e + j - 1)
                    nc.scalar.activation(h_whole[j % 2][:, :], pH[j % 2][:, 0:CAP], ACT.Gelu_apprx_tanh,
                                         bias=b1T[:, j, bass.ds(e, 1)]).then_inc(h_out, 1)
                    if j % 2 == 0:
                        act.wait_ge(h_out, NF * e + j + 1)
                        if j == 0:
                            act.wait_ge(o_done, 2 * e)
                        nc.scalar.activation(hT[0][:, j, 0:CAP], h_whole[0][:, :], ACT.Copy).then_inc(h_high[0], 1)
                        if there(e + 1):
                            weights_high(e + 1, 1 - par, j // 2)
                if there(e + 1):
                    for n in range(4, NF):
                        weights_high(e + 1, 1 - par, n)

            steps(act, step)

        @block.vector
        def _(dve):
            def weights_low(e, par, n):
                dve.wait_ge(wt_high, NF * e + n + 1)
                high, low = weight_bank(par, n)
                nc.vector.tensor_tensor(low, pW[n % 2][:, :], high, ALU.subtract).then_inc(wt_out, 1)

            links = [0]

            def chained(ins):
                links[0] += 1
                ins.then_inc(link, 1)
                dve.wait_ge(link, links[0])

            dve.wait_ge(made, 2)
            nc.vector.memset(cur[:, :], 0.0).then_inc(cur_made, 1)
            for k in range(NCAND):
                last = nc.vector.memset(bits[:, k, :], (k + 1) << 2 * (ROUNDS - 1))
            last.then_inc(bits_made, 1)
            nc.vector.memset(reset[:, :], 1.0)
            chained(nc.vector.tensor_scalar(valid1[:, :], valid[:, :], -1.0, None, ALU.add))
            nc.vector.memset(reset[:, :].rearrange("p (n t) -> p n t", t=NT)[:, :, 0:1], 0.0)
            chained(nc.vector.tensor_tensor(sc[:, :, :], scores[0:R, :, :].rearrange("p t e -> p e t"),
                                            every(valid[:, :], NE), ALU.mult))
            chained(nc.vector.tensor_tensor(sc[:, :, :], sc[:, :, :], every(valid1[:, :], NE), ALU.add))
            cur_i = cur[:, :].bitcast(I32)
            flat_cand = cand[:, :, :].rearrange("p c e -> p (c e)")
            with dve.Fori(0, ROUNDS) as i:
                dve.wait_ge(cur_made, i + 1)
                dve.wait_ge(bits_made, i + 1)
                nc.vector.tensor_tensor(cand[:, :, :].bitcast(I32), every(cur_i, NCAND), bits[:, :, :],
                                        ALU.bitwise_or).then_inc(cand_made, 1)
                dve.wait_ge(cand_made, i + 1)
                nc.vector.tensor_tensor(over[:, :, :].rearrange("p (c e) t -> p c e t", c=NCAND),
                                        sc[:, :, :].unsqueeze(1).broadcast_to([R, NCAND, NE, NT]),
                                        cand[:, :, :].unsqueeze(3).broadcast_to([R, NCAND, NE, NT]),
                                        ALU.is_ge).then_inc(counted, 1)
                dve.wait_ge(counted, i + 1)
                with nc.allow_low_precision("counts up to NT are exact in bfloat16"):
                    nc.vector.tensor_reduce(cnt[:, :], over[:, :, :], AX_X, ALU.add).then_inc(reduced, 1)
                nc.vector.tensor_scalar(bits[:, :, :], bits[:, :, :], 2, None,
                                        ALU.logical_shift_right).then_inc(bits_made, 1)
                dve.wait_ge(summed, i + 1)
                nc.vector.scalar_tensor_tensor(kept[:, :, :].rearrange("p c e -> p (c e)"), pH[0][0:R, 0:NCAND * NE],
                                               float(CAP), flat_cand, ALU.is_ge, ALU.mult).then_inc(kept_made, 1)
                dve.wait_ge(kept_made, i + 1)
                nc.vector.tensor_reduce(most[:, :], kept[:, :, :].rearrange("p c e -> p e c"), AX_X,
                                        ALU.max).then_inc(most_made, 1)
                dve.wait_ge(most_made, i + 1)
                nc.vector.tensor_tensor(cur[:, :], cur[:, :], most[:, :], ALU.max).then_inc(cur_made, 1)
            dve.wait_ge(cur_made, ROUNDS + 1)
            nc.vector.tensor_tensor(sel[:, 0, :, :], sc[:, :, :], spread(cur[:, :], NT),
                                    ALU.is_gt).then_inc(routed, 1)
            nc.vector.tensor_tensor(sel[:, 1, :, :], sc[:, :, :], spread(cur[:, :], NT),
                                    ALU.is_equal).then_inc(routed, 1)
            flat = lambda t: t[:, :, :, :].rearrange("p a e t -> p (a e t)")
            dve.wait_ge(prefix_done, 1)
            counts = pH[1][0:R, 0:2 * NE * NT]
            chained(nc.vector.tensor_tensor_scan(flat(incl), reset[:, :], counts, 0.0, ALU.mult, ALU.add))
            chained(nc.vector.tensor_tensor(flat(excl), flat(incl), counts, ALU.subtract))
            chained(nc.vector.tensor_tensor(flat(posn), flat(excl), pH[0][0:R, 0:2 * NE * NT], ALU.add))
            over_count = incl[:, 0, :, NT - 1]
            nc.vector.scalar_tensor_tensor(slot_g[:, :, :], posn[:, 0, :, :], -FAR, sel[:, 0, :, :], ALU.add, ALU.mult)
            chained(nc.vector.tensor_tensor(slot_q[:, :, :], posn[:, 1, :, :], spread(over_count, NT), ALU.add))
            chained(nc.vector.scalar_tensor_tensor(slot_e[:, :, :], slot_q[:, :, :], -FAR, sel[:, 1, :, :],
                                                   ALU.add, ALU.mult))
            chained(nc.vector.scalar_tensor_tensor(slot[:, :, :], slot_g[:, :, :], FAR, slot_e[:, :, :],
                                                   ALU.add, ALU.add))
            nc.vector.tensor_scalar(hi_i[:, :, :], slot[:, :, :], 7, None, ALU.logical_shift_right)
            chained(nc.vector.tensor_scalar(lo_i[:, :, :], slot[:, :, :], P - 1, None, ALU.bitwise_and))
            nc.vector.tensor_copy(hi[:, :], hi_i[:, :, :].rearrange("p e t -> p (e t)"))
            chained(nc.vector.tensor_copy(lo[:, :, :], lo_i[:, :, :]))
            chained(nc.vector.tensor_tensor(in_tile[:, :, :], spread(hi[:, :], NST), every(iota_j[:, :], NE * NT),
                                            ALU.is_equal))
            m = marks[:, :, :, :, :].rearrange("p e t v j -> p (e t) v j")
            nc.vector.tensor_tensor(m[:, :, 0, :], in_tile[:, :, :],
                                    spread(tile_no[:, :, :].rearrange("p e t -> p (e t)"), NST), ALU.mult)
            nc.vector.tensor_scalar(m[:, :, 1, :], in_tile[:, :, :], row_no[:, 0:1], None,
                                    ALU.mult).then_inc(marks_made, 1)

            def hot_tiles(e, t0, t1):
                if t0 == 0:
                    dve.wait_ge(ids_done, e)
                for t in range(t0, t1):
                    row_slot = lo[:, bass.ds(e, 1), t:t + 1].rearrange("p a t -> p (a t)")
                    last = nc.vector.tensor_scalar(hot[:, t, :], iota_s[:, :], row_slot, None, ALU.is_equal)
                if t1 == NT:
                    last.then_inc(hot_made, 1)

            def tokens_out(e, par):
                dve.wait_ge(ids_done, e + 1)
                nc.vector.tensor_scalar(tile_rows[:, :], ids[:, 0:NST], float(R), None,
                                        ALU.mult).then_inc(tile_rows_made, 1)
                dve.wait_ge(tile_rows_made, e + 1)
                nc.vector.tensor_tensor(to_gather[par][:, :], tile_rows[:, :], ids[:, NST:2 * NST],
                                        ALU.add).then_inc(to_gather_made, 1)

            for e in range(2):
                hot_tiles(e, 0, NT)
                tokens_out(e, e)

            def rows_out(e, par):
                for k in range(2):
                    dve.wait_ge(yt_done, 2 * e + k + 1)
                    nc.vector.tensor_copy(yT[par][0][:, k, :], pY[k][:, 0:CAP]).then_inc(yt_high, 1)
                for k in range(2):
                    dve.wait_ge(yt_high, 2 * e + k + 1)
                    nc.vector.tensor_tensor(yT[par][1][:, k, :], pY[k][:, 0:CAP], yT[par][0][:, k, :],
                                            ALU.subtract).then_inc(yt_out, 1)

            rows_out(0, 0)

            def step(dve, e, half, par):
                for j in range(NF):
                    if j % 2 == 0:
                        dve.wait_ge(h_high[0], NF // 2 * e + j // 2 + 1)
                    else:
                        if there(e + 1):
                            weights_low(e + 1, 1 - par, j // 2)
                        dve.wait_ge(h_out, NF * e + j + 1)
                        nc.vector.tensor_copy(hT[0][:, j, 0:CAP], h_whole[1][:, :]).then_inc(h_high[1], 1)
                        dve.wait_ge(h_high[1], NF // 2 * e + j // 2 + 1)
                    nc.vector.tensor_tensor(hT[1][:, j, 0:CAP], h_whole[j % 2][:, :], hT[0][:, j, 0:CAP],
                                            ALU.subtract).then_inc(h_low, 1)
                for n, (t0, t1) in enumerate(((0, 6), (6, 12), (12, 17), (17, NT))):
                    if there(e + 1):
                        weights_low(e + 1, 1 - par, 4 + n)
                    if n == 2 and there(e + 1):
                        rows_out(e + 1, 1 - par)
                    if there(e + 2):
                        hot_tiles(e + 2, t0, t1)
                dve.wait_ge(y_here[par], 16 * NST * (half + 1))
                if not isinstance(e, int) or e > 1:
                    dve.wait_ge(scattered, 16 * NST * (e - 1))
                nc.vector.tensor_copy(to_scatter[par][:, :], to_gather[par][:, :]).then_inc(to_scatter_made, 1)
                if there(e + 2):
                    tokens_out(e + 2, par)
                dve.wait_ge(b2_here[par], 16 * (half + 1))
                dve.wait_ge(ow_made, NST * e)
                for bank, j0, nt, n in ((0, 0, 2, P), (1, 2, 1, LAST)):
                    dve.wait_ge(o_done, 2 * e + bank + 1)
                    nc.vector.tensor_tensor(ob[0:n, j0:j0 + nt, :],
                                            pO[bank][0:n, 0:nt * D].rearrange("p (t d) -> p t d", t=nt),
                                            every(b2[par][0:n, :], nt), ALU.add).then_inc(ob_made, 1)
                dve.wait_ge(ob_made, 2 * (e + 1))
                dve.wait_ge(scattered, 16 * NST * e)
                for j in range(NST):
                    n = rows_in[j]
                    score = yg[par][0:n, j, bass.ds(D + e, 1)]
                    nc.vector.tensor_scalar(ow[0:n, j, :], ob[0:n, j, :], score, None, ALU.mult).then_inc(ow_made, 1)

            steps(dve, step)


class RetentionReady:

    N_LOADS = 12

    def __init__(self, nc, ctx, *weights):
        self.nc, self.weights = nc, weights
        rWq, sWg = weights[0], weights[8]
        sb = lambda n, s, d=F32: ctx.enter_context(nc.sbuf_tensor("r_" + n, s, d))
        self.loaded, self.made, self.setup = (
            ctx.enter_context(nc.semaphore("r_" + n)) for n in ("loaded", "made", "setup"))
        H1 = rWq.shape[0]
        FS = sWg.shape[1]
        FB = FS - P
        PER = IPG * H1
        self.sizes = H1, FS, FB, PER
        self.w_q = sb("w_q", [P, H1, P])
        self.w_k = sb("w_k", [P, H1, P])
        self.w_v = sb("w_v", [P, H1, P])
        self.w_g = sb("w_g", [P, 2, D])
        self.w_o = sb("w_o", [P, 2, D])
        self.w_r = sb("w_r", [P, 2, P])
        self.w_sg = sb("w_sg", [P, 2, FS])
        self.w_su = sb("w_su", [P, 2, FS])
        self.w_sd0 = sb("w_sd0", [P, D])
        self.w_sd1 = sb("w_sd1", [FB, D])
        self.gam_rows = sb("gam_rows", [2, P])
        self.bet_rows = sb("bet_rows", [2, P])
        self.gam_bet = sb("gam_bet", [P, 4])
        self.gap = sb("gap", [R, R])
        self.gammas = sb("gammas", [R, R])
        self.power = sb("power", [R, H1, R])
        self.decay_a = sb("decay_a", [R, H1, R])
        self.decay = sb("decay", [R, H1, R])
        self.pair_a = sb("pair_a", [P, P])
        self.pair_b = sb("pair_b", [P, P])
        self.pair = sb("pair", [P, P])
        self.half_neg = sb("half_neg", [P, PER])

    def load(self, sp):
        rWq, rWk, rWv, rWg, rWo, gn_gamma, gn_beta, router_w, sWg, sWu, sWd = self.weights
        loaded, made, FS = self.loaded, self.made, self.sizes[1]
        for dst, src in [
            (self.gam_rows[:, :], gn_gamma.rearrange("(k p) -> k p", p=P)),
            (self.bet_rows[:, :], gn_beta.rearrange("(k p) -> k p", p=P)),
            (self.w_q[:, :, :], rWq.rearrange("h p n -> p h n")),
            (self.w_k[:, :, :], rWk.rearrange("h p n -> p h n")),
            (self.w_v[:, :, :], rWv.rearrange("h p n -> p h n")),
            (self.w_g[:, :, :], rWg.rearrange("(k p) n -> p k n", p=P)),
            (self.w_o[:, :, :], rWo.rearrange("(k p) n -> p k n", p=P)),
            (self.w_sg[:, :, :], sWg.rearrange("(k p) n -> p k n", p=P)),
            (self.w_su[:, :, :], sWu.rearrange("(k p) n -> p k n", p=P)),
            (self.w_sd0[:, :], sWd[0:P, :]),
            (self.w_sd1[:, :], sWd[P:FS, :]),
        ]:
            sp.dma_start(dst, src).then_inc(loaded, 16)
        sp.wait_ge(made, 1)
        sp.dma_start(self.w_r[:, :, 0:NE], router_w.rearrange("(k p) e -> p k e", p=P)).then_inc(loaded, 16)

    def make_powers(self, pool, h):
        nc, made, setup = self.nc, self.made, self.setup
        if h == 0:
            nc.gpsimd.memset(self.w_r[:, :, :], 0.0).then_inc(made, 1)
            nc.gpsimd.memset(self.half_neg[:, :], -0.5)
            nc.gpsimd.iota(self.gap[:, :], pattern=[[1, R]], base=0, channel_multiplier=-1,
                           allow_small_or_imprecise_dtypes=True)
        nc.gpsimd.memset(self.gammas[:, :], 1.0 - 2.0 ** (-5 - h)).then_inc(setup, 1)
        pool.wait_ge(setup, 2 * h + 1)
        nc.gpsimd.tensor_tensor(self.power[:, h, :], self.gammas[:, :], self.gap[:, :], ALU.pow).then_inc(setup, 1)
        pool.wait_ge(setup, 2 * h + 2)

    def make_decay(self, pool):
        nc, made, setup, H1 = self.nc, self.made, self.setup, self.sizes[0]
        for b in range(IPT):
            cols = slice(b * S, (b + 1) * S)
            nc.gpsimd.affine_select(out=self.decay_a[:, :, cols], in_=self.power[:, :, cols], compare_op=ALU.is_ge,
                                    fill=0.0, base=-b * S, pattern=[[0, H1], [0, S]], channel_multiplier=1)
        nc.gpsimd.memset(self.pair_a[:, :], 1.0 / (2 * S)).then_inc(setup, 1)
        pool.wait_ge(setup, 2 * H1 + 1)
        for b in range(IPT):
            cols = slice(b * S, (b + 1) * S)
            nc.gpsimd.affine_select(out=self.decay[:, :, cols], in_=self.decay_a[:, :, cols], compare_op=ALU.is_gt,
                                    fill=0.0, base=(b + 1) * S, pattern=[[0, H1], [0, S]], channel_multiplier=-1)
        pa, pb, pc = (x[:, :].rearrange("p (g e) -> p g e", e=2) for x in (self.pair_a, self.pair_b, self.pair))
        nc.gpsimd.affine_select(out=pb, in_=pa, compare_op=ALU.is_ge, fill=0.0, base=0,
                                pattern=[[-2, P // 2], [0, 2]], channel_multiplier=1).then_inc(made, 1)
        pool.wait_ge(made, 2)
        nc.gpsimd.affine_select(out=pc, in_=pb, compare_op=ALU.is_ge, fill=0.0, base=1,
                                pattern=[[2, P // 2], [0, 2]], channel_multiplier=-1).then_inc(made, 2)
        pool.wait_ge(made, 4)


def retention(nc, ctx, const, ready, acc_rows, h, x3_rows, logits):
    sb = lambda n, s, d=F32: ctx.enter_context(nc.sbuf_tensor("r_" + n, s, d))
    sem = lambda n: semaphore(nc, const, "r_" + n)
    H1, FS, FB, PER = ready.sizes
    loaded, made = ready.loaded, ready.made

    stats2 = sb("stats2", [R, 2, 6])
    mv2 = sb("mv2", [R, 2, 2])
    ve2 = sb("ve2", [R, 2])
    rstd2 = sb("rstd2", [R, 2])
    xn = sb("xn", [R, 2, D])
    xnT = sb("xnT", [P, 2, GT])
    QT = [sb(f"QT{i}", [P, H1, GT]) for i in range(2)]
    KT = [sb(f"KT{i}", [P, H1, GT]) for i in range(2)]
    V = [sb(f"V{i}", [R, 2, H1, P]) for i in range(2)]
    gate = [sb(f"gate{i}", [P, 2, GT]) for i in range(2)]
    dec = sb("dec", [R, 2, H1, R])
    ysum = sb("ysum", [P, PER])
    ymean = sb("ymean", [P, PER])
    yc = [sb(f"yc{i}", [P, PER, S]) for i in range(2)]
    ysq = sb("ysq", [P, PER, S])
    ysum2 = sb("ysum2", [P, PER])
    yvar = sb("yvar", [P, PER])
    yrstd = sb("yrstd", [P, PER])
    z1 = sb("z1", [P, 2, GT])
    z2 = sb("z2", [P, 2, GT])
    zT = sb("zT", [P, 2, GT])
    stats3 = sb("stats3", [R, 2, 6])
    mv3 = sb("mv3", [R, 2, 2])
    ve3 = sb("ve3", [R, 2])
    rstd3 = sb("rstd3", [R, 2])
    x3 = sb("x3", [R, 2, D])
    x3T = sb("x3T", [P, 2, GT])
    sg0 = sb("sg0", [P, GT])
    sg1 = sb("sg1", [FB, GT])
    hid0 = sb("hid0", [P, GT])
    hid1 = sb("hid1", [FB, GT])

    bank = [ctx.enter_context(nc.psum_tensor(f"r_bank{i}", [P, 512], F32)) for i in range(8)]
    pS, pY, pM, pF0, pF1, pT0, pT1, pT2 = bank

    gb_done, gb_out = sem("gb_done"), sem("gb_out")
    h2_here = [sem(f"h2_here{i}") for i in range(2)]
    ln2_stat, ln2_var, ln2_eps, ln2_rstd, xn_made = (
        sem(n) for n in ("ln2_stat", "ln2_var", "ln2_eps", "ln2_rstd", "xn_made"))
    xnT_done, xnT_out = sem("xnT_done"), sem("xnT_out")
    q_done, q_out, k_done, k_out, v_done, v_out, g_done, g_out = (
        sem(n) for n in ("q_done", "q_out", "k_done", "k_out", "v_done", "v_out", "g_done", "g_out"))
    s_done, s_out, y_done, y_sum, m_done, m_out, y_cent, y_sq, y_sum2, v2_done, y_var, y_rstd = (
        sem(n) for n in ("s_done", "s_out", "y_done", "y_sum", "m_done", "m_out", "y_cent", "y_sq", "y_sum2",
                         "v2_done", "y_var", "y_rstd"))
    z1_made, z2_made, z_made, wo_done, h3_made = (
        sem(n) for n in ("z1_made", "z2_made", "z_made", "wo_done", "h3_made"))
    ln3_stat, ln3_var, ln3_eps, ln3_rstd, x3_made, x3_stored = (
        sem(n) for n in ("ln3_stat", "ln3_var", "ln3_eps", "ln3_rstd", "x3_made", "x3_stored"))
    x3T_done, x3T_out, lg_done, lg_out = sem("x3T_done"), sem("x3T_out"), sem("lg_done"), sem("lg_out")
    sh_done, silu_done, hid_made, dn_done, h4_made = (
        sem(n) for n in ("sh_done", "silu_done", "hid_made", "dn_done", "h4_made"))

    acc_t = acc_rows.rearrange("(t p) d -> p t d", p=R)
    pair_of = lambda n: h[:, bass.ds(2 * n, 2), :]
    x3_t = x3_rows.rearrange("(t p) d -> p t d", p=R)

    def steps(eng, step):
        for g in range(-1, 2):
            step(eng, g, g % 2)
        with eng.Fori(1, NG // 2 - 1) as i:
            for par in range(2):
                step(eng, 2 * i + par, par)
        for g in range(NG - 3, NG + 2):
            step(eng, g, g % 2)

    def there(n):
        return not isinstance(n, int) or 0 <= n < NG

    def later(n, first=1):
        return not isinstance(n, int) or n >= first

    with nc.Block() as block:

        @block.sync
        def _(sp):
            for n, (t0, t1) in enumerate(((0, 4), (4, NT))):
                sp.dma_start(h[:, t0:t1, :], acc_t[:, t0:t1, :]).then_inc(h2_here[n], 16)
            def store(g):
                sp.wait_ge(x3_made, 2 * (g + 1))
                sp.dma_start(x3_t[:, bass.ds(2 * g, 2), :], x3[:, :, :]).then_inc(x3_stored, 16)

            store(0)
            with sp.Fori(1, NG) as g:
                store(g)
            sp.wait_ge(x3_stored, 16 * NG)

        @block.tensor
        def _(pe):
            pe.wait_ge(loaded, 16 * ready.N_LOADS)
            nc.tensor.transpose(pS[:, 0:2], ready.gam_rows[:, :], const.ident[0:2, 0:2])
            nc.tensor.transpose(pS[:, 2:4], ready.bet_rows[:, :], const.ident[0:2, 0:2]).then_inc(gb_done, 1)
            pe.wait_ge(gb_out, 1)
            pe.wait_ge(made, 4)

            def transposes(dst, src, done):
                for tile in range(2):
                    for k in range(2):
                        mm = nc.tensor.transpose(dst[:, k * GT + tile * R:k * GT + (tile + 1) * R],
                                                 src[:, tile, k * P:(k + 1) * P], const.ident[0:R, 0:R])
                mm.then_inc(done, 1)

            def step(pe, g, par):
                f, b, t = g + 1, g - 1, g - 2
                attend, front, back, tail = there(g), there(f), there(b), there(t)
                if back:
                    pe.wait_ge(y_sum2, b + 1)
                    pe.wait_ge(h3_made, b)
                    nc.tensor.matmul(pM[:, 0:PER], ready.pair[:, :], ysum2[:, :], start=True,
                                     stop=True).then_inc(v2_done, 1)
                if front:
                    pe.wait_ge(xn_made, 2 * (f + 1))
                    pe.wait_ge(g_out, f)
                    transposes(pF0, xn, xnT_done)
                if attend:
                    pe.wait_ge(q_out, g + 1)
                    pe.wait_ge(k_out, g + 1)
                    pe.wait_ge(s_out, g)
                    for tile in range(2):
                        for hd in range(H1):
                            cols = slice(tile * R, (tile + 1) * R)
                            mm = nc.tensor.matmul(pS[0:R, (tile * H1 + hd) * R:(tile * H1 + hd + 1) * R],
                                                  KT[par][:, hd, cols], QT[par][:, hd, cols], start=True, stop=True)
                    mm.then_inc(s_done, 1)
                if front:
                    pe.wait_ge(xnT_out, f + 1)
                    pe.wait_ge(v_out, f)
                    for hd in range(H1):
                        mm = nc.tensor.matmul(pF1[:, hd * GT:(hd + 1) * GT], ready.w_q[:, hd, :], xnT[:, hd, :],
                                              start=True, stop=True)
                    mm.then_inc(q_done, 1)
                    for hd in range(H1):
                        mm = nc.tensor.matmul(pF0[:, hd * GT:(hd + 1) * GT], ready.w_k[:, hd, :], xnT[:, hd, :],
                                              start=True, stop=True)
                    mm.then_inc(k_done, 1)
                if attend:
                    pe.wait_ge(s_out, g + 1)
                    pe.wait_ge(v_out, g + 1)
                    pe.wait_ge(y_cent, g)
                    for tile in range(2):
                        for hd in range(H1):
                            mm = nc.tensor.matmul(pY[:, hd * GT + tile * R:hd * GT + (tile + 1) * R],
                                                  V[par][:, tile, hd, :], dec[:, tile, hd, :], start=True, stop=True)
                    mm.then_inc(y_done, 1)
                if tail:
                    pe.wait_ge(x3_made, 2 * (t + 1))
                    pe.wait_ge(lg_out, t)
                    transposes(pT0, x3, x3T_done)
                if front:
                    pe.wait_ge(q_out, f + 1)
                    for tile in range(2):
                        for hd in range(H1):
                            mm = nc.tensor.matmul(pF1[0:R, (tile * H1 + hd) * P:(tile * H1 + hd + 1) * P],
                                                  xnT[:, hd, tile * R:(tile + 1) * R], ready.w_v[:, hd, :],
                                                  start=True, stop=True)
                    mm.then_inc(v_done, 1)
                if attend:
                    pe.wait_ge(y_sum, g + 1)
                    if back:
                        pe.wait_ge(y_var, b + 1)
                    nc.tensor.matmul(pM[:, 0:PER], ready.pair[:, :], ysum[:, :], start=True,
                                     stop=True).then_inc(m_done, 1)
                if front:
                    pe.wait_ge(k_out, f + 1)
                    for m in range(2):
                        for k in range(2):
                            mm = nc.tensor.matmul(pF0[:, m * GT:(m + 1) * GT], ready.w_g[:, k, m * P:(m + 1) * P],
                                                  xnT[:, k, :], start=(k == 0), stop=(k == 1))
                    mm.then_inc(g_done, 1)
                if tail:
                    pe.wait_ge(x3T_out, t + 1)
                    pe.wait_ge(h4_made, t)
                    for n, w in ((0, ready.w_sg), (1, ready.w_su)):
                        for k in range(2):
                            nc.tensor.matmul(pT1[:, n * GT:(n + 1) * GT], w[:, k, 0:P], x3T[:, k, :],
                                             start=(k == 0), stop=(k == 1))
                    for n, w in ((0, ready.w_sg), (1, ready.w_su)):
                        for k in range(2):
                            mm = nc.tensor.matmul(pT2[0:FB, n * GT:(n + 1) * GT], w[:, k, P:FS], x3T[:, k, :],
                                                  start=(k == 0), stop=(k == 1))
                    mm.then_inc(sh_done, 1)
                    for tile in range(2):
                        for k in range(2):
                            mm = nc.tensor.matmul(pT0[0:R, tile * P:(tile + 1) * P], x3T[:, k, tile * R:(tile + 1) * R],
                                                  ready.w_r[:, k, :], start=(k == 0), stop=(k == 1))
                    mm.then_inc(lg_done, 1)
                if back:
                    pe.wait_ge(z_made, b + 1)
                    if attend:
                        pe.wait_ge(m_out, g + 1)
                    for tile in range(2):
                        for k in range(2):
                            mm = nc.tensor.matmul(pM[0:R, tile * D:(tile + 1) * D], zT[:, k, tile * R:(tile + 1) * R],
                                                  ready.w_o[:, k, :], start=(k == 0), stop=(k == 1))
                    mm.then_inc(wo_done, 1)
                if tail:
                    pe.wait_ge(hid_made, 2 * (t + 1))
                    for tile in range(2):
                        cols = slice(tile * R, (tile + 1) * R)
                        nc.tensor.matmul(pT1[0:R, tile * D:(tile + 1) * D], hid0[:, cols], ready.w_sd0[:, :],
                                         start=True, stop=False)
                        mm = nc.tensor.matmul(pT1[0:R, tile * D:(tile + 1) * D], hid1[:, cols], ready.w_sd1[:, :],
                                              start=False, stop=True)
                    mm.then_inc(dn_done, 1)

            steps(pe, step)

        @block.scalar
        def _(act):
            act.wait_ge(gb_done, 1)
            nc.scalar.activation(ready.gam_bet[:, :], pS[:, 0:4], ACT.Copy).then_inc(gb_out, 1)
            act.wait_ge(gb_out, 1)

            def out_of(dst, src, func, done, out, n):
                act.wait_ge(done, n + 1)
                nc.scalar.activation(dst, src, func).then_inc(out, 1)

            flat = lambda a: a[:, :, :].rearrange("p a b -> p (a b)")

            def step(act, g, par):
                f, b, t, other = g + 1, g - 1, g - 2, 1 - par
                attend, front, back, tail = there(g), there(f), there(b), there(t)
                if front:
                    act.wait_ge(g_done, f)
                    out_of(flat(xnT), pF0[:, 0:2 * GT], ACT.Copy, xnT_done, xnT_out, f)
                    out_of(flat(QT[other]), pF1[:, 0:2 * GT], ACT.Copy, q_done, q_out, f)
                    out_of(flat(KT[other]), pF0[:, 0:2 * GT], ACT.Copy, k_done, k_out, f)
                if tail:
                    act.wait_ge(lg_done, t)
                    out_of(flat(x3T), pT0[:, 0:2 * GT], ACT.Copy, x3T_done, x3T_out, t)
                if attend:
                    act.wait_ge(y_cent, g + 1)
                    act.wait_ge(y_sum2, g)
                    nc.scalar.activation(ysq[:, :, :], yc[par][:, :, :], ACT.Square).then_inc(y_sq, 1)
                if back:
                    act.wait_ge(z1_made, b + 1)
                    act.wait_ge(z_made, b)
                    for k in range(2):
                        last = nc.scalar.activation(z2[:, k, :], z1[:, k, :], ACT.Identity,
                                                    bias=ready.gam_bet[:, 2 + k:3 + k],
                                                    scale=ready.gam_bet[:, k:k + 1])
                    last.then_inc(z2_made, 1)
                if tail:
                    act.wait_ge(sh_done, t + 1)
                    act.wait_ge(hid_made, 2 * t)
                    nc.scalar.activation(sg0[:, :], pT1[:, 0:GT], ACT.Silu)
                    nc.scalar.activation(sg1[:, :], pT2[0:FB, 0:GT], ACT.Silu).then_inc(silu_done, 1)
                if front:
                    if later(f, 2):
                        act.wait_ge(z_made, f - 1)
                    out_of(flat(gate[other]), pF0[:, 0:2 * GT], ACT.Relu, g_done, g_out, f)

            steps(act, step)

        @block.gpsimd
        def _(pool):
            def rstd_of(mv, ve, rstd, stat, eps, done, n):
                wait_alone(pool, const, stat, 2 * (n + 1))
                nc.gpsimd.tensor_scalar(ve[:, :], mv[:, :, 1], LN_EPS, None, ALU.add).then_inc(eps, 1)
                pool.wait_ge(eps, n + 1)
                nc.gpsimd.tensor_tensor(rstd[:, :], ve[:, :], const.neg_half[0:R, :], ALU.pow).then_inc(done, 1)

            def step(pool, g, par):
                b, t, n, other = g - 1, g - 2, g + 2, 1 - par
                if there(t):
                    rstd_of(mv3, ve3, rstd3, ln3_var, ln3_eps, ln3_rstd, t)
                if there(b):
                    pool.wait_ge(y_var, b + 1)
                    nc.gpsimd.tensor_tensor(yrstd[:, :], yvar[:, :], ready.half_neg[:, :],
                                            ALU.pow).then_inc(y_rstd, 1)
                    pool.wait_ge(y_rstd, b + 1)
                    pool.wait_ge(z2_made, b)
                    nc.gpsimd.tensor_tensor(z1[:, :, :].rearrange("p k (b s) -> p (k b) s", s=S), yc[other][:, :, :],
                                            spread(yrstd[:, :], S), ALU.mult).then_inc(z1_made, 1)
                if there(n):
                    rstd_of(mv2, ve2, rstd2, ln2_var, ln2_eps, ln2_rstd, n)
                if there(b):
                    pool.wait_ge(z2_made, b + 1)
                    pool.wait_ge(g_out, b + 1)
                    pool.wait_ge(wo_done, b)
                    nc.gpsimd.tensor_tensor(zT[:, :, :], z2[:, :, :], gate[other][:, :, :],
                                            ALU.mult).then_inc(z_made, 1)

            rstd_of(mv2, ve2, rstd2, ln2_var, ln2_eps, ln2_rstd, 0)
            steps(pool, step)

        @block.vector
        def _(dve):
            def rows_of(n, tile):
                return h[:, bass.ds(2 * n + tile, 1), :].rearrange("p a d -> p (a d)")

            def norm_stats(stats, mv, stat, var, n):
                for tile in range(2):
                    nc.vector.bn_stats(stats[:, tile, :], rows_of(n, tile)).then_inc(stat, 1)
                for tile in range(2):
                    wait_alone(dve, const, stat, 2 * n + tile + 1)
                    nc.vector.bn_aggr(mv[:, tile, :], stats[:, tile, :]).then_inc(var, 1)

            def normalise(dst, mv, rstd, rstd_made, normed, n):
                dve.wait_ge(rstd_made, n + 1)
                for tile in range(2):
                    nc.vector.tensor_scalar(dst[:, tile, :], rows_of(n, tile), mv[:, tile, 0:1],
                                            rstd[:, tile:tile + 1], ALU.subtract, ALU.mult).then_inc(normed, 1)

            def first_stats(n):
                if isinstance(n, int) and n in (0, 2):
                    dve.wait_ge(h2_here[n // 2], 16)
                norm_stats(stats2, mv2, ln2_stat, ln2_var, n)

            def first_norm(n):
                dve.wait_ge(xnT_done, n)
                normalise(xn, mv2, rstd2, ln2_rstd, xn_made, n)

            first_stats(0)
            first_norm(0)
            dve.wait_ge(made, 4)

            def step(dve, g, par):
                f, b, t, n, other = g + 1, g - 1, g - 2, g + 2, 1 - par
                attend, front, back, tail, ahead = there(g), there(f), there(b), there(t), there(n)
                if tail:
                    wait_alone(dve, const, h3_made, t + 1)
                    norm_stats(stats3, mv3, ln3_stat, ln3_var, t)
                if back:
                    dve.wait_ge(v2_done, b + 1)
                    dve.wait_ge(y_rstd, b)
                    nc.vector.tensor_scalar(yvar[:, :], pM[:, 0:PER], GN_EPS, None, ALU.add).then_inc(y_var, 1)
                if attend:
                    dve.wait_ge(s_done, g + 1)
                    dve.wait_ge(y_done, g)
                    nc.vector.tensor_tensor(dec[:, :, :, :].rearrange("p a b c -> p a (b c)"),
                                            pS[0:R, 0:2 * GT].rearrange("p (a b) -> p a b", a=2),
                                            both(ready.decay[:, :, :].rearrange("p h s -> p (h s)")),
                                            ALU.mult).then_inc(s_out, 1)
                if tail:
                    dve.wait_ge(x3T_done, t)
                    dve.wait_ge(x3_stored, 16 * t)
                    normalise(x3, mv3, rstd3, ln3_rstd, x3_made, t)
                if ahead:
                    first_stats(n)
                if attend:
                    dve.wait_ge(y_done, g + 1)
                    dve.wait_ge(m_done, g)
                    yv = pY[:, 0:2 * GT].rearrange("p (n s) -> p n s", s=S)
                    nc.vector.tensor_reduce(ysum[:, :], yv, AX_X, ALU.add).then_inc(y_sum, 1)
                if front:
                    dve.wait_ge(v_done, f + 1)
                    nc.vector.tensor_copy(V[other][:, :, :, :].rearrange("p a b c -> p (a b c)"),
                                          pF1[0:R, :]).then_inc(v_out, 1)
                if attend:
                    dve.wait_ge(m_done, g + 1)
                    nc.vector.tensor_copy(ymean[:, :], pM[:, 0:PER]).then_inc(m_out, 1)
                    dve.wait_ge(m_out, g + 1)
                    if later(g, 2):
                        dve.wait_ge(z1_made, g - 1)
                        dve.wait_ge(y_sq, g - 1)
                    nc.vector.tensor_tensor(yc[par][:, :, :], yv, spread(ymean[:, :], S),
                                            ALU.subtract).then_inc(y_cent, 1)
                if ahead:
                    first_norm(n)
                if attend:
                    dve.wait_ge(y_sq, g + 1)
                    dve.wait_ge(v2_done, g)
                    nc.vector.tensor_reduce(ysum2[:, :], ysq[:, :, :], AX_X, ALU.add).then_inc(y_sum2, 1)
                if tail:
                    dve.wait_ge(silu_done, t + 1)
                    dve.wait_ge(dn_done, t)
                    nc.vector.tensor_tensor(hid0[:, :], sg0[:, :], pT1[:, GT:2 * GT], ALU.mult).then_inc(hid_made, 1)
                    nc.vector.tensor_tensor(hid1[:, :], sg1[:, :], pT2[0:FB, GT:2 * GT],
                                            ALU.mult).then_inc(hid_made, 1)
                    dve.wait_ge(lg_done, t + 1)
                    nc.vector.tensor_copy(logits[0:R, bass.ds(2 * t, 2), :],
                                          pT0[0:R, 0:2 * P].rearrange("p (t e) -> p t e", t=2)[:, :, 0:NE]
                                          ).then_inc(lg_out, 1)
                if back:
                    dve.wait_ge(wo_done, b + 1)
                    nc.vector.tensor_tensor(pair_of(b), pM[0:R, :].rearrange("p (t d) -> p t d", t=2), pair_of(b),
                                            ALU.add).then_inc(h3_made, 1)
                if tail:
                    dve.wait_ge(dn_done, t + 1)
                    nc.vector.tensor_tensor(pair_of(t), pT1[0:R, :].rearrange("p (t d) -> p t d", t=2), pair_of(t),
                                            ALU.add).then_inc(h4_made, 1)

            steps(dve, step)


def token_choice(nc, ctx, const, logits, expert_bias, eWg, eWu, eWd, h, pair_rows, x3_rows, out):
    sb = lambda n, s, d=F32: ctx.enter_context(nc.sbuf_tensor("t_" + n, s, d))
    sem = lambda n: semaphore(nc, const, "t_" + n)
    ps = lambda n, d=F32: ctx.enter_context(nc.psum_tensor("t_" + n, [P, 512], d))
    F = eWg.shape[2]
    FB = F - P
    DUMP = TOPK * NT * R
    FULL = TOK // R
    CHUNKS = [(c, min(c + 4, FULL), R) for c in range(0, FULL, 4)] + [(FULL, NT, TOK - FULL * R)]
    NV = 5
    BY_POOL = (2, 3)
    BIG = 1.0e30

    bias = sb("bias", [R, NE])
    valid = sb("valid", [R, NT])
    sig = sb("sig", [R, NT, NE])
    tot = sb("tot", [R, NT, NE])
    best = sb("best", [R, NT])
    tie = sb("tie", [R, NT, NE])
    rank = sb("rank", [R, NT, NE])
    first = sb("first", [R, NT])
    pick = [sb(f"pick{k}", [R, NT, NE]) for k in range(TOPK)]
    rest = sb("rest", [R, NT, NE])
    prod = sb("prod", [R, NT, NE])
    w = sb("w", [R, TOPK, NT])
    wsum = sb("wsum", [R, NT])
    winv = sb("winv", [R, NT])
    wn = sb("wn", [R, TOPK, NT])
    w_left = sb("w_left", [R, TOPK, NT])
    chosen = sb("chosen", [R, NE, NT], BF16)
    ones_b = sb("ones_b", [R, P], BF16)
    tri = sb("tri", [R, R], BF16)
    reset = sb("reset", [R, NE * NT])
    incl = sb("incl", [R, NE, NT])
    excl = sb("excl", [R, NE, NT])
    posn = sb("posn", [R, NE, NT])
    tiles_i = sb("tiles_i", [R, NE], I32)
    tiles_s = sb("tiles_s", [R, NE], I32)
    tiles = sb("tiles", [R, NE])
    one8 = sb("one8", [R, NE])
    upto = sb("upto", [R, NE])
    start = sb("start", [R, NE])
    slot_all = sb("slot_all", [R, NE, NT])
    slot_f = sb("slot_f", [R, TOPK, NT])
    slot = sb("slot", [R, TOPK, NT], I32)
    hi_i = sb("hi_i", [R, TOPK, NT], I32)
    lo_i = sb("lo_i", [R, TOPK, NT], I32)
    hi = sb("hi", [R, TOPK * NT])
    lo = sb("lo", [R, TOPK * NT])
    iota_s = sb("iota_s", [R, P], BF16)
    iota_j = sb("iota_j", [R, NTILE])
    iota_w = sb("iota_w", [R, NE])
    values = sb("values", [R, NV, TOPK * NT], BF16)
    in_tile = sb("in_tile", [R, TOPK * NT, NTILE], BF16)
    marks = sb("marks", [R, TOPK * NT, NV, NTILE], BF16)
    hot = sb("hot", [R, TOPK * NT, P], BF16)
    told = sb("told", [P, NV, NTILE])
    tok_a = sb("tok_a", [P, NTILE])
    tok_b = sb("tok_b", [P, NTILE])
    tok_c = sb("tok_c", [P, NTILE])
    free = sb("free", [P, NTILE])
    second = sb("second", [P, NTILE])
    dump = sb("dump", [P, NTILE])
    src_idx = sb("src_idx", [P, NTILE], I32)
    dst_idx = sb("dst_idx", [P, NTILE], I32)
    w_a = sb("w_a", [P, NTILE])
    w_slot = sb("w_slot", [P, NTILE])
    owner_m = sb("owner_m", [1, NTILE, NE])
    owner_f = sb("owner_f", [1, NTILE])
    owner = sb("owner", [1, NTILE], I32)

    w_gu = sb("w_gu", [P, NE, 2, 2 * F])
    w_d0 = sb("w_d0", [P, NE, D])
    w_d1 = sb("w_d1", [FB, NE, D])
    tok_in = [sb(f"tok_in{i}", [P, 1], I32) for i in range(2)]
    tok_out = [sb(f"tok_out{i}", [P, 1], I32) for i in range(2)]
    xg = [sb(f"xg{i}", [P, D]) for i in range(2)]
    xT = [sb(f"xT{i}", [P, 2, P]) for i in range(2)]
    sg = [sb(f"sg{i}", [P, F]) for i in range(2)]
    hid = [sb(f"hid{i}", [P, F]) for i in range(2)]
    hT = [sb(f"hT{i}", [P, 2, P]) for i in range(2)]
    ow = [sb(f"ow{i}", [P, D]) for i in range(2)]
    picks = sb("picks", [R, TOPK, NT, D])

    pX = [ps(f"x{i}") for i in range(2)]
    pG = [ps(f"g{i}") for i in range(2)]
    pT = [ps(f"t{i}") for i in range(2)]
    pD = [ps(f"d{i}") for i in range(2)]

    def steps(eng, parts):
        def step(half, par):
            for lead, part in parts.items():
                n = 2 * half + par + lead
                if not isinstance(n, int) or 0 <= n < NTILE:
                    shift, parity = divmod(par + lead, 2)
                    part(n, half + shift, parity)

        for j in range(-2, 2):
            step(j // 2, j % 2)
        with eng.Fori(1, NTILE // 2 - 2) as i:
            for par in range(2):
                step(i, par)
        for j in range(NTILE - 4, NTILE + 1):
            step(j // 2, j % 2)

    def follows(nth):
        return not isinstance(nth, int) or nth > 0

    loaded, w_here, made, link, sig_made = sem("loaded"), sem("w_here"), sem("made"), sem("link"), sem("sig_made")
    chosen_made, prefix_done, in_tile_made, pool_marked, marks_made, told_done, idx_made = (
        sem(n) for n in ("chosen_made", "prefix_done", "in_tile_made", "pool_marked",
                         "marks_made", "told_done", "idx_made"))
    tok_in_made = sem("tok_in_made")
    scattered = [sem(f"scattered{i}") for i in range(2)]
    picked = [sem(f"picked{c}") for c in range(len(CHUNKS))]
    x_here = [sem(f"x_here{i}") for i in range(2)]
    xT_done, xT_out, g_done, silu_done, hid_made, hT_done, hT_out, d_done, ow_made = (
        sem(n) for n in ("xT_done", "xT_out", "g_done", "silu_done", "hid_made", "hT_done",
                         "hT_out", "d_done", "ow_made"))
    first_added, out_made, out_done = sem("first_added"), sem("out_made"), sem("out_done")

    with nc.Block() as block:

        @block.sync
        def _(sp):
            sp.dma_start(bias[:, :], expert_bias.rearrange("(a e) -> a e", a=1).broadcast_to([R, NE])
                         ).then_inc(loaded, 16)
            for dst, src in [
                (w_gu[:, :, 0, 0:F], eWg[:, 0:P, :].rearrange("e p f -> p e f")),
                (w_gu[:, :, 1, 0:F], eWg[:, P:D, :].rearrange("e p f -> p e f")),
                (w_gu[:, :, 0, F:2 * F], eWu[:, 0:P, :].rearrange("e p f -> p e f")),
                (w_gu[:, :, 1, F:2 * F], eWu[:, P:D, :].rearrange("e p f -> p e f")),
                (w_d0[:, :, :], eWd[:, 0:P, :].rearrange("e p d -> p e d")),
                (w_d1[:, :, :], eWd[:, P:F, :].rearrange("e p d -> p e d")),
            ]:
                sp.dma_start(dst, src).then_inc(w_here, 16)
            for par in range(2):
                sp.wait_ge(scattered[par], 16 * NTILE // 2)
            pair_t = pair_rows[0:TOPK * NT * R, :].rearrange("(k t p) d -> p k t d", k=TOPK, p=R)
            for c, (t0, t1, rows) in enumerate(CHUNKS):
                for k in range(TOPK):
                    sp.dma_start(picks[0:rows, k, t0:t1, :], pair_t[0:rows, k, t0:t1, :]).then_inc(picked[c], 16)
            for c, (t0, t1, rows) in enumerate(CHUNKS):
                sp.wait_ge(out_made, c + 1)
                o = out.rearrange("b s d -> (b s) d")[t0 * R:t0 * R + (t1 - t0) * rows, :]
                sp.dma_start(o.rearrange("(t p) d -> p t d", p=rows), picks[0:rows, 1, t0:t1, :]).then_inc(out_done, 16)
            sp.wait_ge(out_done, 16 * len(CHUNKS))

        @block.gpsimd
        def _(pool):
            nc.gpsimd.memset(ones_b[:, :], 1.0)
            nc.gpsimd.memset(valid[:, :], 1.0)
            nc.gpsimd.memset(one8[:, :], 1.0)
            nc.gpsimd.memset(reset[:, :], 1.0).then_inc(made, 1)
            pool.wait_ge(made, 1)
            nc.gpsimd.memset(reset[:, :].rearrange("p (n t) -> p n t", t=NT)[:, :, 0:1], 0.0)
            nc.gpsimd.affine_select(out=tri[:, :], in_=ones_b[:, 0:R], compare_op=ALU.is_gt, fill=0.0,
                                    base=0, pattern=[[1, R]], channel_multiplier=-1)
            nc.gpsimd.affine_select(out=valid[:, NT - 1:NT], in_=ones_b[:, 0:1], compare_op=ALU.is_gt, fill=0.0,
                                    base=TOK - (NT - 1) * R, pattern=[[0, 1]], channel_multiplier=-1)
            iota = lambda o, pattern, base=0, mult=0: nc.gpsimd.iota(
                o, pattern=pattern, base=base, channel_multiplier=mult, allow_small_or_imprecise_dtypes=True)
            iota(iota_s[:, :], [[1, P]])
            iota(iota_j[:, :], [[1, NTILE]])
            iota(iota_w[:, :], [[-1, NE]], base=NE)
            iota(values[:, 0, :], [[1, TOPK * NT]])
            iota(values[:, 1, :], [[0, TOPK * NT]], base=1, mult=1)
            iota(dump[:, :], [[P, NTILE]], base=DUMP, mult=1).then_inc(made, 1)

            def gather(n, nth, par):
                wait_alone(pool, const, tok_in_made, n + 1)
                nc.gpsimd.indirect_dma_start(out=xg[par][:, :], out_offset=None, in_=x3_rows[:, :],
                                             in_offset=bass.IndirectOffsetOnAxis(ap=tok_in[par][:, 0:1], axis=0)
                                             ).then_inc(x_here[par], 16)

            def scatter(n, nth, par):
                wait_alone(pool, const, ow_made, n + 1)
                nc.gpsimd.indirect_dma_start(out=pair_rows[:, :],
                                             out_offset=bass.IndirectOffsetOnAxis(ap=tok_out[par][:, 0:1], axis=0),
                                             in_=ow[par][:, :], in_offset=None).then_inc(scattered[par], 16)

            pool.wait_ge(in_tile_made, 1)
            for k in range(TOPK):
                cols = slice(k * NT, (k + 1) * NT)
                for v in range(BY_POOL[k]):
                    nc.gpsimd.tensor_tensor(marks[:, cols, v, :], in_tile[:, cols, :],
                                            spread(values[:, v, cols], NTILE), ALU.mult).then_inc(pool_marked, 1)
            for n in range(2):
                gather(n, 0, n)
            steps(pool, {4: gather, -1: scatter})

        @block.tensor
        def _(pe):
            pe.wait_ge(chosen_made, 1)
            pe.wait_ge(made, 2)
            c = chosen[:, :, :].rearrange("p e t -> p (e t)")
            nc.tensor.matmul(pX[0][0:R, 0:NE * NT], tri[:, :], c, start=True, stop=True)
            nc.tensor.matmul(pX[1][0:R, 0:NE * NT], ones_b[:, 0:R], c, start=True, stop=True).then_inc(prefix_done, 1)
            for n in range(TOPK * NT):
                if n % NT == 0:
                    pe.wait_ge(pool_marked, sum(BY_POOL[:n // NT + 1]))
                if n % 2 == 0:
                    pe.wait_ge(marks_made, n // 2 + 1)
                mm = nc.tensor.matmul(pG[0][:, 0:NV * NTILE], hot[:, n, :],
                                      marks[:, n, :, :].rearrange("p v j -> p (v j)"),
                                      start=(n == 0), stop=(n == TOPK * NT - 1))
            mm.then_inc(told_done, 1)
            pe.wait_ge(w_here, 16 * 6)
            pe.wait_ge(idx_made, 2)

            def expert(n):
                return pe.value_load(owner[0:1, bass.ds(n, 1)], min_val=0, max_val=NE - 1)

            def transpose_rows(n, nth, par):
                pe.wait_ge(x_here[par], 16 * (nth + 1))
                if follows(nth):
                    pe.wait_ge(xT_out, n - 1)
                for k in range(2):
                    mm = nc.tensor.transpose(pX[par][:, k * P:(k + 1) * P], xg[par][:, k * P:(k + 1) * P],
                                             const.ident[:, :])
                mm.then_inc(xT_done, 1)

            def gate_up(n, nth, par):
                e = expert(n)
                pe.wait_ge(xT_out, n + 1)
                if follows(nth):
                    pe.wait_ge(hid_made, n - 1)
                for k in range(2):
                    mm = nc.tensor.matmul(pG[par][:, 0:2 * F], xT[par][:, k, :], w_gu[:, bass.ds(e, 1), k, :],
                                          start=(k == 0), stop=(k == 1))
                mm.then_inc(g_done, 1)

            def hidden_transposes(n, nth, par):
                pe.wait_ge(hid_made, n + 1)
                if follows(nth):
                    pe.wait_ge(hT_out, n - 1)
                nc.tensor.transpose(pT[par][:, 0:P], hid[par][:, 0:P], const.ident[:, :])
                nc.tensor.transpose(pT[par][0:FB, P:2 * P], hid[par][:, P:F], const.ident[:, :]).then_inc(hT_done, 1)

            def down(n, nth, par):
                e = expert(n)
                pe.wait_ge(hT_out, n + 1)
                if follows(nth):
                    pe.wait_ge(ow_made, n - 1)
                nc.tensor.matmul(pD[par][:, 0:D], hT[par][:, 0, :], w_d0[:, bass.ds(e, 1), :], start=True, stop=False)
                nc.tensor.matmul(pD[par][:, 0:D], hT[par][0:FB, 1, :], w_d1[:, bass.ds(e, 1), :],
                                 start=False, stop=True).then_inc(d_done, 1)

            steps(pe, {2: transpose_rows, 1: gate_up, 0: hidden_transposes, -1: down})

        @block.scalar
        def _(act):
            nc.scalar.activation(sig[:, :, :], logits[0:R, :, :], ACT.Sigmoid).then_inc(sig_made, 1)

            def silu(n, nth, par):
                act.wait_ge(g_done, n + 1)
                if follows(nth):
                    act.wait_ge(hid_made, n - 1)
                nc.scalar.activation(sg[par][:, :], pG[par][:, 0:F], ACT.Silu).then_inc(silu_done, 1)

            def hidden_out(n, nth, par):
                act.wait_ge(hT_done, n + 1)
                if follows(nth):
                    act.wait_ge(d_done, n - 1)
                nc.scalar.activation(hT[par][:, 0, :], pT[par][:, 0:P], ACT.Copy)
                nc.scalar.activation(hT[par][0:FB, 1, :], pT[par][0:FB, P:2 * P], ACT.Copy).then_inc(hT_out, 1)

            steps(act, {1: silu, 0: hidden_out})

        @block.vector
        def _(dve):
            links = [0]

            def chained(ins):
                links[0] += 1
                ins.then_inc(link, 1)
                dve.wait_ge(link, links[0])

            dve.wait_ge(loaded, 16)
            dve.wait_ge(sig_made, 1)
            dve.wait_ge(made, 2)
            chained(nc.vector.tensor_tensor(tot[:, :, :], sig[:, :, :], every(bias[:, :], NT), ALU.add))
            for k in range(TOPK):
                src = (tot, rest)[k]
                chained(nc.vector.tensor_reduce(best[:, :], src[:, :, :], AX_X, ALU.max))
                chained(nc.vector.tensor_tensor(tie[:, :, :], src[:, :, :], spread(best[:, :], NE), ALU.is_equal))
                chained(nc.vector.tensor_tensor(rank[:, :, :], tie[:, :, :], every(iota_w[:, :], NT), ALU.mult))
                chained(nc.vector.tensor_reduce(first[:, :], rank[:, :, :], AX_X, ALU.max))
                chained(nc.vector.tensor_tensor(pick[k][:, :, :], rank[:, :, :], spread(first[:, :], NE), ALU.is_equal))
                if k == 0:
                    chained(nc.vector.scalar_tensor_tensor(rest[:, :, :], pick[0][:, :, :], -BIG, tot[:, :, :],
                                                           ALU.mult, ALU.add))
                chained(nc.vector.tensor_tensor(prod[:, :, :], pick[k][:, :, :], sig[:, :, :], ALU.mult))
                chained(nc.vector.tensor_reduce(w[:, k, :], prod[:, :, :], AX_X, ALU.add))
            chained(nc.vector.tensor_tensor(prod[:, :, :], pick[0][:, :, :], pick[1][:, :, :], ALU.add))
            nc.vector.tensor_tensor(chosen[:, :, :], prod[:, :, :].rearrange("p t e -> p e t"), every(valid[:, :], NE),
                                    ALU.mult).then_inc(chosen_made, 1)
            chained(nc.vector.tensor_tensor(wsum[:, :], w[:, 0, :], w[:, 1, :], ALU.add))
            chained(nc.vector.tensor_scalar(wsum[:, :], wsum[:, :], 1e-20, None, ALU.add))
            chained(nc.vector.reciprocal(winv[:, :], wsum[:, :]))
            chained(nc.vector.tensor_tensor(wn[:, :, :], w[:, :, :], every(winv[:, :], TOPK), ALU.mult))
            vw = lambda n: values[:, 2 + n, :].rearrange("p (k t) -> p k t", k=TOPK)
            chained(nc.vector.tensor_copy(vw(0), wn[:, :, :]))
            chained(nc.vector.tensor_tensor(w_left[:, :, :], wn[:, :, :], vw(0), ALU.subtract))
            chained(nc.vector.tensor_copy(vw(1), w_left[:, :, :]))
            chained(nc.vector.tensor_tensor(vw(2), w_left[:, :, :], vw(1), ALU.subtract))
            dve.wait_ge(prefix_done, 1)
            fl = lambda a: a[:, :, :].rearrange("p a b -> p (a b)")
            counts = pX[1][0:R, 0:NE * NT]
            chained(nc.vector.tensor_tensor_scan(fl(incl), reset[:, :], counts, 0.0, ALU.mult, ALU.add))
            chained(nc.vector.tensor_tensor(fl(excl), fl(incl), counts, ALU.subtract))
            nc.vector.tensor_tensor(fl(posn), fl(excl), pX[0][0:R, 0:NE * NT], ALU.add)
            chained(nc.vector.tensor_scalar(tiles_i[:, :], incl[:, :, NT - 1], float(P - 1), None, ALU.add))
            chained(nc.vector.tensor_scalar(tiles_s[:, :], tiles_i[:, :], 7, None, ALU.logical_shift_right))
            chained(nc.vector.tensor_copy(tiles[:, :], tiles_s[:, :]))
            chained(nc.vector.tensor_tensor_scan(upto[:, :], one8[:, :], tiles[:, :], 0.0, ALU.mult, ALU.add))
            chained(nc.vector.tensor_tensor(start[:, :], upto[:, :], tiles[:, :], ALU.subtract))
            chained(nc.vector.tensor_scalar(start[:, :], start[:, :], float(P), None, ALU.mult))
            chained(nc.vector.tensor_tensor(slot_all[:, :, :], posn[:, :, :], spread(start[:, :], NT), ALU.add))
            for k in range(TOPK):
                chained(nc.vector.tensor_tensor(prod[:, :, :], pick[k][:, :, :],
                                                slot_all[:, :, :].rearrange("p e t -> p t e"), ALU.mult))
                chained(nc.vector.tensor_reduce(slot_f[:, k, :], prod[:, :, :], AX_X, ALU.add))
            far = float(P * 127)
            chained(nc.vector.scalar_tensor_tensor(slot_f[:, :, :], slot_f[:, :, :], -far, every(valid[:, :], TOPK),
                                                   ALU.add, ALU.mult))
            chained(nc.vector.tensor_scalar(slot[:, :, :], slot_f[:, :, :], far, None, ALU.add))
            nc.vector.tensor_scalar(hi_i[:, :, :], slot[:, :, :], 7, None, ALU.logical_shift_right)
            chained(nc.vector.tensor_scalar(lo_i[:, :, :], slot[:, :, :], P - 1, None, ALU.bitwise_and))
            nc.vector.tensor_copy(hi[:, :], fl(hi_i))
            chained(nc.vector.tensor_copy(lo[:, :], fl(lo_i)))
            nc.vector.tensor_tensor(in_tile[:, :, :], spread(hi[:, :], NTILE), every(iota_j[:, :], TOPK * NT),
                                    ALU.is_equal).then_inc(in_tile_made, 1)
            dve.wait_ge(in_tile_made, 1)
            for n0 in range(0, TOPK * NT, 2):
                if n0 % NT == 0:
                    cols = slice(n0, n0 + NT)
                    for v in range(BY_POOL[n0 // NT], NV):
                        nc.vector.tensor_tensor(marks[:, cols, v, :], in_tile[:, cols, :],
                                                spread(values[:, v, cols], NTILE), ALU.mult)
                for n in range(n0, n0 + 2):
                    last = nc.vector.tensor_scalar(hot[:, n, :], iota_s[:, :], lo[:, n:n + 1], None, ALU.is_equal)
                last.then_inc(marks_made, 1)
            dve.wait_ge(told_done, 1)
            chained(nc.vector.tensor_copy(told[:, :, :], pG[0][:, 0:NV * NTILE].rearrange("p (v j) -> p v j", v=NV)))
            nc.vector.scalar_tensor_tensor(tok_a[:, :], told[:, 0, :], float(R), told[:, 1, :], ALU.mult, ALU.add)
            nc.vector.tensor_scalar(second[:, :], told[:, 0, :], float(NT), -float(NT * R), ALU.is_ge, ALU.mult)
            chained(nc.vector.tensor_scalar(free[:, :], told[:, 1, :], 0.0, None, ALU.is_equal))
            nc.vector.tensor_tensor(tok_c[:, :], tok_a[:, :], free[:, :], ALU.add)
            chained(nc.vector.tensor_tensor(tok_b[:, :], free[:, :], dump[:, :], ALU.mult))
            nc.vector.scalar_tensor_tensor(src_idx[:, :], tok_c[:, :], -1.0, second[:, :], ALU.add, ALU.add)
            nc.vector.scalar_tensor_tensor(dst_idx[:, :], tok_c[:, :], -1.0, tok_b[:, :], ALU.add, ALU.add)
            chained(nc.vector.tensor_tensor(w_a[:, :], told[:, 3, :], told[:, 4, :], ALU.add))
            nc.vector.tensor_tensor(w_slot[:, :], w_a[:, :], told[:, 2, :], ALU.add).then_inc(idx_made, 1)
            dve.wait_ge(idx_made, 1)

            def take_tokens(n, nth, par):
                if follows(nth):
                    dve.wait_ge(xT_done, n - 1)
                nc.vector.tensor_copy(tok_in[par][:, :], src_idx[:, bass.ds(n, 1)]).then_inc(tok_in_made, 1)

            def rows_out(n, nth, par):
                dve.wait_ge(xT_done, n + 1)
                if follows(nth):
                    dve.wait_ge(g_done, n - 1)
                nc.vector.tensor_copy(xT[par][:, :, :].rearrange("p k s -> p (k s)"),
                                      pX[par][:, 0:2 * P]).then_inc(xT_out, 1)

            def hidden(n, nth, par):
                dve.wait_ge(silu_done, n + 1)
                if follows(nth):
                    dve.wait_ge(hT_done, n - 1)
                nc.vector.tensor_tensor(hid[par][:, :], sg[par][:, :], pG[par][:, F:2 * F],
                                        ALU.mult).then_inc(hid_made, 1)

            def weigh(n, nth, par):
                dve.wait_ge(d_done, n + 1)
                dve.wait_ge(scattered[par], 16 * nth)
                nc.vector.tensor_copy(tok_out[par][:, :], dst_idx[:, bass.ds(n, 1)])
                nc.vector.tensor_scalar(ow[par][:, :], pD[par][:, 0:D], w_slot[:, bass.ds(n, 1)], None,
                                        ALU.mult).then_inc(ow_made, 1)

            for n in range(2):
                take_tokens(n, 0, n)
            chained(nc.vector.tensor_tensor(owner_m[:, :, :], every(upto[0:1, :], NTILE), spread(iota_j[0:1, :], NE),
                                            ALU.is_le))
            chained(nc.vector.tensor_reduce(owner_f[:, :], owner_m[:, :, :], AX_X, ALU.add))
            nc.vector.tensor_scalar(owner[:, :], owner_f[:, :], float(NE - 1), None, ALU.min).then_inc(idx_made, 1)
            steps(dve, {2: rows_out, 4: take_tokens, 1: hidden, -1: weigh})

            for c, (t0, t1, rows) in enumerate(CHUNKS):
                dve.wait_ge(picked[c], 32)
                a, b = (picks[0:rows, k, t0:t1, :] for k in range(TOPK))
                nc.vector.tensor_tensor(a, a, h[0:rows, t0:t1, :], ALU.add).then_inc(first_added, 1)
                dve.wait_ge(first_added, c + 1)
                nc.vector.tensor_tensor(b, a, b, ALU.add).then_inc(out_made, 1)


def wait_alone(eng, const, sem, value):
    eng.wait_ge(sem, value)
    eng.sem_inc(const.waits_passed, 1)


def split_product(nc, out, slices, waits={}, last=(0, 1)):
    passes = [(0, 0)] + [p for p in ((0, 1), (1, 0)) if p != last] + [last]
    for n, (a, b) in enumerate(passes):
        for k, (left, right) in enumerate(slices):
            if (n, k) in waits:
                waits[n, k]()
            product = nc.tensor.matmul(out, left[a], right[b], start=(n == k == 0),
                                       stop=(n == 2 and k == len(slices) - 1))
    return product


def semaphore(nc, const, name):
    s = nc.alloc_semaphore(name=name)
    const.semaphores.append(s)
    return s


def end_stage(nc, const):
    nc.clear_and_free_semaphores(const.semaphores)
    nc.all_engine_barrier()
    const.semaphores = []


def every(ap, n):
    return ap.unsqueeze(1).broadcast_to([ap.shape[0], n, ap.shape[1]])


def both(ap):
    return every(ap, 2)


def spread(ap, n):
    return ap.unsqueeze(2).broadcast_to([ap.shape[0], ap.shape[1], n])


Q_BANK = (1, 2, 0, 2)
KV_BANK = 1


def q_columns(bank, m):
    return bank[:, m * GT:(m + 1) * GT].rearrange("p (b s) -> p b s", s=S)


def patch_columns(bank, q):
    return bank[:, q * XR:(q + 1) * XR].rearrange("p (b c t) -> p c b t", b=IPG, c=C)


def patch_slots(patT, j, q):
    half, w = divmod(q, 2)
    a = patT[:, :, :].rearrange("p (c a) (b s) -> p a c b s", a=2, s=S)[:, half, :, :, 1:S]
    return a.rearrange("p c b (t w) -> p w c b t", w=NPH)[:, 2 * j + w, :, :, :]


_INS = ['x', 'L0_tok_W', 'L0_tok_b', 'L0_tok_cls_token', 'L0_tok_pos_embed', 'L0_attn_Wq', 'L0_attn_bq', 'L0_attn_Wk',
        'L0_attn_bk', 'L0_attn_Wv', 'L0_attn_bv', 'L0_attn_Wo', 'L0_attn_bo', 'L0_ffn_gate_w', 'L0_ffn_ln_w',
        'L0_ffn_ln_b', 'L0_ffn_fc1s', 'L0_ffn_b1s', 'L0_ffn_fc2s', 'L0_ffn_b2s', 'L1_attn_Wq', 'L1_attn_Wk',
        'L1_attn_Wv', 'L1_attn_Wg', 'L1_attn_Wo', 'L1_attn_gn_gamma', 'L1_attn_gn_beta', 'L1_ffn_W_gate_router',
        'L1_ffn_expert_bias', 'L1_ffn_Wg', 'L1_ffn_Wu', 'L1_ffn_Wd', 'L1_ffn_Wg_s', 'L1_ffn_Wu_s', 'L1_ffn_Wd_s']
_OUTS = [((NB, S, D), 'float32')]


def kernel(**inputs):
    import numpy as _np
    import concourse.bacc as _bacc
    from concourse import mybir as _mybir
    from concourse.bass_utils import run_bass_kernel_spmd as _run

    nc = _bacc.Bacc("TRN2", target_bir_lowering=False, num_devices=1)
    arrays, args = {}, []
    for name in _INS:
        a = _np.ascontiguousarray(inputs[name])
        arrays[f"in_{name}_dram"] = a
        args.append(nc.dram_tensor(f"in_{name}_dram", a.shape, _mybir.dt.from_np(a.dtype), kind="ExternalInput").ap())
    for i, (shape, dtype) in enumerate(_OUTS):
        dt = _mybir.dt.from_np(_np.dtype(dtype))
        args.append(nc.dram_tensor(f"out_{i}_dram", shape, dt, kind="ExternalOutput").ap())
    program(nc, *args)
    r = _run(nc, [arrays], core_ids=[0])
    got = tuple(r.results[0][f"out_{i}_dram"] for i in range(len(_OUTS)))
    return got[0]
```
